# Optimizing a Trainium2 kernel written in Bass

```python
import numpy as np
import jax
import jax.numpy as jnp

def _softmax(x, axis=-1):
    return jax.nn.softmax(x, axis=axis)

def _gelu(x):
    return jax.nn.gelu(x, approximate=True)

def _silu(x):
    return jax.nn.silu(x)

def _sigmoid(x):
    return jax.nn.sigmoid(x)

def _layernorm(x, axis=-1, eps=1e-05):
    m = jnp.mean(x, axis=axis, keepdims=True)
    v = jnp.var(x, axis=axis, keepdims=True)
    return (x - m) / jnp.sqrt(v + eps)

def _scatter_add(tgt, idx, src, axis=0):
    return tgt.at[idx].add(src)

def _segment_sum(src, seg, n):
    return jax.ops.segment_sum(src, seg, n)
kernel_name = 'mk_adj_ffn_d2_adj_r2_81d02d'

def setup_inputs(seed: int=0):
    np.random.seed(seed)
    _w = jnp.asarray

    def _rec_inputs():
        import jax
        import jax.numpy as jnp
        _gk = jax.random.key(seed)
        x = -0.0002928 + 1 * jax.random.normal(jax.random.fold_in(_gk, 1), (128, 64, 128), jnp.float32)
        _a = jax.random.bernoulli(jax.random.fold_in(_gk, 2), 0.0625, (128, 64, 64))
        _a = jnp.logical_or(_a, jnp.swapaxes(_a, -1, -2))
        _a = jnp.logical_or(_a, jnp.eye(64, dtype=bool))
        _af = _a.astype(jnp.float32)
        _af = _af * jax.random.uniform(jax.random.fold_in(_gk, 3), (128, 64, 64), jnp.float32, 0.05, 1)
        adj = _af
        _nm = jnp.ones((128, 64), dtype=bool)
        nodemask = jnp.where(_nm, 1.0, 0.0).astype(jnp.int32)
        return (x, adj, nodemask)
    x, adj, nodemask = _rec_inputs()

    def _L0_gnn_setup():
        import jax, jax.numpy as jnp
        import numpy as np
        LN_EPS = 1e-05
        key = jax.random.key(seed)
        k1, k2, k3, k4 = jax.random.split(key, 4)
        B, N, F, O = (8, 1024, 128, 128)
        x = jax.random.normal(k1, (B, N, F), dtype=jnp.float32)
        adj = jax.random.uniform(k2, (B, N, N), dtype=jnp.float32)
        gamma = jnp.ones((F,), jnp.float32)
        beta = jnp.zeros((F,), jnp.float32)
        W_self = jax.random.normal(k3, (F, O), dtype=jnp.float32) * (1.0 / np.sqrt(F))
        W_neigh = jax.random.normal(k4, (F, O), dtype=jnp.float32) * (1.0 / np.sqrt(F))
        return {'x': x, 'adj': adj, 'gamma': gamma, 'beta': beta, 'W_self': W_self, 'W_neigh': W_neigh}
    _L0_gnn_all = _L0_gnn_setup()
    _L0_gnn_in = {k: v for k, v in _L0_gnn_all.items() if k in ('gamma', 'beta', 'W_self', 'W_neigh')}
    del _L0_gnn_all

    def _L0_ffn_setup():
        import jax, jax.numpy as jnp
        import numpy as np
        B, T, C = (64, 192, 128)
        NH, NKV = (4, 2)
        HD = C // NH
        NREP = NH // NKV
        NE, TOPK = (8, 2)
        HID = int(8 / 3 * C)
        EPS_RMS = 1e-06

        def _rope_tables(t_len):
            inv_freq = 1.0 / 10000.0 ** (np.arange(0, HD, 2, dtype=np.float32) / HD)
            t = np.arange(t_len, dtype=np.float32)
            freqs = np.outer(t, inv_freq)
            emb = np.concatenate([freqs, freqs], axis=-1)
            return (jnp.asarray(np.cos(emb)), jnp.asarray(np.sin(emb)))

        def _rotate_half(x):
            h = x.shape[-1] // 2
            return jnp.concatenate([-x[..., h:], x[..., :h]], axis=-1)

        def _rmsnorm(v, w):
            return v * jax.lax.rsqrt(jnp.mean(v * v, axis=-1, keepdims=True) + EPS_RMS) * w
        key = jax.random.key(seed)
        ks = jax.random.split(key, 10)
        s = lambda k, shape: jax.random.normal(k, shape, jnp.float32) * 0.02
        return {'x': jax.random.normal(ks[0], (B, T, C), jnp.float32), 'ln1_w': jnp.ones((C,), jnp.float32), 'ln2_w': jnp.ones((C,), jnp.float32), 'wq': s(ks[1], (NH * HD, C)), 'wk': s(ks[2], (NKV * HD, C)), 'wv': s(ks[3], (NKV * HD, C)), 'wo': s(ks[4], (C, C)), 'router_w': s(ks[5], (NE, C)), 'w1': s(ks[6], (NE, HID, C)), 'w2': s(ks[7], (NE, C, HID)), 'w3': s(ks[8], (NE, HID, C))}
    _L0_ffn_all = _L0_ffn_setup()
    _L0_ffn_in = {k: v for k, v in _L0_ffn_all.items() if k in ('ln1_w', 'ln2_w', 'wq', 'wk', 'wv', 'wo', 'router_w', 'w1', 'w2', 'w3')}
    del _L0_ffn_all

    def _L1_gnn_setup():
        import jax, jax.numpy as jnp
        import numpy as np
        HIDDEN = 128
        NEG_INF = -1e+30
        key = jax.random.key(seed)
        k1, k2, k3, k4 = jax.random.split(key, 4)
        B, S, H = (4, 2048, HIDDEN)
        matrix = jax.random.normal(k1, (B, S, H), dtype=jnp.float32)
        mask = jax.random.randint(k2, (B, S), 0, 2, dtype=jnp.int32)
        adj = jax.random.uniform(k3, (B, S, S), dtype=jnp.float32)
        limit = float(np.sqrt(6.0 / (H + H)))
        W = jax.random.uniform(k4, (H, H), dtype=jnp.float32, minval=-limit, maxval=limit)
        return {'matrix': matrix, 'mask': mask, 'adj': adj, 'W': W}
    _L1_gnn_all = _L1_gnn_setup()
    _L1_gnn_in = {k: v for k, v in _L1_gnn_all.items() if k in ('W',)}
    del _L1_gnn_all

    def _L1_ffn_setup():
        import jax, jax.numpy as jnp
        import numpy as np
        B, A = (2048, 8)
        IN, OUT = (128, 128)
        SH1, SH2 = (128, 128)
        EH1, EH2 = (128, 64)
        E, TOPK = (4, 2)

        def _shared_mlp(x, W1, b1, W2, b2, W3, b3):
            h = jax.nn.relu(x @ W1 + b1)
            h = jax.nn.relu(h @ W2 + b2)
            return h @ W3 + b3

        def _experts_mlp(x, eW1, eb1, eW2, eb2, eW3, eb3):
            h = jax.nn.relu(jnp.einsum('baf,efh->ebah', x, eW1) + eb1[:, None, None, :])
            h = jax.nn.relu(jnp.einsum('ebah,ehg->ebag', h, eW2) + eb2[:, None, None, :])
            o = jnp.einsum('ebag,ego->ebao', h, eW3) + eb3[:, None, None, :]
            return jnp.moveaxis(o, 0, -1)
        key = jax.random.key(seed)
        ks = jax.random.split(key, 16)
        s = 0.05
        return {'x': jax.random.normal(ks[0], (B, A, IN), jnp.float32), 'sW1': jax.random.normal(ks[1], (IN, SH1), jnp.float32) * s, 'sb1': jnp.zeros((SH1,), jnp.float32), 'sW2': jax.random.normal(ks[2], (SH1, SH2), jnp.float32) * s, 'sb2': jnp.zeros((SH2,), jnp.float32), 'sW3': jax.random.normal(ks[3], (SH2, OUT), jnp.float32) * s, 'sb3': jnp.zeros((OUT,), jnp.float32), 'eW1': jax.random.normal(ks[4], (E, IN, EH1), jnp.float32) * s, 'eb1': jnp.zeros((E, EH1), jnp.float32), 'eW2': jax.random.normal(ks[5], (E, EH1, EH2), jnp.float32) * s, 'eb2': jnp.zeros((E, EH2), jnp.float32), 'eW3': jax.random.normal(ks[6], (E, EH2, OUT), jnp.float32) * s, 'eb3': jnp.zeros((E, OUT), jnp.float32), 'gW': jax.random.normal(ks[7], (IN, E), jnp.float32) * s, 'gb': jnp.zeros((E,), jnp.float32)}
    _L1_ffn_all = _L1_ffn_setup()
    _L1_ffn_in = {k: v for k, v in _L1_ffn_all.items() if k in ('sW1', 'sb1', 'sW2', 'sb2', 'sW3', 'sb3', 'eW1', 'eb1', 'eW2', 'eb2', 'eW3', 'eb3', 'gW', 'gb')}
    del _L1_ffn_all
    return {'x': x, 'adj': adj, 'nodemask': nodemask, 'L0_gnn_gamma': _L0_gnn_in['gamma'], 'L0_gnn_beta': _L0_gnn_in['beta'], 'L0_gnn_W_self': _L0_gnn_in['W_self'], 'L0_gnn_W_neigh': _L0_gnn_in['W_neigh'], 'L0_ffn_ln1_w': _L0_ffn_in['ln1_w'], 'L0_ffn_ln2_w': _L0_ffn_in['ln2_w'], 'L0_ffn_wq': _L0_ffn_in['wq'], 'L0_ffn_wk': _L0_ffn_in['wk'], 'L0_ffn_wv': _L0_ffn_in['wv'], 'L0_ffn_wo': _L0_ffn_in['wo'], 'L0_ffn_router_w': _L0_ffn_in['router_w'], 'L0_ffn_w1': _L0_ffn_in['w1'], 'L0_ffn_w2': _L0_ffn_in['w2'], 'L0_ffn_w3': _L0_ffn_in['w3'], 'L1_gnn_W': _L1_gnn_in['W'], 'L1_ffn_sW1': _L1_ffn_in['sW1'], 'L1_ffn_sb1': _L1_ffn_in['sb1'], 'L1_ffn_sW2': _L1_ffn_in['sW2'], 'L1_ffn_sb2': _L1_ffn_in['sb2'], 'L1_ffn_sW3': _L1_ffn_in['sW3'], 'L1_ffn_sb3': _L1_ffn_in['sb3'], 'L1_ffn_eW1': _L1_ffn_in['eW1'], 'L1_ffn_eb1': _L1_ffn_in['eb1'], 'L1_ffn_eW2': _L1_ffn_in['eW2'], 'L1_ffn_eb2': _L1_ffn_in['eb2'], 'L1_ffn_eW3': _L1_ffn_in['eW3'], 'L1_ffn_eb3': _L1_ffn_in['eb3'], 'L1_ffn_gW': _L1_ffn_in['gW'], 'L1_ffn_gb': _L1_ffn_in['gb']}

def reference(x, adj, nodemask, L0_gnn_gamma, L0_gnn_beta, L0_gnn_W_self, L0_gnn_W_neigh, L0_ffn_ln1_w, L0_ffn_ln2_w, L0_ffn_wq, L0_ffn_wk, L0_ffn_wv, L0_ffn_wo, L0_ffn_router_w, L0_ffn_w1, L0_ffn_w2, L0_ffn_w3, L1_gnn_W, L1_ffn_sW1, L1_ffn_sb1, L1_ffn_sW2, L1_ffn_sb2, L1_ffn_sW3, L1_ffn_sb3, L1_ffn_eW1, L1_ffn_eb1, L1_ffn_eW2, L1_ffn_eb2, L1_ffn_eW3, L1_ffn_eb3, L1_ffn_gW, L1_ffn_gb):
    import jax
    import jax.numpy as jnp

    def _L0_gnn_ref(x, adj, gamma, beta, W_self, W_neigh):
        import jax, jax.numpy as jnp
        import numpy as np
        LN_EPS = 1e-05
        mu = jnp.mean(x, axis=-1, keepdims=True)
        var = jnp.mean(jnp.square(x - mu), axis=-1, keepdims=True)
        xn = (x - mu) * jax.lax.rsqrt(var + LN_EPS) * gamma + beta
        d_out = jnp.sum(adj, axis=1)
        d_in = jnp.sum(adj, axis=2)
        s_out = jnp.where(d_out != 0, jax.lax.rsqrt(d_out), 0.0)
        s_in = jnp.where(d_in != 0, jax.lax.rsqrt(d_in), 0.0)
        A_norm = s_out[:, :, None] * adj * s_in[:, None, :]
        eye = jnp.eye(adj.shape[1], dtype=adj.dtype)
        L = eye[None, :, :] - A_norm
        neighbor = jnp.einsum('bij,bjf->bif', L, xn)
        pre = xn @ W_self + neighbor @ W_neigh
        return jax.nn.softplus(pre)

    def _L0_ffn_ref(x, ln1_w, ln2_w, wq, wk, wv, wo, router_w, w1, w2, w3):
        import jax, jax.numpy as jnp
        import numpy as np
        B, T, C = (64, 192, 128)
        NH, NKV = (4, 2)
        HD = C // NH
        NREP = NH // NKV
        NE, TOPK = (8, 2)
        HID = int(8 / 3 * C)
        EPS_RMS = 1e-06

        def _rope_tables(t_len):
            inv_freq = 1.0 / 10000.0 ** (np.arange(0, HD, 2, dtype=np.float32) / HD)
            t = np.arange(t_len, dtype=np.float32)
            freqs = np.outer(t, inv_freq)
            emb = np.concatenate([freqs, freqs], axis=-1)
            return (jnp.asarray(np.cos(emb)), jnp.asarray(np.sin(emb)))

        def _rotate_half(x):
            h = x.shape[-1] // 2
            return jnp.concatenate([-x[..., h:], x[..., :h]], axis=-1)

        def _rmsnorm(v, w):
            return v * jax.lax.rsqrt(jnp.mean(v * v, axis=-1, keepdims=True) + EPS_RMS) * w
        Bx, Tx, Cx = x.shape
        h = _rmsnorm(x, ln1_w)
        q = (h @ wq.T).reshape(Bx, Tx, NH, HD).transpose(0, 2, 1, 3)
        k = (h @ wk.T).reshape(Bx, Tx, NKV, HD).transpose(0, 2, 1, 3)
        v = (h @ wv.T).reshape(Bx, Tx, NKV, HD).transpose(0, 2, 1, 3)
        cos, sin = _rope_tables(Tx)
        cos, sin = (cos[None, None], sin[None, None])
        q = q * cos + _rotate_half(q) * sin
        k = k * cos + _rotate_half(k) * sin
        k = jnp.repeat(k, NREP, axis=1)
        v = jnp.repeat(v, NREP, axis=1)
        scores = jnp.einsum('bhtd,bhsd->bhts', q, k) / jnp.sqrt(jnp.float32(HD))
        causal = jnp.tril(jnp.ones((Tx, Tx), dtype=bool))
        scores = jnp.where(causal[None, None], scores, jnp.float32(-1e+30))
        att = jax.nn.softmax(scores, axis=-1)
        y = jnp.einsum('bhts,bhsd->bhtd', att, v).transpose(0, 2, 1, 3).reshape(Bx, Tx, Cx)
        x = x + y @ wo.T
        flat = _rmsnorm(x, ln2_w).reshape(-1, Cx)
        probs = jax.nn.softmax(flat @ router_w.T, axis=-1)
        tp, ti = jax.lax.top_k(probs, TOPK)
        tp = tp / (jnp.sum(tp, axis=-1, keepdims=True) + 1e-09)
        weights = jnp.sum(tp[..., None] * jax.nn.one_hot(ti, NE, dtype=flat.dtype), axis=1)
        out = jnp.zeros_like(flat)
        for e in range(NE):
            hh = jax.nn.silu(flat @ w1[e].T) * (flat @ w3[e].T)
            out = out + weights[:, e:e + 1] * (hh @ w2[e].T)
        return x + out.reshape(Bx, Tx, Cx)

    def _L1_gnn_ref(matrix, mask, adj, W):
        import jax, jax.numpy as jnp
        import numpy as np
        HIDDEN = 128
        NEG_INF = -1e+30
        intermediate = jnp.einsum('bsh,hd->bsd', matrix, W)
        similarities = jnp.einsum('bsd,btd->bst', intermediate, matrix)
        similarities = similarities * adj
        key_mask = mask[:, None, :].astype(bool)
        masked = jnp.where(key_mask, similarities, NEG_INF)
        attn = jax.nn.softmax(masked, axis=-1)
        output = jnp.einsum('bst,bth->bsh', attn, matrix)
        return output

    def _L1_ffn_ref(x, sW1, sb1, sW2, sb2, sW3, sb3, eW1, eb1, eW2, eb2, eW3, eb3, gW, gb):
        import jax, jax.numpy as jnp
        import numpy as np
        B, A = (2048, 8)
        IN, OUT = (128, 128)
        SH1, SH2 = (128, 128)
        EH1, EH2 = (128, 64)
        E, TOPK = (4, 2)

        def _shared_mlp(x, W1, b1, W2, b2, W3, b3):
            h = jax.nn.relu(x @ W1 + b1)
            h = jax.nn.relu(h @ W2 + b2)
            return h @ W3 + b3

        def _experts_mlp(x, eW1, eb1, eW2, eb2, eW3, eb3):
            h = jax.nn.relu(jnp.einsum('baf,efh->ebah', x, eW1) + eb1[:, None, None, :])
            h = jax.nn.relu(jnp.einsum('ebah,ehg->ebag', h, eW2) + eb2[:, None, None, :])
            o = jnp.einsum('ebag,ego->ebao', h, eW3) + eb3[:, None, None, :]
            return jnp.moveaxis(o, 0, -1)
        all_out = _experts_mlp(x, eW1, eb1, eW2, eb2, eW3, eb3)
        shared = _shared_mlp(x, sW1, sb1, sW2, sb2, sW3, sb3)
        gates = jax.nn.softmax(x @ gW + gb, axis=-1)
        topv, topi = jax.lax.top_k(gates, TOPK)
        topw = jax.nn.softmax(topv, axis=-1)
        sel = jnp.take_along_axis(all_out, topi[:, :, None, :], axis=-1)
        gated = jnp.sum(sel * topw[:, :, None, :], axis=-1)
        return shared + gated
    x = x + _L0_gnn_ref(_layernorm(x, axis=-1), adj, L0_gnn_gamma, L0_gnn_beta, L0_gnn_W_self, L0_gnn_W_neigh)
    x = x + _L0_ffn_ref(_layernorm(x, axis=-1), L0_ffn_ln1_w, L0_ffn_ln2_w, L0_ffn_wq, L0_ffn_wk, L0_ffn_wv, L0_ffn_wo, L0_ffn_router_w, L0_ffn_w1, L0_ffn_w2, L0_ffn_w3)
    x = x + _L1_gnn_ref(_layernorm(x, axis=-1), nodemask, adj, L1_gnn_W)
    x = x + _L1_ffn_ref(_layernorm(x, axis=-1), L1_ffn_sW1, L1_ffn_sb1, L1_ffn_sW2, L1_ffn_sb2, L1_ffn_sW3, L1_ffn_sb3, L1_ffn_eW1, L1_ffn_eb1, L1_ffn_eW2, L1_ffn_eb2, L1_ffn_eW3, L1_ffn_eb3, L1_ffn_gW, L1_ffn_gb)
    return x

_drawn_inputs = setup_inputs


def setup_inputs(seed=0):
    import zlib

    import numpy as np

    out = dict(_drawn_inputs(seed))
    spreads = {'L0_gnn_gamma': (1.0, 0.2),
     'L0_gnn_beta': (0.0, 0.1),
     'L0_ffn_ln1_w': (1.0, 0.6),
     'L0_ffn_ln2_w': (1.0, 0.6),
     'L1_ffn_sb1': (0.0, 2.0),
     'L1_ffn_sb2': (0.0, 2.0),
     'L1_ffn_sb3': (0.0, 0.8),
     'L1_ffn_eb1': (0.0, 0.8),
     'L1_ffn_eb2': (0.0, 0.8),
     'L1_ffn_eb3': (0.0, 1.779),
     'L1_ffn_gb': (0.0, 0.8)}
    factors = {'L0_ffn_wq': 8.0,
     'L0_ffn_wk': 8.0,
     'L0_ffn_wv': 7.798,
     'L0_ffn_wo': 7.495,
     'L0_ffn_router_w': 8.0,
     'L0_ffn_w1': 8.0,
     'L0_ffn_w2': 8.0,
     'L0_ffn_w3': 8.0,
     'L1_ffn_sW1': 12.681,
     'L1_ffn_eW1': 5.699,
     'L1_ffn_eW2': 4.955,
     'L1_ffn_eW3': 3.671,
     'L1_ffn_gW': 3.028,
     'L1_ffn_sW2': 3.673}
    for name, (base, spread) in spreads.items():
        noise = np.random.default_rng([zlib.crc32(name.encode()), seed]).standard_normal(out[name].shape)
        drawn = base * np.exp(spread * noise) if base else spread * noise
        out[name] = jnp.asarray(drawn.astype(out[name].dtype))
    for name, factor in factors.items():
        out[name] = (out[name] * factor).astype(out[name].dtype)
    return out
```

```python
from contextlib import ExitStack

import numpy as np

import concourse.bass as bass
from concourse import mybir

F32 = mybir.dt.float32
I32 = mybir.dt.int32
BF16 = mybir.dt.bfloat16
ALU = mybir.AluOpType
ACT = mybir.ActivationFunctionType
AX = mybir.AxisListType.X

P = 128
D = 128
N = 64
B = 128
T = B * N // P
GT = 4
G = T // GT
H, HD = 4, 32
KV = 2
NE, HID = 8, 341
HC = 3
SE = 4
EPS = 1e-5
EPS_RMS = 1e-6
NEG = -1e30
REGION = B * N + P
SLOTS = 2 * B * N // P + NE

T_ID, T_LOW, T_COS, T_SIN, T_CAUSAL, T_REV, T_REGION, T_TILE, T_SLOT, T_PAIR, T_REV4 = (
    0, 128, 256, 288, 320, 384, 392, 400, 464, 464 + SLOTS, 464 + SLOTS + 256)
T_ROW = T_REV4 + SE
T_ALL = T_ROW + 1


def tables():
    t = np.zeros((P, T_ALL), np.float32)
    r = np.arange(P)
    t[:, T_ID:T_ID + P] = np.eye(P)
    t[:, T_LOW:T_LOW + P] = r[:, None] < r[None, :]
    f = np.outer(np.arange(N, dtype=np.float32), 1.0 / 10000.0 ** (np.arange(0, HD, 2, dtype=np.float32) / HD))
    cos, sin = np.cos(f), np.sin(f)
    t[:, T_COS:T_COS + HD] = np.tile(np.concatenate([cos, cos], 1), (2, 1))
    t[:, T_SIN:T_SIN + HD] = np.tile(np.concatenate([-sin, sin], 1), (2, 1))
    n = np.arange(N)
    t[:, T_CAUSAL:T_CAUSAL + N] = np.tile(np.where(n[None, :] <= n[:, None], 0.0, NEG), (2, 1))
    t[:, T_REV:T_REV + NE] = NE - np.arange(NE)
    t[:, T_REGION:T_REGION + NE] = REGION * np.arange(NE)
    t[:, T_TILE:T_TILE + 64] = P * np.arange(64)
    t[:, T_SLOT:T_SLOT + SLOTS] = np.arange(SLOTS)
    for e in range(SE):
        t[e, T_PAIR + e // 2 * P + e % 2 * 64:T_PAIR + e // 2 * P + e % 2 * 64 + 64] = 1.0
    t[:, T_REV4:T_REV4 + SE] = SE - np.arange(SE)
    t[:, T_ROW] = r
    return t


def need(eng, semaphore, count):
    if not isinstance(count, int) or count > 0:
        eng.wait_ge(semaphore, count)


def alone(eng, passed):
    eng.sem_inc(passed, 1)


def live(g, groups=G):
    return not isinstance(g, int) or 0 <= g < groups


def pipeline(eng, body, lag, groups=G, unroll=2, lead=2, prepare=None):
    first = lag + lead + (groups - lag - lead) % unroll
    for i in range(first):
        if prepare and i % unroll == 0:
            prepare(i, unroll)
        body(i, i % unroll)
    with eng.Fori(first, groups - unroll + 1, unroll) as i:
        if prepare:
            prepare(i, unroll)
        for k in range(unroll):
            body(eng.snap(i + k) if k else i, (first + k) % unroll)
    for i in range(groups, groups + lag):
        if prepare and (i - groups) % unroll == 0:
            prepare(i, unroll)
        body(i, i % unroll)


def tile4(g):
    return bass.ds(g * GT, GT)


class Signals:

    def __init__(self, nc, prefix):
        self.nc, self.prefix, self.held = nc, prefix, []

    def new(self, name):
        self.held.append(self.nc.alloc_semaphore(f"{self.prefix}_{name}"))
        return self.held[-1]

    def give_back(self):
        self.nc.clear_and_free_semaphores(self.held)
        self.nc.all_engine_barrier()


def graph_conv(nc, c):
    with ExitStack() as ctx:
        def sb(name, shape, dt=F32):
            return ctx.enter_context(nc.sbuf_tensor("a_" + name, shape, dt))

        def bank(name, shape=(P, GT, D)):
            return ctx.enter_context(nc.psum_tensor("a_" + name, list(shape), F32))

        signals = Signals(nc, "a")
        sem = signals.new

        st = sb("st", [P, 2, GT, 6])
        mv = sb("mv", [P, 2, GT, 2])
        var = sb("var", [P, 2, GT])
        rstd = sb("rstd", [P, 2, GT])
        z = sb("z", [P, 2, GT, D])
        xn = sb("xn", [P, 2, GT, D])
        xnT = sb("xnT", [P, 2, GT, D])
        adj_s = sb("adj_s", [P, 2, GT, P])
        lapT = sb("lapT", [P, 2, GT, P])
        nbT = sb("nbT", [P, 2, GT, P])
        ab = sb("ab", [P, 2, GT, D])
        lg = sb("lg", [P, 2, GT, D])
        deg = sb("deg", [P, 2, T])
        nz = sb("nz", [P, 2, T])
        lnd = sb("lnd", [P, 2, T])
        s0 = sb("s0", [P, 2, T])
        sq = sb("sq", [P, 2, T])
        sc = sb("sc", [P, 2, T])
        zT_ps = bank("zT_ps")
        adjT_ps = bank("adjT_ps")
        nb_ps = bank("nb_ps")
        pre_ps = [bank("pre_ps0"), bank("pre_ps1")]
        deg_ps = bank("deg_ps", (P, T))

        colsum = sem("colsum"); degs = sem("degs"); lns = sem("lns"); scales = sem("scales")
        zeroed = sem("zeroed"); dchain = sem("dchain")
        bn = sem("bn"); stats = sem("stats"); pvar = sem("pvar"); rstd_ok = sem("rstd_ok")
        z_ok = sem("z_ok"); zT_ok = sem("zT_ok"); xnT_ok = sem("xnT_ok"); xg_ok = sem("xg_ok"); xn_ok = sem("xn_ok")
        adj_ok = sem("adj_ok"); adj_half = sem("adj_half"); adjT_ok = sem("adjT_ok"); lapT_ok = sem("lapT_ok")
        nb_ok = sem("nb_ok"); nbT_ok = sem("nbT_ok"); pre_ok = sem("pre_ok")
        ab_ok = sem("ab_ok"); ex_ok = sem("ex_ok"); lg_ok = sem("lg_ok"); sp_ok = sem("sp_ok"); x_ok = sem("x_ok")
        LAG = 3

        with nc.Block() as block:
            @block.vector
            def _(eng):
                eng.wait_ge(c.adj_in, 16)
                eng.tensor_reduce(deg[:, 0, :], c.adj[:], AX, ALU.add).then_inc(dchain, 1)
                eng.wait_ge(colsum, 1)
                eng.tensor_copy(deg[:, 1, :], deg_ps[:]).then_inc(dchain, 1)
                eng.wait_ge(dchain, 2)
                eng.tensor_scalar(nz[:], deg[:], 0.0, None, ALU.not_equal).then_inc(dchain, 1)
                eng.tensor_scalar(sq[:], deg[:], 0.0, None, ALU.is_equal).then_inc(dchain, 1)
                eng.wait_ge(dchain, 4)
                eng.tensor_tensor(deg[:], deg[:], sq[:], ALU.add).then_inc(degs, 1)
                eng.wait_ge(lns, 2)
                eng.tensor_tensor(sq[:], s0[:], s0[:], ALU.mult).then_inc(dchain, 1)
                eng.wait_ge(dchain, 5)
                eng.tensor_tensor(sq[:], sq[:], deg[:], ALU.mult).then_inc(dchain, 1)
                eng.wait_ge(dchain, 6)
                eng.tensor_scalar(sq[:], sq[:], -0.5, 1.5, ALU.mult, ALU.add).then_inc(dchain, 1)
                eng.wait_ge(dchain, 7)
                eng.tensor_tensor(sq[:], sq[:], s0[:], ALU.mult).then_inc(dchain, 1)
                eng.wait_ge(dchain, 8)
                eng.tensor_tensor(sc[:], sq[:], nz[:], ALU.mult).then_inc(dchain, 1)
                eng.wait_ge(dchain, 9)
                eng.tensor_scalar(sc[:, 1, :], sc[:, 1, :], -1.0, None, ALU.mult).then_inc(scales, 1)
                eng.wait_ge(scales, 1)
                eng.wait_ge(c.x_in, 16)

                def body(i, p):
                    g, b = i, p
                    if live(g):
                        for t in range(GT):
                            m = eng.bn_stats(st[:, b, t, :], c.x[:, bass.ds(g * GT + t, 1), :].rearrange("p a f -> p (a f)"))
                        m.then_inc(bn, 1)
                    g, b = i - 3, (p + 1) % 2
                    if live(g):
                        eng.wait_ge(lg_ok, g + 1)
                        eng.scalar_tensor_tensor(lg[:, b], pre_ps[b][:], 0.0, lg[:, b], ALU.max, ALU.add).then_inc(sp_ok, 1)
                    g, b = i, p
                    if live(g):
                        eng.wait_ge(bn, g + 1)
                        need(eng, rstd_ok, g - 1)
                        need(eng, z_ok, g - 1)
                        alone(eng, c.passed)
                        for t in range(GT):
                            m = eng.bn_aggr(mv[:, b, t, :], st[:, b, t, :])
                        m.then_inc(stats, 1)
                    g, b = i - 3, (p + 1) % 2
                    if live(g):
                        eng.wait_ge(sp_ok, g + 1)
                        eng.tensor_tensor(c.x[:, tile4(g), :], c.x[:, tile4(g), :], lg[:, b], ALU.add).then_inc(x_ok, 1)
                    g, b = i - 2, p
                    if live(g):
                        eng.wait_ge(nb_ok, g + 1)
                        eng.wait_ge(xnT_ok, g + 1)
                        need(eng, pre_ok, g - 1)
                        eng.tensor_tensor(nbT[:, b], nb_ps[:], xnT[:, b], ALU.add).then_inc(nbT_ok, 1)
                    g, b = i - 1, (p + 1) % 2
                    if live(g):
                        eng.wait_ge(adjT_ok, g + 1)
                        need(eng, nb_ok, g - 1)
                        eng.tensor_tensor(lapT[:, b], adjT_ps[:], sc[:, 0, tile4(g)].unsqueeze(2).broadcast_to([P, GT, P]),
                                          ALU.mult).then_inc(lapT_ok, 1)
                    g, b = i, p
                    if live(g):
                        eng.wait_ge(rstd_ok, g + 1)
                        need(eng, xg_ok, g - 1)
                        need(eng, zT_ok, g - 1)
                        for t in range(GT):
                            m = eng.tensor_scalar(z[:, b, t, :], c.x[:, bass.ds(g * GT + t, 1), :].rearrange("p a f -> p (a f)"),
                                                  mv[:, b, t, 0:1], rstd[:, b, t:t + 1], ALU.subtract, ALU.mult)
                        m.then_inc(z_ok, 1)
                pipeline(eng, body, LAG)

            @block.gpsimd
            def _(eng):
                eng.memset(adj_s[:], 0.0).then_inc(zeroed, 1)
                eng.wait_ge(zeroed, 1)
                eng.wait_ge(scales, 1)
                eng.wait_ge(c.weights_in, c.weights_count)

                def body(i, p):
                    g, b = i - 1, (p + 1) % 2
                    if live(g):
                        eng.wait_ge(z_ok, g + 1)
                        need(eng, nb_ok, g - 1)
                        eng.tensor_tensor(xn[:, b], z[:, b], c.gamma_row[:].unsqueeze(1).broadcast_to([P, GT, D]),
                                          ALU.mult).then_inc(xg_ok, 1)
                    g, b = i, p
                    if live(g):
                        eng.wait_ge(stats, g + 1)
                        alone(eng, c.passed)
                        eng.tensor_scalar(var[:, b], mv[:, b, :, 1], 1.0 + EPS, EPS * EPS, ALU.mult, ALU.add).then_inc(pvar, 1)
                        eng.wait_ge(pvar, g + 1)
                        eng.tensor_tensor(rstd[:, b], var[:, b], c.minus_half[:, 0:GT], ALU.pow).then_inc(rstd_ok, 1)
                        need(eng, adjT_ok, g - 1)
                        for j, (last, done) in enumerate(((rstd_ok, adj_half), (adj_half, adj_ok))):
                            eng.wait_ge(last, g + 1)
                            q = slice(N * j, N * j + N)
                            eng.tensor_tensor(adj_s[q, b, :, q], c.adj[q, tile4(g), :],
                                              sc[q, 1, tile4(g)].unsqueeze(2).broadcast_to([N, GT, N]), ALU.mult)\
                               .then_inc(done, 1)
                        eng.wait_ge(adj_ok, g + 1)
                    g, b = i - 1, (p + 1) % 2
                    if live(g):
                        eng.wait_ge(xg_ok, g + 1)
                        eng.tensor_tensor(xn[:, b], xn[:, b], c.beta_row[:].unsqueeze(1).broadcast_to([P, GT, D]),
                                          ALU.add).then_inc(xn_ok, 1)
                pipeline(eng, body, LAG)

            @block.scalar
            def _(eng):
                eng.preload_act_table_set("natural_log_exp_and_others")
                eng.wait_ge(degs, 1)
                eng.activation(lnd[:], deg[:], ACT.Ln).then_inc(lns, 1)
                eng.wait_ge(lns, 1)
                eng.activation(s0[:], lnd[:], ACT.Exp, scale=-0.5).then_inc(lns, 1)
                eng.wait_ge(c.weights_in, c.weights_count)

                def body(i, p):
                    g, b = i - 1, (p + 1) % 2
                    if live(g):
                        eng.wait_ge(zT_ok, g + 1)
                        need(eng, pre_ok, g - 1)
                        eng.activation(xnT[:, b], zT_ps[:], ACT.Identity, bias=c.beta[:, 0:1], scale=c.gamma[:, 0:1])\
                           .then_inc(xnT_ok, 1)
                    g, b = i - 2, p
                    if live(g):
                        eng.wait_ge(pre_ok, g + 1)
                        eng.activation(ab[:, b], pre_ps[b][:], ACT.Abs).then_inc(ab_ok, 1)
                        eng.wait_ge(ab_ok, g + 1)
                        eng.activation(ab[:, b], ab[:, b], ACT.Exp, scale=-1.0).then_inc(ex_ok, 1)
                        eng.wait_ge(ex_ok, g + 1)
                        need(eng, x_ok, g - 1)
                        eng.activation(lg[:, b], ab[:, b], ACT.Ln, bias=1.0).then_inc(lg_ok, 1)
                pipeline(eng, body, LAG)

            @block.tensor
            def _(eng):
                eng.wait_ge(c.weights_in, c.weights_count)
                eng.wait_ge(c.ones_ok, 1)
                eng.wait_ge(c.adj_in, 16)
                for t in range(T):
                    for j in range(2):
                        q = slice(N * j, N * j + N)
                        m = eng.matmul(deg_ps[q, t:t + 1], c.adj[q, t, :], c.ones[q, 0:1], start=True, stop=True)
                m.then_inc(colsum, 1)

                def body(i, p):
                    g, b = i - 2, p
                    if live(g):
                        eng.wait_ge(xn_ok, g + 1)
                        eng.wait_ge(lapT_ok, g + 1)
                        need(eng, nbT_ok, g)
                        for t in range(GT):
                            m = eng.matmul(nb_ps[:, t, :], xn[:, b, t, :], lapT[:, b, t, :], start=True, stop=True)
                        m.then_inc(nb_ok, 1)
                    g, b = i - 1, (p + 1) % 2
                    if live(g):
                        eng.wait_ge(adj_ok, g + 1)
                        need(eng, lapT_ok, g)
                        for t in range(GT):
                            m = eng.transpose(adjT_ps[:, t, :], adj_s[:, b, t, :], c.ident[:])
                        m.then_inc(adjT_ok, 1)
                        eng.wait_ge(z_ok, g + 1)
                        need(eng, xnT_ok, g)
                        for t in range(GT):
                            m = eng.transpose(zT_ps[:, t, :], z[:, b, t, :], c.ident[:])
                        m.then_inc(zT_ok, 1)
                    g, b = i - 2, p
                    if live(g):
                        eng.wait_ge(nbT_ok, g + 1)
                        need(eng, sp_ok, g - 1)
                        for t in range(GT):
                            eng.matmul(pre_ps[b][:, t, :], xnT[:, b, t, :], c.w_self[:], start=True, stop=False)
                            m = eng.matmul(pre_ps[b][:, t, :], nbT[:, b, t, :], c.w_neigh[:], start=False, stop=True)
                        m.then_inc(pre_ok, 1)
                pipeline(eng, body, LAG)
        signals.give_back()


def attention(nc, c):
    LAG, U = 4, 4
    TB = 2 * GT
    with ExitStack() as ctx:
        def sb(name, shape, dt=F32):
            return ctx.enter_context(nc.sbuf_tensor("b_" + name, shape, dt))

        signals = Signals(nc, "b")
        sem = signals.new

        st = sb("st", [P, 2, GT, 6])
        mv = sb("mv", [P, 2, GT, 2])
        var = sb("var", [P, 2, 2 * GT])
        rr = sb("rr", [P, 2, 2 * GT])
        h = sb("h", [P, 2, GT, D])
        f = sb("f", [P, U, GT, D])
        hT = sb("hT", [P, 2, GT, P])
        qk = sb("qk", [P, 2, GT, 2 * H, HD])
        turn = sb("turn", [P, GT * 6, HD])
        half = sb("half", [P, GT * 6, HD])
        qT = sb("qT", [P, 2, GT * P])
        kT = sb("kT", [P, 2, GT * P])
        vx = sb("vx", [P, 2, 2 * GT, KV, 2, HD + 1])
        s_sb = sb("s_sb", [P, 2, GT, H, N])
        mx = sb("mx", [P, GT, H])
        pT = sb("pT", [P, 2, GT, KV, P])
        rcp = sb("rcp", [P, 2, 2 * H])
        y = sb("y", [P, 2, GT, D])
        yT = sb("yT", [P, 2, GT, P])
        junk = sb("junk", [P, GT, D])
        ssq = sb("ssq", [P, 2, GT])
        var3 = sb("var3", [P, 2, GT])
        r3 = sb("r3", [P, 2, GT])
        flat = sb("flat", [P, 2, TB, D])
        fT = sb("fT", [P, 2, GT, P])
        lg = sb("lg", [P, TB, NE])
        m1 = sb("m1", [P, TB]); m2 = sb("m2", [P, TB]); km = sb("km", [P, TB])
        ra = sb("ra", [P, TB, NE]); rb = sb("rb", [P, TB, NE])
        ex = sb("ex", [P, TB, NE + 1])
        m16 = sb("m16", [P, TB, NE], BF16)
        zsum = sb("zsum", [P, TB]); wa = sb("wa", [P, TB]); wb = sb("wb", [P, TB])
        slot = sb("slot", [P, 2, 2, TB], I32)
        ps = ctx.enter_context(nc.psum_tensor("b_ps", [P, 8, 512], F32))

        s_ps = ps[:, 0:4, 0:GT * N].rearrange("p h (t n) -> p h t n", n=N)
        v_ps = ps[:, 0, :].rearrange("p (t j e) -> p t j e", t=GT, j=2)
        qT_ps, kT_ps = ps[:, 1, :], ps[:, 2, :]
        fT_ps = ps[:, 3, :].rearrange("p (t f) -> p t f", f=P)
        hT_ps = ps[:, 4, :].rearrange("p (t f) -> p t f", f=P)
        qk_ps = ps[:, 4:6, 0:384].rearrange("p k (a d) -> p k a d", d=HD)
        lg_ps = ps[:, 5, 0:GT * NE].rearrange("p (t e) -> p t e", e=NE)
        rank_ps = ps[:, 4, 0:TB * NE].rearrange("p (t e) -> p t e", e=NE)
        pT_ps = ps[:, 6:8, :].rearrange("p k (t g q) -> p (k t) g q", t=2, g=KV)
        y_ps = ps[:, 6:8, 0:4 * KV * (HD + 1) * 1 * 1].rearrange("p k (a e) -> p k a e", e=HD + 1)
        yT_ps = ps[:, 6, :].rearrange("p (t f) -> p t f", f=P)
        at_ps = ps[:, 7, :].rearrange("p (t f) -> p t f", f=P)

        s = Memory()
        s.bn, s.stats, s.masked, s.top = sem("bn"), sem("stats"), sem("masked"), sem("top")
        s.centred, s.turned1, s.turned, s.recip = sem("centred"), sem("turned1"), sem("turned"), sem("recip")
        s.y_ok, s.h_ok, s.x1_ok, s.x_ok = sem("y_ok"), sem("h_ok"), sem("x1_ok"), sem("x_ok")
        s.flat_ok, s.lg_ok, s.var_ok, s.rr_ok = sem("flat_ok"), sem("lg_ok"), sem("var_ok"), sem("rr_ok")
        s.var3_ok, s.r3_ok, s.hT_done, s.qk_done = sem("var3_ok"), sem("r3_ok"), sem("hT_done"), sem("qk_done")
        s.v_done, s.qkT_done, s.s_done, s.pT_done = sem("v_done"), sem("qkT_done"), sem("s_done"), sem("pT_done")
        s.y_done, s.yT_done, s.at_done, s.fT_done = sem("y_done"), sem("yT_done"), sem("at_done"), sem("fT_done")
        s.lg_done, s.hT_ok, s.v_ok, s.qkT_ok = sem("lg_done"), sem("hT_ok"), sem("v_ok"), sem("qkT_ok")
        s.e_ok, s.pT_ok, s.yT_ok, s.ssq_ok = sem("e_ok"), sem("pT_ok"), sem("yT_ok"), sem("ssq_ok")
        s.fT_ok, s.rank_in, s.ex_in, s.ex_ok = sem("fT_ok"), sem("rank_in"), sem("ex_in"), sem("ex_ok")
        s.rank_done, s.slot_ok, s.chain, s.filled = sem("rank_done"), sem("slot_ok"), sem("chain"), sem("filled")
        scattered = [sem("scattered0"), sem("scattered1")]
        STEPS = 26

        with nc.Block() as block:
            @block.sync
            def _(sp):
                for to, of in c.late_loads:
                    sp.dma_start(to, of).then_inc(c.late_in, 16)
                sp.dma_start(c.w13[:], c.dram["w13"]).then_inc(c.experts_in, 16)
                for k in range(HC):
                    n = min(P, HID - k * P)
                    if n < P:
                        sp.wait_ge(c.pad_ok, 1)
                    sp.dma_start(c.w2[0:n, :, k, :], c.dram["w2"][k * P:k * P + n]).then_inc(c.experts_in, 16)

            @block.vector
            def _(eng):
                cos = c.tab[:, T_COS:T_COS + HD].unsqueeze(1).unsqueeze(1)
                sin = c.tab[:, T_SIN:T_SIN + HD].unsqueeze(1).unsqueeze(1)
                causal = c.tab[:, T_CAUSAL:T_CAUSAL + N].unsqueeze(1).unsqueeze(1).broadcast_to([P, H, GT, N])
                eng.memset(c.cum[:], 0.0).then_inc(s.filled, 1)
                eng.memset(c.cum16[:], 0.0).then_inc(s.filled, 1)
                eng.tensor_copy(c.low16[:], c.tab[:, T_LOW:T_LOW + P]).then_inc(s.filled, 1)

                def route(g, q):
                    par = q // 2
                    base, count = (g - 1) * (STEPS // 2), [0]

                    def step(instruction):
                        count[0] += 1
                        instruction.then_inc(s.chain, 1)
                        eng.wait_ge(s.chain, base + count[0])

                    tiles = bass.ds((g - 1) * GT, TB)
                    o1, o2 = c.o1[:, tiles, :], c.o2[:, tiles, :]
                    rev = c.tab[:, T_REV:T_REV + NE].unsqueeze(1).broadcast_to([P, TB, NE])

                    def wide(a):
                        return a.unsqueeze(2).broadcast_to([P, TB, NE])

                    step(eng.tensor_reduce(m1[:], lg[:], AX, ALU.max))
                    step(eng.tensor_tensor(ra[:], lg[:], wide(m1[:]), ALU.is_equal))
                    step(eng.tensor_tensor(ra[:], ra[:], rev, ALU.mult))
                    step(eng.tensor_reduce(km[:], ra[:], AX, ALU.max))
                    step(eng.tensor_tensor(o1, ra[:], wide(km[:]), ALU.is_equal))
                    step(eng.scalar_tensor_tensor(rb[:], o1, NEG, lg[:], ALU.mult, ALU.add))
                    step(eng.tensor_reduce(m2[:], rb[:], AX, ALU.max))
                    step(eng.tensor_tensor(rb[:], rb[:], wide(m2[:]), ALU.is_equal))
                    step(eng.tensor_tensor(rb[:], rb[:], rev, ALU.mult))
                    step(eng.tensor_reduce(km[:], rb[:], AX, ALU.max))
                    step(eng.tensor_tensor(o2, rb[:], wide(km[:]), ALU.is_equal))
                    step(eng.tensor_tensor(m16[:], o1, o2, ALU.add))
                    eng.tensor_tensor(ra[:], o1, o2, ALU.add).then_inc(s.rank_in, 2)
                    eng.tensor_tensor(ex[:, :, 0:NE], lg[:], wide(m1[:]), ALU.subtract)
                    eng.tensor_tensor(ex[:, :, NE], m2[:], m1[:], ALU.subtract).then_inc(s.ex_in, 2)
                    eng.wait_ge(s.rank_done, g + 1)
                    eng.wait_ge(s.rank_in, g + 1)
                    step(eng.tensor_tensor(rb[:], rank_ps, c.tab[:, T_REGION:T_REGION + NE].unsqueeze(1)
                                           .broadcast_to([P, TB, NE]), ALU.add))
                    step(eng.tensor_reduce(km[:, 0:NE], ra[:].rearrange("p t e -> p e t"), AX, ALU.add))
                    step(eng.tensor_tensor(c.cum[:], c.cum[:], km[:, 0:NE], ALU.add))
                    step(eng.tensor_copy(c.cum16[:], c.cum[:]))
                    step(eng.tensor_tensor(ra[:], rb[:], o1, ALU.mult))
                    step(eng.tensor_reduce(c.place[:, 0, tiles], ra[:], AX, ALU.add))
                    step(eng.tensor_tensor(ra[:], rb[:], o2, ALU.mult))
                    step(eng.tensor_reduce(c.place[:, 1, tiles], ra[:], AX, ALU.add))
                    need(eng, scattered[par], 64 * (g - q))
                    eng.tensor_copy(slot[:, par], c.place[:, :, tiles]).then_inc(s.slot_ok, 2)
                    eng.wait_ge(s.ex_ok, g + 1)
                    step(eng.tensor_reduce(zsum[:], ex[:, :, 0:NE], AX, ALU.add))
                    step(eng.scalar_tensor_tensor(wa[:], zsum[:], 1e-9, ex[:, :, NE], ALU.mult, ALU.add))
                    step(eng.tensor_scalar(wa[:], wa[:], 1.0, None, ALU.add))
                    step(eng.reciprocal(wb[:], wa[:]))
                    step(eng.tensor_tensor(c.weight[:, 1, tiles], wb[:], ex[:, :, NE], ALU.mult))
                    step(eng.tensor_copy(c.weight[:, 0, tiles], wb[:]))
                    assert count[0] == STEPS

                def body(i, q):
                    b = q % 2
                    g = i - 2
                    if live(g):
                        eng.wait_ge(s.s_done, g + 1)
                        need(eng, s.pT_done, g - 1)
                        eng.tensor_tensor(s_sb[:, b].rearrange("p t h n -> p h t n"), s_ps, causal, ALU.add).then_inc(s.masked, 1)
                    g = i
                    if live(g):
                        for t in range(GT):
                            m = eng.bn_stats(st[:, b, t, :], c.x[:, bass.ds(g * GT + t, 1), :].rearrange("p a f -> p (a f)"))
                        m.then_inc(s.bn, 1)
                    g = i - 2
                    if live(g):
                        eng.wait_ge(s.masked, g + 1)
                        eng.tensor_reduce(mx[:], s_sb[:, b], AX, ALU.max).then_inc(s.top, 1)
                    g = i
                    if live(g):
                        eng.wait_ge(s.bn, g + 1)
                        need(eng, s.rr_ok, g - 1)
                        alone(eng, c.passed)
                        for t in range(GT):
                            m = eng.bn_aggr(mv[:, b, t, :], st[:, b, t, :])
                        m.then_inc(s.stats, 1)
                    g = i - 2
                    if live(g):
                        eng.wait_ge(s.top, g + 1)
                        eng.tensor_tensor(s_sb[:, b], s_sb[:, b], mx[:].unsqueeze(3)
                                          .broadcast_to([P, GT, H, N]), ALU.subtract).then_inc(s.centred, 1)
                    g = i - 4
                    if live(g):
                        eng.wait_ge(s.r3_ok, g + 1)
                        need(eng, scattered[q // 2], 64 * (g - q))
                        for t in range(GT):
                            m = eng.tensor_scalar(flat[:, q // 2, q % 2 * GT + t, :], f[:, q, t, :], r3[:, b, t:t + 1], None,
                                                  ALU.mult)
                        m.then_inc(s.flat_ok, 1)
                    g = i - 3
                    if live(g):
                        eng.wait_ge(s.y_done, g + 1)
                        eng.reciprocal(rcp[:], y_ps[:, :, :, HD]).then_inc(s.recip, 1)
                        eng.wait_ge(s.recip, g + 1)
                        need(eng, s.yT_done, g - 1)
                        eng.tensor_tensor(y[:, 1 - b].rearrange("p (k t) (a d) -> p k (t a) d", k=2, d=HD), y_ps[:, :, :, 0:HD],
                                          rcp[:].unsqueeze(3).broadcast_to([P, 2, 2 * H, HD]), ALU.mult).then_inc(s.y_ok, 1)
                    g = i - 1
                    if live(g):
                        o = turn[:].rearrange("p (k a) d -> p k a d", k=2)
                        o2 = half[:].rearrange("p (k a) d -> p k a d", k=2)
                        shape = [P, 2, 2 * 6, HD]
                        lo, hi = slice(0, HD // 2), slice(HD // 2, HD)
                        hshape = [P, 2, 2 * 6, HD // 2]
                        eng.wait_ge(s.qk_done, g + 1)
                        need(eng, s.qkT_done, g - 1)
                        need(eng, s.turned, g)
                        eng.tensor_tensor(o, qk_ps, cos.broadcast_to(shape), ALU.mult)
                        eng.tensor_tensor(o2[:, :, :, lo], qk_ps[:, :, :, hi], sin[:, :, :, lo].broadcast_to(hshape), ALU.mult)
                        eng.tensor_tensor(o2[:, :, :, hi], qk_ps[:, :, :, lo], sin[:, :, :, hi].broadcast_to(hshape), ALU.mult)\
                           .then_inc(s.turned1, 1)
                        eng.wait_ge(s.turned1, g + 1)
                        t4, h4 = (a[:].rearrange("p (t a) d -> p t a d", t=GT) for a in (turn, half))
                        eng.tensor_tensor(qk[:, 1 - b, :, 0:H], t4[:, :, 0:H], h4[:, :, 0:H], ALU.add)
                        for k in range(KV):
                            one = slice(H + k, H + k + 1)
                            m = eng.tensor_tensor(qk[:, 1 - b, :, H + 2 * k:H + 2 * k + 2], t4[:, :, one].broadcast_to([P, GT, 2, HD]),
                                                  h4[:, :, one].broadcast_to([P, GT, 2, HD]), ALU.add)
                        m.then_inc(s.turned, 1)
                    g = i
                    if live(g):
                        eng.wait_ge(s.rr_ok, g + 1)
                        need(eng, s.hT_done, g - 1)
                        need(eng, s.flat_ok, g - 3)
                        for t in range(GT):
                            x_t = c.x[:, bass.ds(g * GT + t, 1), :].rearrange("p a f -> p (a f)")
                            eng.tensor_scalar(h[:, b, t, :], x_t, mv[:, b, t, 0:1], rr[:, b, GT + t:GT + t + 1],
                                              ALU.subtract, ALU.mult)
                            m = eng.tensor_scalar(f[:, q, t, :], x_t, mv[:, b, t, 0:1], rr[:, b, t:t + 1],
                                                  ALU.subtract, ALU.mult)
                        m.then_inc(s.h_ok, 1)
                    g = i - 3
                    if live(g):
                        fq = f[:, (q + 1) % U]
                        eng.wait_ge(s.at_done, g + 1)
                        eng.wait_ge(s.h_ok, g + 1)
                        eng.tensor_tensor(fq, at_ps, fq, ALU.add).then_inc(s.x1_ok, 1)
                        eng.wait_ge(s.x1_ok, g + 1)
                        eng.tensor_tensor(c.x[:, tile4(g), :], c.x[:, tile4(g), :], fq, ALU.add).then_inc(s.x_ok, 1)
                    g = i - 4
                    if live(g):
                        eng.wait_ge(s.lg_done, g + 1)
                        eng.tensor_copy(lg[:, b * GT:b * GT + GT, :], lg_ps).then_inc(s.lg_ok, 1)
                        if q % 2:
                            eng.wait_ge(s.lg_ok, g + 1)
                            route(g, q)
                pipeline(eng, body, LAG, unroll=U, lead=U)

            @block.gpsimd
            def _(eng):
                eng.memset(c.w2[64:P, :, HC - 1, :], 0.0).then_inc(c.pad_ok, 1)
                eng.wait_ge(c.pad_ok, 1)
                eng.memset(vx[:], 0.0).then_inc(s.filled, 1)
                eng.wait_ge(s.filled, 4)
                eng.memset(vx[0:N, :, :, :, 0, HD:HD + 1], 1.0).then_inc(s.filled, 1)
                eng.wait_ge(s.filled, 5)
                eng.memset(vx[N:P, :, :, :, 1, HD:HD + 1], 1.0).then_inc(s.filled, 1)
                eng.wait_ge(s.filled, 6)

                def body(i, q):
                    b = q % 2
                    g = i
                    if live(g):
                        eng.wait_ge(s.stats, g + 1)
                        alone(eng, c.passed)
                        eng.tensor_scalar(var[:, b, 0:GT], mv[:, b, :, 1], 1.0, EPS, ALU.mult, ALU.add)
                        eng.tensor_scalar(var[:, b, GT:2 * GT], mv[:, b, :, 1], 1.0 + EPS_RMS, EPS_RMS * EPS, ALU.mult, ALU.add)\
                           .then_inc(s.var_ok, 1)
                        eng.wait_ge(s.var_ok, g + 1)
                        need(eng, s.h_ok, g - 1)
                        eng.tensor_tensor(rr[:, b], var[:, b], c.minus_half[:], ALU.pow).then_inc(s.rr_ok, 1)
                    g = i - 3
                    if live(g):
                        eng.wait_ge(s.ssq_ok, g + 1)
                        alone(eng, c.passed)
                        eng.tensor_scalar(var3[:, 1 - b], ssq[:, 1 - b], 1.0 / D, EPS_RMS, ALU.mult, ALU.add).then_inc(s.var3_ok, 1)
                        eng.wait_ge(s.var3_ok, g + 1)
                        need(eng, s.flat_ok, g - 1)
                        eng.tensor_tensor(r3[:, 1 - b], var3[:, 1 - b], c.minus_half[:, 0:GT], ALU.pow).then_inc(s.r3_ok, 1)
                    for g, first in ((i - 4, 0), (i - 5, GT)):
                        par = (q if not first else q - 1) // 2 % 2
                        if live(g) and (q + (first > 0)) % 2:
                            eng.wait_ge(s.slot_ok, g + 1)
                            alone(eng, c.passed)
                            for t in range(first, first + GT):
                                for k in range(2):
                                    eng.indirect_dma_start(
                                        c.dram["rows"], bass.IndirectOffsetOnAxis(ap=slot[:, par, k, t:t + 1], axis=0),
                                        flat[:, par, t, :], None).then_inc(scattered[par], 16)
                pipeline(eng, body, LAG + 1, unroll=U, lead=U - 1)
                for k in range(2):
                    eng.wait_ge(scattered[k], 16 * 2 * TB * (T // TB // 2))

            @block.scalar
            def _(eng):
                eng.preload_act_table_set("exp_and_others")
                eng.wait_ge(s.filled, 6)

                def body(i, q):
                    b = q % 2
                    g = i - 1
                    if live(g):
                        eng.wait_ge(s.hT_done, g + 1)
                        need(eng, s.v_done, g - 1)
                        eng.activation(hT[:, 1 - b], hT_ps, ACT.Copy, scale=c.ln1).then_inc(s.hT_ok, 1)
                    g = i - 3
                    if live(g):
                        eng.wait_ge(s.pT_done, g + 1)
                        need(eng, s.y_done, g - 1)
                        eng.activation(pT[:, 1 - b], pT_ps, ACT.Copy).then_inc(s.pT_ok, 1)
                    g = i - 2
                    if live(g):
                        eng.wait_ge(s.centred, g + 1)
                        eng.activation(s_sb[:, b], s_sb[:, b], ACT.Exp, scale=float(1.0 / np.sqrt(np.float32(HD)))).then_inc(s.e_ok, 1)
                    g = i - 1
                    if live(g):
                        eng.wait_ge(s.v_done, g + 1)
                        need(eng, s.y_done, g - 1)
                        for k in range(2):
                            r = slice(N * k, N * k + N)
                            m = eng.activation(vx[r, 1 - b, :, :, k, 0:HD],
                                               v_ps[r].rearrange("p t j (g e) -> p (t j) g e", g=KV), ACT.Copy)
                        m.then_inc(s.v_ok, 1)
                    g = i - 4
                    if live(g):
                        eng.wait_ge(s.fT_done, g + 1)
                        need(eng, s.lg_done, g - 1)
                        eng.activation(fT[:, b], fT_ps, ACT.Copy, scale=c.ln2).then_inc(s.fT_ok, 1)
                    g = i - 3
                    if live(g):
                        eng.wait_ge(s.yT_done, g + 1)
                        need(eng, s.at_done, g - 1)
                        eng.activation(yT[:, 1 - b], yT_ps, ACT.Copy).then_inc(s.yT_ok, 1)
                    g = i - 1
                    if live(g):
                        eng.wait_ge(s.qkT_done, g + 1)
                        need(eng, s.s_done, g - 1)
                        eng.activation(qT[:, 1 - b], qT_ps, ACT.Copy)
                        eng.activation(kT[:, 1 - b], kT_ps, ACT.Copy).then_inc(s.qkT_ok, 1)
                    g = i - 3
                    if live(g):
                        eng.wait_ge(s.x1_ok, g + 1)
                        need(eng, s.var3_ok, g - 1)
                        need(eng, s.ssq_ok, g)
                        for t in range(GT):
                            m = eng.activation(junk[:, t, :], f[:, (q + 1) % U, t, :], ACT.Square, accum_out=ssq[:, 1 - b, t:t + 1])
                        m.then_inc(s.ssq_ok, 1)
                    g = i - 4
                    if live(g) and q % 2:
                        eng.wait_ge(s.ex_in, g + 1)
                        eng.activation(ex[:], ex[:], ACT.Exp).then_inc(s.ex_ok, 2)
                pipeline(eng, body, LAG, unroll=U, lead=U)

            @block.tensor
            def _(eng):
                eng.wait_ge(s.filled, 6)

                def body(i, q):
                    b = q % 2
                    g = i - 2
                    if live(g):
                        eng.wait_ge(s.qkT_ok, g + 1)
                        eng.wait_ge(s.v_ok, g + 1)
                        need(eng, s.fT_ok, g - 2)
                        for t in range(GT):
                            for j in range(2):
                                cols = slice(t * P + j * N, t * P + j * N + N)
                                for hd in range(H):
                                    r = slice(HD * hd, HD * hd + HD)
                                    m = eng.matmul(s_ps[N * j:N * j + N, hd, t, :], qT[r, b, cols], kT[r, b, cols],
                                                   start=True, stop=True)
                        m.then_inc(s.s_done, 1)
                    g = i - 1
                    if live(g):
                        eng.wait_ge(s.h_ok, g + 1)
                        need(eng, s.turned1, g)
                        need(eng, s.slot_ok, g - 3 - q % 2)
                        for t in range(GT):
                            m = eng.transpose(hT_ps[:, t, :], h[:, 1 - b, t, :], c.ident[:])
                        m.then_inc(s.hT_done, 1)
                    g = i - 3
                    if live(g):
                        eng.wait_ge(s.e_ok, g + 1)
                        need(eng, s.yT_ok, g)
                        need(eng, s.x1_ok, g)
                        for t in range(GT):
                            for k in range(KV):
                                m = eng.transpose(pT_ps[:, t, k, :], s_sb[:, 1 - b, t, 2 * k:2 * k + 2, :].rearrange("p a n -> p (a n)"), c.ident[:])
                        m.then_inc(s.pT_done, 1)
                    g = i - 1
                    if live(g):
                        eng.wait_ge(s.hT_ok, g + 1)
                        need(eng, s.lg_ok, g - 3)
                        for t in range(GT):
                            m = eng.matmul(qk_ps[:, t // 2, t % 2 * 6:t % 2 * 6 + 6, :], hT[:, 1 - b, t, :], c.wqk[:],
                                           start=True, stop=True)
                        m.then_inc(s.qk_done, 1)
                    g = i - 3
                    if live(g):
                        eng.wait_ge(s.pT_ok, g + 1)
                        for t in range(GT):
                            for j in range(2):
                                for k in range(KV):
                                    o = (t % 2 * KV + k) * 2
                                    m = eng.matmul(y_ps[N * j:N * j + N, t // 2, o:o + 2, :],
                                                   pT[:, 1 - b, t, k, N * j:N * j + N], vx[:, 1 - b, 2 * t + j, k],
                                                   start=True, stop=True)
                        m.then_inc(s.y_done, 1)
                    g = i - 1
                    if live(g):
                        need(eng, s.masked, g)
                        for t in range(GT):
                            for j in range(2):
                                for k in range(2):
                                    m = eng.matmul(v_ps[N * k:N * k + N, t, j, :], hT[:, 1 - b, t, N * j:N * j + N], c.wv[:],
                                                   start=True, stop=True)
                        m.then_inc(s.v_done, 1)
                    g = i - 4
                    if live(g):
                        eng.wait_ge(s.flat_ok, g + 1)
                        for t in range(GT):
                            m = eng.transpose(fT_ps[:, t, :], flat[:, q // 2, b * GT + t, :], c.ident[:])
                        m.then_inc(s.fT_done, 1)
                    g = i - 3
                    if live(g):
                        eng.wait_ge(s.y_ok, g + 1)
                        for t in range(GT):
                            m = eng.transpose(yT_ps[:, t, :], y[:, 1 - b, t, :], c.ident[:])
                        m.then_inc(s.yT_done, 1)
                        eng.wait_ge(s.yT_ok, g + 1)
                        for t in range(GT):
                            m = eng.matmul(at_ps[:, t, :], yT[:, 1 - b, t, :], c.wo[:], start=True, stop=True)
                        m.then_inc(s.at_done, 1)
                    g = i - 1
                    if live(g):
                        eng.wait_ge(s.turned, g + 1)
                        for t in range(GT):
                            qt = qk[:, 1 - b, t, 0:H, :].rearrange("p a d -> p (a d)")
                            kt = qk[:, 1 - b, t, H:2 * H, :].rearrange("p a d -> p (a d)")
                            eng.transpose(qT_ps[:, t * P:t * P + P], qt, c.ident[:])
                            m = eng.transpose(kT_ps[:, t * P:t * P + P], kt, c.ident[:])
                        m.then_inc(s.qkT_done, 1)
                    g = i - 4
                    if live(g):
                        eng.wait_ge(s.fT_ok, g + 1)
                        if isinstance(i, int):
                            need(eng, s.turned1, min(i, G))
                        else:
                            eng.wait_ge(s.turned1, i)
                        for t in range(GT):
                            m = eng.matmul(lg_ps[:, t, :], fT[:, b, t, :], c.router[:], start=True, stop=True)
                        m.then_inc(s.lg_done, 1)
                        if q % 2:
                            eng.wait_ge(s.rank_in, g + 1)
                            eng.matmul(rank_ps, c.low16[:], m16[:], start=True, stop=False)
                            for k in range(1, TB):
                                eng.matmul(rank_ps[:, k:TB, :], c.ones16[:], m16[:, 0:TB - k, :], start=False, stop=False)
                            eng.matmul(rank_ps, c.ones16[:], c.cum16[:].unsqueeze(1).broadcast_to([P, TB, NE]),
                                       start=False, stop=True).then_inc(s.rank_done, 2)
                pipeline(eng, body, LAG, unroll=U, lead=U)
        signals.give_back()


def moe_phases(nc, c, sb, sem):
    c.w13 = sb("w13", [D, NE, 2, HID])
    c.w2 = sb("w2", [P, NE, HC, D])
    c.o1 = sb("o1", [P, T, NE]); c.o2 = sb("o2", [P, T, NE])
    c.place = sb("place", [P, 2, T])
    c.weight = sb("weight", [P, 2, T])
    c.cum = sb("cum", [P, NE]); c.cum16 = sb("cum16", [P, NE], BF16)
    c.experts_in, c.pad_ok = sem("experts_in"), sem("pad_ok")
    attention(nc, c)
    plan(nc, c, sb, sem)
    experts(nc, c)


def plan(nc, c, sb, sem):
    c.back = sb("back", [P, 2, T], I32)
    c.expert = sb("expert", [P, SLOTS], I32)
    c.source = sb("source", [P, SLOTS], I32)
    with ExitStack() as ctx:
        def tmp(name, shape, dt=F32):
            return ctx.enter_context(nc.sbuf_tensor("c_" + name, shape, dt))

        count = tmp("count", [P, NE]); more = tmp("more", [P, NE, N]); tiles = tmp("tiles", [P, NE])
        start = tmp("start", [P, NE + 1]); shift = tmp("shift", [P, NE]); wide = tmp("wide", [P, T, NE])
        moved = tmp("moved", [P, 2, T]); past = tmp("past", [P, SLOTS, NE]); part = tmp("part", [P, SLOTS, NE])
        which = tmp("which", [P, SLOTS]); begun = tmp("begun", [P, SLOTS]); row = tmp("row", [P, SLOTS])
        used = tmp("used", [P, SLOTS]); pad = tmp("pad", [P, NE]); pad_at = tmp("pad_at", [P, NE], I32)
        zeros = tmp("zeros", [P, D])
        signals = Signals(nc, "c")
        ps = ctx.enter_context(nc.psum_tensor("c_ps", [P, NE], F32))
        counted = signals.new("counted")
        chain = signals.new("chain")
        pads_ok = signals.new("pads_ok")
        zero_ok = signals.new("zero_ok")
        padded = signals.new("padded")

        with nc.Block() as block:
            @block.tensor
            def _(eng):
                eng.matmul(ps[:], c.ones16[:], c.cum16[:], start=True, stop=True).then_inc(counted, 1)

            @block.vector
            def _(eng):
                n = [0]

                def step(instruction):
                    n[0] += 1
                    instruction.then_inc(chain, 1)
                    eng.wait_ge(chain, n[0])

                regions = c.tab[:, T_REGION:T_REGION + NE]
                eng.wait_ge(counted, 1)
                step(eng.tensor_copy(count[:], ps[:]))
                step(eng.tensor_tensor(pad[:], count[:], regions, ALU.add))
                step(eng.tensor_scalar(pad[:], pad[:], c.tab[:, T_ROW:T_ROW + 1], None, ALU.add))
                eng.tensor_copy(pad_at[:], pad[:]).then_inc(pads_ok, 1)
                step(eng.tensor_tensor(more[:], count[:].unsqueeze(2).broadcast_to([P, NE, N]),
                                       c.tab[:, T_TILE:T_TILE + N].unsqueeze(1).broadcast_to([P, NE, N]), ALU.is_gt))
                step(eng.tensor_reduce(tiles[:], more[:], AX, ALU.add))
                step(eng.memset(start[:, 0:1], 0.0))
                for e in range(NE):
                    step(eng.tensor_tensor(start[:, e + 1:e + 2], start[:, e:e + 1], tiles[:, e:e + 1], ALU.add))
                step(eng.scalar_tensor_tensor(shift[:], start[:, 0:NE], float(P), regions, ALU.mult, ALU.subtract))
                for k, o in enumerate((c.o1, c.o2)):
                    step(eng.tensor_tensor(wide[:], o[:], shift[:].unsqueeze(1).broadcast_to([P, T, NE]), ALU.mult))
                    step(eng.tensor_reduce(moved[:, k], wide[:], AX, ALU.add))
                step(eng.tensor_tensor(moved[:], moved[:], c.place[:], ALU.add))
                step(eng.tensor_copy(c.back[:], moved[:]))
                slots = c.tab[:, T_SLOT:T_SLOT + SLOTS]
                step(eng.tensor_tensor(past[:], slots.unsqueeze(2).broadcast_to([P, SLOTS, NE]),
                                       start[:, 1:NE + 1].unsqueeze(1).broadcast_to([P, SLOTS, NE]), ALU.is_ge))
                step(eng.tensor_reduce(which[:], past[:], AX, ALU.add))
                step(eng.tensor_tensor(part[:], past[:], tiles[:].unsqueeze(1).broadcast_to([P, SLOTS, NE]), ALU.mult))
                step(eng.tensor_reduce(begun[:], part[:], AX, ALU.add))
                step(eng.tensor_tensor(row[:], slots, begun[:], ALU.subtract))
                step(eng.tensor_scalar(row[:], row[:], float(P), None, ALU.mult))
                step(eng.scalar_tensor_tensor(row[:], which[:], float(REGION), row[:], ALU.mult, ALU.add))
                step(eng.tensor_scalar(used[:], slots, start[:, NE:NE + 1], None, ALU.is_lt))
                step(eng.tensor_tensor(row[:], row[:], used[:], ALU.mult))
                step(eng.tensor_copy(c.source[:], row[:]))
                step(eng.tensor_scalar(which[:], which[:], float(NE - 1), None, ALU.min))
                step(eng.tensor_copy(c.expert[:], which[:]))

            @block.gpsimd
            def _(eng):
                eng.memset(zeros[:], 0.0).then_inc(zero_ok, 1)
                eng.wait_ge(zero_ok, 1)
                eng.wait_ge(pads_ok, 1)
                for e in range(NE):
                    eng.indirect_dma_start(c.dram["rows"], bass.IndirectOffsetOnAxis(ap=pad_at[:, e:e + 1], axis=0),
                                           zeros[:], None).then_inc(padded, 16)
                eng.wait_ge(padded, 16 * NE)
        signals.give_back()


def experts(nc, c):
    LAG, U = 4, 4
    with ExitStack() as ctx:
        def sb(name, shape, dt=F32):
            return ctx.enter_context(nc.sbuf_tensor("d_" + name, shape, dt))

        rows = sb("rows", [P, U, D])
        rT = sb("rT", [P, 2, P])
        th = sb("th", [P, 2, HID])
        u = sb("u", [P, 2, HID])
        hid = sb("hid", [P, 2, HC * P])
        hT = sb("hT", [P, 2, HC, P])
        y = sb("y", [P, U, D])
        keep = sb("keep", [P, T, N])
        signals = Signals(nc, "d")
        ps = ctx.enter_context(nc.psum_tensor("d_ps", [P, 8, 512], F32))
        a_ps = [ps[:, 0, 0:HID], ps[:, 1, 0:HID]]
        b_ps = [ps[:, 2, 0:HID], ps[:, 3, 0:HID]]
        rT_ps = [ps[:, 4, 0:P], ps[:, 7, 0:P]]
        hT_ps = ps[:, 5, 0:HC * P].rearrange("p (k r) -> p k r", k=HC)
        y_ps = ps[:, 6, 0:D]

        s = Memory()
        s.rT_done, s.rT_ok, s.ab_done, s.th_ok = signals.new("rT_done"), signals.new("rT_ok"), signals.new("ab_done"), signals.new("th_ok")
        s.u_ok, s.hid_ok, s.hT_done, s.hT_ok = signals.new("u_ok"), signals.new("hid_ok"), signals.new("hT_done"), signals.new("hT_ok")
        s.y_done, s.y_ok, s.pad = signals.new("y_done"), signals.new("y_ok"), signals.new("pad")
        s.a_done = signals.new("a_done")
        loaded = [signals.new(f"loaded{k}") for k in range(U)]
        stored = [signals.new(f"stored{k}") for k in range(U)]

        def run(eng, body):
            pipeline(eng, body, LAG, groups=SLOTS, unroll=U, lead=U)

        mask = sb("mask", [P, T, N], I32)
        mask_in = signals.new("mask_in")
        mask_ok = signals.new("mask_ok")

        with nc.Block() as block:
            @block.gpsimd
            def _(eng):
                eng.wait_ge(mask_in, 32)
                eng.tensor_scalar(c.masked[:], mask[:], 0.0, None, ALU.is_equal).then_inc(mask_ok, 1)
                eng.wait_ge(mask_ok, 1)
                eng.tensor_scalar(keep[:], c.masked[:], -1.0, 1.0, ALU.mult, ALU.add).then_inc(mask_ok, 1)
                eng.wait_ge(mask_ok, 2)
                eng.tensor_tensor(c.adj[:], c.adj[:], keep[:], ALU.mult).then_inc(mask_ok, 1)
                eng.tensor_scalar(c.masked[:], c.masked[:], NEG, None, ALU.mult).then_inc(mask_ok, 1)

            @block.sync
            def _(eng):
                for j in range(2):
                    eng.dma_start(mask[N * j:N * j + N], c.dram["nodemask"].rearrange("(t j) n -> j t n", j=2)[j]
                                  .partition_broadcast(N)).then_inc(mask_in, 16)

                def body(i, q):
                    g = i
                    if live(g, SLOTS):
                        row = eng.value_load(c.source[0:1, bass.ds(g, 1)], min_val=0, max_val=NE * REGION - P)
                        need(eng, s.rT_done, g - U + 1)
                        eng.dma_start(rows[:, q, :], c.dram["rows"][bass.ds(row, P), :]).then_inc(loaded[q], 16)
                    g = i - 7
                    if live(g, SLOTS):
                        eng.wait_ge(s.y_ok, g + 1)
                        eng.dma_start(c.dram["picked"][bass.ds(g * P, P), :], y[:, (q + 1) % U, :])\
                           .then_inc(stored[(q + 1) % U], 16)
                pipeline(eng, body, 7, groups=SLOTS, unroll=U, lead=U)
                for k in range(U):
                    eng.wait_ge(stored[k], 16 * SLOTS // U)

            @block.tensor
            def _(eng):
                eng.wait_ge(c.experts_in, 16 * (1 + HC))
                eng.wait_ge(s.pad, 1)
                before = [eng.alloc_register(f"expert_before{k}") for k in range(U)]
                now = [eng.alloc_register(f"expert_now{k}") for k in range(U)]

                def prepare(i, count):
                    for k in range(U):
                        if not isinstance(i, int) or i > 0:
                            eng.reg_mov(before[k], now[k])
                    if live(i, SLOTS):
                        eng.load(now, c.expert[0:1, bass.ds(i, U)])

                def expert_of(k):
                    return eng.snap(now[k] if k >= 0 else before[k + U]).with_bounds(min_val=0, max_val=NE - 1)

                def body(i, q):
                    b = q % 2
                    g = i - 1
                    if live(g, SLOTS):
                        eng.wait_ge(loaded[(q - 1) % U], 4 * (g - (q - 1) % U) + 16)
                        need(eng, s.rT_ok, g - 1)
                        eng.transpose(rT_ps[1 - b], rows[:, (q - 1) % U, :], c.ident[:]).then_inc(s.rT_done, 1)
                    g = i - 2
                    if live(g, SLOTS):
                        e = expert_of(q - 2)
                        eng.wait_ge(s.rT_ok, g + 1)
                        need(eng, s.hid_ok, g - 1)
                        for k, (out, done) in enumerate(((a_ps[b], s.a_done), (b_ps[b], s.ab_done))):
                            eng.matmul(out, rT[:, b], c.w13[:, bass.ds(e, 1), k, :].rearrange("p a h -> p (a h)"),
                                       start=True, stop=True).then_inc(done, 1)
                    g = i - 3
                    if live(g, SLOTS):
                        eng.wait_ge(s.hid_ok, g + 1)
                        need(eng, s.hT_ok, g)
                        for k in range(HC):
                            m = eng.transpose(hT_ps[:, k, :], hid[:, 1 - b, k * P:k * P + P], c.ident[:])
                        m.then_inc(s.hT_done, 1)
                    g = i - 4
                    if live(g, SLOTS):
                        e = expert_of(q - 4)
                        eng.wait_ge(s.hT_ok, g + 1)
                        need(eng, s.y_ok, g)
                        for k in range(HC):
                            m = eng.matmul(y_ps, hT[:, b, k, :], c.w2[:, bass.ds(e, 1), k, :].rearrange("p a f -> p (a f)"),
                                           start=(k == 0), stop=(k == HC - 1))
                        m.then_inc(s.y_done, 1)
                pipeline(eng, body, LAG, groups=SLOTS, unroll=U, lead=U, prepare=prepare)

            @block.scalar
            def _(eng):
                def body(i, q):
                    b = q % 2
                    g = i - 1
                    if live(g, SLOTS):
                        eng.wait_ge(s.rT_done, g + 1)
                        need(eng, s.ab_done, g - 1)
                        eng.activation(rT[:, 1 - b], rT_ps[1 - b], ACT.Copy, scale=c.ln2).then_inc(s.rT_ok, 1)
                    g = i - 2
                    if live(g, SLOTS):
                        eng.wait_ge(s.a_done, g + 1)
                        need(eng, s.u_ok, g - 1)
                        eng.activation(th[:, b], a_ps[b], ACT.Tanh, scale=0.5).then_inc(s.th_ok, 1)
                    g = i - 4
                    if live(g, SLOTS):
                        eng.wait_ge(s.y_done, g + 1)
                        need(eng, stored[q], 4 * (g - q))
                        eng.activation(y[:, q, :], y_ps, ACT.Copy).then_inc(s.y_ok, 1)
                run(eng, body)

            @block.vector
            def _(eng):
                eng.memset(hid[:, :, HID:HC * P], 0.0).then_inc(s.pad, 1)

                def body(i, q):
                    b = q % 2
                    g = i - 3
                    if live(g, SLOTS):
                        eng.wait_ge(s.hT_done, g + 1)
                        need(eng, s.y_done, g - 1)
                        eng.tensor_copy(hT[:, 1 - b], hT_ps).then_inc(s.hT_ok, 1)
                    g = i - 2
                    if live(g, SLOTS):
                        eng.wait_ge(s.th_ok, g + 1)
                        eng.scalar_tensor_tensor(u[:, b], th[:, b], 1.0, a_ps[b], ALU.add, ALU.mult).then_inc(s.u_ok, 1)
                        eng.wait_ge(s.u_ok, g + 1)
                        eng.wait_ge(s.ab_done, g + 1)
                        need(eng, s.hT_done, g - 1)
                        eng.scalar_tensor_tensor(hid[:, b, 0:HID], u[:, b], 0.5, b_ps[b], ALU.mult, ALU.mult).then_inc(s.hid_ok, 1)
                run(eng, body)
        signals.give_back()


def last_round(nc, c):
    LAG, U = 5, 4
    with ExitStack() as ctx:
        def sb(name, shape, dt=F32):
            return ctx.enter_context(nc.sbuf_tensor("e_" + name, shape, dt))

        at = sb("at", [P, 2, 2, GT], I32)
        got = sb("got", [P, 2, 2, GT, D])
        st = sb("st", [P, 2, GT, 6]); mv = sb("mv", [P, 2, GT, 2])
        var = sb("var", [P, 2, GT]); rstd = sb("rstd", [P, 2, GT])
        z = sb("z", [P, U, GT, D])
        zT = sb("zT", [P, GT, P]); wT = sb("wT", [P, GT * P])
        sim = sb("sim", [P, GT, N]); top = sb("top", [P, GT]); total = sb("total", [P, GT]); inv = sb("inv", [P, GT])
        att = sb("att", [P, GT, P]); attT = sb("attT", [P, GT, P])
        z2 = sb("z2", [P, 2, GT, D]); z2T = sb("z2T", [P, GT * P])
        h1 = sb("h1", [P, GT * P]); h2 = sb("h2", [P, GT * P])
        e1 = sb("e1", [P, SE, GT * P]); e2 = sb("e2", [P, 2, GT * P]); e2g = sb("e2g", [P, 2, GT * P])
        gl = sb("gl", [P, GT, SE]); ga = sb("ga", [P, GT, SE]); o1 = sb("o1", [P, GT, SE]); o2 = sb("o2", [P, GT, SE])
        gv = sb("gv", [P, GT, SE])
        v1 = sb("v1", [P, GT]); v2 = sb("v2", [P, GT]); km = sb("km", [P, GT]); gd = sb("gd", [P, GT])
        gw1 = sb("gw1", [P, GT]); gw2 = sb("gw2", [P, GT])
        gate = sb("gate", [P, GT, SE + 1]); gateT = sb("gateT", [SE + 1, GT * P])
        ps = ctx.enter_context(nc.psum_tensor("e_ps", [P, 8, 512], F32))

        def tiles(bank):
            return ps[:, bank, :].rearrange("p (t f) -> p t f", f=P)

        z2T_ps, attT_ps, gateT_ps = tiles(0), tiles(0), ps[0:SE + 1, 0, :]
        zT_ps, sim_ps = tiles(1), ps[:, 1, 0:GT * N].rearrange("p (t n) -> p t n", n=N)
        h1_ps, h2_ps, out_ps = ps[:, 2, :], ps[:, 2, :], tiles(2)
        wT_ps, e1c_ps, e2b_ps = ps[:, 3, :], ps[:, 3, :], ps[:, 3, :]
        e1a_ps, e2a_ps = ps[:, 4, :], ps[:, 4, :]
        e1b_ps, wide0_ps = ps[:, 5, :], ps[:, 5, :]
        gl_ps, e1d_ps, wide1_ps = ps[:, 6, 0:GT * SE].rearrange("p (t e) -> p t e", e=SE), ps[:, 6, :], ps[:, 6, :]
        av_ps = tiles(7)
        e1_ps = [e1a_ps, e1b_ps, e1c_ps, e1d_ps]
        e2_ps, wide_ps = [e2a_ps, e2b_ps], [wide0_ps, wide1_ps]

        def sem(name):
            return ctx.enter_context(nc.semaphore("e_" + name))

        s = Memory()
        s.at_ok, s.picked1, s.picked, s.bn = sem("at_ok"), sem("picked1"), sem("picked"), sem("bn")
        s.stats, s.var_ok, s.rstd_ok, s.z_ok = sem("stats"), sem("var_ok"), sem("rstd_ok"), sem("z_ok")
        s.bn2, s.stats2, s.var2_ok, s.rstd2_ok = sem("bn2"), sem("stats2"), sem("var2_ok"), sem("rstd2_ok")
        s.z2_ok, s.zT_done, s.zT_ok, s.wT_done = sem("z2_ok"), sem("zT_done"), sem("zT_ok"), sem("wT_done")
        s.wT_ok, s.sim_done, s.sim1, s.sim2 = sem("wT_ok"), sem("sim_done"), sem("sim1"), sem("sim2")
        s.top_ok, s.sim_ok, s.att_ok, s.total_ok = sem("top_ok"), sem("sim_ok"), sem("att_ok"), sem("total_ok")
        s.inv_ok, s.attT_done, s.attT_ok, s.av_done = sem("inv_ok"), sem("attT_done"), sem("attT_ok"), sem("av_done")
        s.x1_ok, s.z2T_done, s.z2T_ok, s.gl_done = sem("x1_ok"), sem("z2T_done"), sem("z2T_ok"), sem("gl_done")
        s.gl_ok, s.gx_in, s.gx_ok, s.gd_in = sem("gl_ok"), sem("gx_in"), sem("gx_ok"), sem("gd_in")
        s.gd_ok, s.gate_ok, s.gateT_done, s.gateT_ok = sem("gd_ok"), sem("gate_ok"), sem("gateT_done"), sem("gateT_ok")
        s.h1_done, s.h1_ok, s.h2_done, s.h2_ok = sem("h1_done"), sem("h1_ok"), sem("h2_done"), sem("h2_ok")
        s.e1_done, s.e1_ok, s.e2_done, s.e2_ok = sem("e1_done"), sem("e1_ok"), sem("e2_done"), sem("e2_ok")
        s.wide_done, s.e2g_ok, s.out_done, s.x2_ok = sem("wide_done"), sem("e2g_ok"), sem("out_done"), sem("x2_ok")
        s.chain, s.cleared = sem("chain"), sem("cleared")
        got_in = [ctx.enter_context(nc.semaphore(f"e_got{k}")) for k in range(2)]
        STEPS = 20

        def run(eng, body):
            pipeline(eng, body, LAG, unroll=U, lead=U - 1)

        with nc.Block() as block:
            @block.sync
            def _(eng):
                out = c.dram["out"].rearrange("(t b) n f -> (b n) t f", b=2)

                def body(i, q):
                    g = i - 5
                    if live(g):
                        eng.wait_ge(s.x2_ok, g + 1)
                        eng.dma_start(out[:, tile4(g), :], c.x[:, tile4(g), :]).then_inc(c.stored, 16)
                run(eng, body)
                eng.wait_ge(c.stored, 16 * G)

            @block.gpsimd
            def _(eng):
                def rsqrt(g, k, bk, stats, var_ok, used, rstd_ok):
                    eng.wait_ge(stats, g + 1)
                    alone(eng, c.passed)
                    eng.tensor_scalar(var[:, k], mv[:, k, :, 1], 1.0, EPS, ALU.mult, ALU.add).then_inc(var_ok, 1)
                    eng.wait_ge(var_ok, g + 1)
                    need(eng, used, g)
                    eng.tensor_tensor(rstd[:, k], var[:, k], c.minus_half[:, 0:GT], ALU.pow).then_inc(rstd_ok, 1)

                def gather(k, b):
                    for t in range(GT):
                        eng.indirect_dma_start(
                            got[:, b, k, t, :], None, c.dram["picked"],
                            bass.IndirectOffsetOnAxis(ap=at[:, b, k, t:t + 1], axis=0)).then_inc(got_in[b], 16)

                def body(i, q):
                    b = q % 2
                    g = i - 1
                    if live(g):
                        rsqrt(g, 0, 1 - b, s.stats, s.var_ok, s.z_ok, s.rstd_ok)
                    g = i
                    if live(g):
                        eng.wait_ge(s.at_ok, g + 1)
                        need(eng, s.picked, g - 1)
                        alone(eng, c.passed)
                        gather(0, b)
                    g = i - 3
                    if live(g):
                        rsqrt(g, 1, 1 - b, s.stats2, s.var2_ok, s.z2_ok, s.rstd2_ok)
                    g = i
                    if live(g):
                        gather(1, b)
                run(eng, body)

            @block.vector
            def _(eng):
                eng.memset(att[:], 0.0).then_inc(s.cleared, 1)
                eng.memset(gate[:, :, SE:SE + 1], 1.0).then_inc(s.cleared, 1)

                def x_of(g, t):
                    return c.x[:, bass.ds(g * GT + t, 1), :].rearrange("p a f -> p (a f)")

                def gates(g):
                    base, count = g * STEPS, [0]

                    def step(instruction):
                        count[0] += 1
                        instruction.then_inc(s.chain, 1)
                        eng.wait_ge(s.chain, base + count[0])

                    def wide(a):
                        return a[:].unsqueeze(2).broadcast_to([P, GT, SE])

                    rev = c.tab[:, T_REV4:T_REV4 + SE].unsqueeze(1).broadcast_to([P, GT, SE])
                    eng.wait_ge(s.gl_done, g + 1)
                    eng.tensor_tensor(gl[:], gl_ps, c.gate_b[:].unsqueeze(1).broadcast_to([P, GT, SE]), ALU.add).then_inc(s.gl_ok, 1)
                    eng.wait_ge(s.gl_ok, g + 1)
                    step(eng.tensor_reduce(v1[:], gl[:], AX, ALU.max))
                    eng.tensor_tensor(gl[:], gl[:], wide(v1), ALU.subtract).then_inc(s.gx_in, 1)
                    eng.wait_ge(s.gx_ok, g + 1)
                    step(eng.tensor_reduce(v1[:], gl[:], AX, ALU.add))
                    step(eng.reciprocal(v2[:], v1[:]))
                    step(eng.tensor_tensor(gv[:], gl[:], wide(v2), ALU.mult))
                    step(eng.tensor_reduce(v1[:], gv[:], AX, ALU.max))
                    step(eng.tensor_tensor(ga[:], gv[:], wide(v1), ALU.is_equal))
                    step(eng.tensor_tensor(ga[:], ga[:], rev, ALU.mult))
                    step(eng.tensor_reduce(km[:], ga[:], AX, ALU.max))
                    step(eng.tensor_tensor(o1[:], ga[:], wide(km), ALU.is_equal))
                    step(eng.scalar_tensor_tensor(gv[:], o1[:], NEG, gv[:], ALU.mult, ALU.add))
                    step(eng.tensor_reduce(v2[:], gv[:], AX, ALU.max))
                    eng.tensor_tensor(gd[:], v2[:], v1[:], ALU.subtract).then_inc(s.gd_in, 1)
                    step(eng.tensor_tensor(ga[:], gv[:], wide(v2), ALU.is_equal))
                    step(eng.tensor_tensor(ga[:], ga[:], rev, ALU.mult))
                    step(eng.tensor_reduce(km[:], ga[:], AX, ALU.max))
                    step(eng.tensor_tensor(o2[:], ga[:], wide(km), ALU.is_equal))
                    eng.wait_ge(s.gd_ok, g + 1)
                    step(eng.tensor_scalar(v1[:], gd[:], 1.0, None, ALU.add))
                    step(eng.reciprocal(gw1[:], v1[:]))
                    step(eng.tensor_tensor(gw2[:], gd[:], gw1[:], ALU.mult))
                    step(eng.tensor_tensor(o1[:], o1[:], wide(gw1), ALU.mult))
                    step(eng.tensor_tensor(o2[:], o2[:], wide(gw2), ALU.mult))
                    need(eng, s.gateT_done, g)
                    eng.tensor_tensor(gate[:, :, 0:SE], o1[:], o2[:], ALU.add).then_inc(s.gate_ok, 1)
                    assert count[0] == STEPS

                def moments(g, k, bn, stats, rstd_ok):
                    alone(eng, c.passed)
                    for t in range(GT):
                        m = eng.bn_stats(st[:, k, t, :], x_of(g, t))
                    m.then_inc(bn, 1)
                    eng.wait_ge(bn, g + 1)
                    need(eng, rstd_ok, g)
                    alone(eng, c.passed)
                    for t in range(GT):
                        m = eng.bn_aggr(mv[:, k, t, :], st[:, k, t, :])
                    m.then_inc(stats, 1)

                def body(i, q):
                    b = q % 2
                    g = i - 5
                    if live(g):
                        eng.wait_ge(s.out_done, g + 1)
                        eng.tensor_tensor(c.x[:, tile4(g), :], out_ps, c.x[:, tile4(g), :], ALU.add).then_inc(s.x2_ok, 1)
                    g = i - 3
                    if live(g):
                        eng.wait_ge(s.sim_done, g + 1)
                        eng.tensor_tensor(sim[:], sim_ps, c.adj[:, tile4(g), :], ALU.mult).then_inc(s.sim1, 1)
                        eng.wait_ge(s.sim1, g + 1)
                        eng.tensor_tensor(sim[:], sim[:], c.masked[:, tile4(g), :], ALU.add).then_inc(s.sim2, 1)
                        eng.wait_ge(s.sim2, g + 1)
                        eng.tensor_reduce(top[:], sim[:], AX, ALU.max).then_inc(s.top_ok, 1)
                        eng.wait_ge(s.top_ok, g + 1)
                        eng.tensor_tensor(sim[:], sim[:], top[:].unsqueeze(2).broadcast_to([P, GT, N]), ALU.subtract)\
                           .then_inc(s.sim_ok, 1)
                    g = i - 4
                    if live(g):
                        gates(g)
                    g = i
                    if live(g):
                        need(eng, got_in[b], 64 * (g - b))
                        eng.tensor_copy(at[:, b], c.back[:, :, tile4(g)]).then_inc(s.at_ok, 1)
                    g = i - 1
                    if live(g):
                        eng.wait_ge(got_in[1 - b], 64 * (g - (1 - b)) + 128)
                        for k, done in enumerate((s.picked1, s.picked)):
                            for t in range(GT):
                                m = eng.scalar_tensor_tensor(
                                    x_of(g, t), got[:, 1 - b, k, t, :],
                                    c.weight[:, k, bass.ds(g * GT + t, 1)], x_of(g, t), ALU.mult, ALU.add)
                            m.then_inc(done, 1)
                            eng.wait_ge(done, g + 1)
                        moments(g, 0, s.bn, s.stats, s.rstd_ok)
                    g = i - 3
                    if live(g):
                        eng.wait_ge(s.att_ok, g + 1)
                        eng.tensor_reduce(total[:], att[:], AX, ALU.add).then_inc(s.total_ok, 1)
                        eng.wait_ge(s.total_ok, g + 1)
                        eng.reciprocal(inv[:], total[:]).then_inc(s.inv_ok, 1)
                    g = i - 1
                    if live(g):
                        eng.wait_ge(s.rstd_ok, g + 1)
                        need(eng, s.av_done, g - 3)
                        for t in range(GT):
                            m = eng.tensor_scalar(z[:, (q - 1) % U, t, :], x_of(g, t), mv[:, 0, t, 0:1], rstd[:, 0, t:t + 1],
                                                  ALU.subtract, ALU.mult)
                        m.then_inc(s.z_ok, 1)
                    g = i - 3
                    if live(g):
                        eng.wait_ge(s.av_done, g + 1)
                        eng.wait_ge(s.inv_ok, g + 1)
                        for t in range(GT):
                            m = eng.scalar_tensor_tensor(x_of(g, t), av_ps[:, t, :], inv[:, t:t + 1], x_of(g, t), ALU.mult, ALU.add)
                        m.then_inc(s.x1_ok, 1)
                        eng.wait_ge(s.x1_ok, g + 1)
                        moments(g, 1, s.bn2, s.stats2, s.rstd2_ok)
                    for k in range(2):
                        g = i - 4
                        if live(g):
                            eng.wait_ge(s.e2_ok, 2 * g + k + 1)
                            eng.wait_ge(s.wide_done, 2 * g + k + 1)
                            need(eng, s.out_done, g)
                            eng.tensor_tensor(e2g[:, k], e2[:, k], wide_ps[k], ALU.mult).then_inc(s.e2g_ok, 1)
                        g = i - 3
                        if live(g) and k == 0:
                            eng.wait_ge(s.rstd2_ok, g + 1)
                            need(eng, s.z2T_done, g - 1)
                            for t in range(GT):
                                m = eng.tensor_scalar(z2[:, 1 - b, t, :], x_of(g, t), mv[:, 1, t, 0:1], rstd[:, 1, t:t + 1],
                                                      ALU.subtract, ALU.mult)
                            m.then_inc(s.z2_ok, 1)
                run(eng, body)

            @block.scalar
            def _(eng):
                eng.preload_act_table_set("exp_and_others")
                eng.wait_ge(s.cleared, 2)

                def relu(out, in_, bias):
                    return eng.activation(out, in_, ACT.Relu, bias=bias)

                def body(i, q):
                    g = i - 4
                    if live(g):
                        eng.wait_ge(s.z2T_done, g + 1)
                        need(eng, s.e1_done, 4 * g)
                        eng.activation(z2T[:], z2T_ps.rearrange("p t f -> p (t f)"), ACT.Copy).then_inc(s.z2T_ok, 1)
                    g = i - 3
                    if live(g):
                        eng.wait_ge(s.sim_ok, g + 1)
                        need(eng, s.attT_done, g)
                        need(eng, s.total_ok, g)
                        for j in range(2):
                            r = slice(N * j, N * j + N)
                            m = eng.activation(att[r, :, r], sim[r], ACT.Exp)
                        m.then_inc(s.att_ok, 1)
                    g = i - 2
                    if live(g):
                        eng.wait_ge(s.zT_done, g + 1)
                        need(eng, s.sim_done, g)
                        eng.activation(zT[:], zT_ps, ACT.Copy).then_inc(s.zT_ok, 1)
                    g = i - 4
                    if live(g):
                        eng.wait_ge(s.gx_in, g + 1)
                        eng.activation(gl[:], gl[:], ACT.Exp).then_inc(s.gx_ok, 1)
                        eng.wait_ge(s.h1_done, g + 1)
                        need(eng, s.h2_done, g)
                        relu(h1[:], h1_ps, c.sb1).then_inc(s.h1_ok, 1)
                    g = i - 2
                    if live(g):
                        eng.wait_ge(s.wT_done, g + 1)
                        eng.activation(wT[:], wT_ps, ACT.Copy).then_inc(s.wT_ok, 1)
                    g = i - 4
                    if live(g):
                        eng.wait_ge(s.gd_in, g + 1)
                        eng.activation(gd[:], gd[:], ACT.Exp).then_inc(s.gd_ok, 1)
                        for e in range(2):
                            eng.wait_ge(s.e1_done, 4 * g + e + 1)
                            relu(e1[:, e], e1_ps[e], c.eb1[:, e:e + 1]).then_inc(s.e1_ok, 1)
                    g = i - 3
                    if live(g):
                        eng.wait_ge(s.attT_done, g + 1)
                        need(eng, s.av_done, g)
                        eng.activation(attT[:], attT_ps, ACT.Copy).then_inc(s.attT_ok, 1)
                    g = i - 4
                    if live(g):
                        eng.wait_ge(s.h2_done, g + 1)
                        need(eng, s.out_done, g)
                        relu(h2[:], h2_ps, c.sb2).then_inc(s.h2_ok, 1)
                        for e in range(2, 4):
                            eng.wait_ge(s.e1_done, 4 * g + e + 1)
                            relu(e1[:, e], e1_ps[e], c.eb1[:, e:e + 1]).then_inc(s.e1_ok, 1)
                        eng.wait_ge(s.e2_done, 2 * g + 1)
                        relu(e2[:, 0], e2_ps[0], c.eb2[:, 0:1]).then_inc(s.e2_ok, 1)
                        eng.wait_ge(s.gateT_done, g + 1)
                        eng.activation(gateT[:], gateT_ps, ACT.Copy).then_inc(s.gateT_ok, 1)
                        eng.wait_ge(s.e2_done, 2 * g + 2)
                        relu(e2[:, 1], e2_ps[1], c.eb2[:, 1:2]).then_inc(s.e2_ok, 1)
                run(eng, body)

            @block.tensor
            def _(eng):
                eng.wait_ge(s.cleared, 2)
                eng.wait_ge(c.late_in, c.late_count)

                def expert1(g, e):
                    eng.matmul(e1_ps[e], c.eW1[:, e, :], z2T[:], start=True, stop=True).then_inc(s.e1_done, 1)

                def expert2(g, k):
                    for j in range(2):
                        m = eng.matmul(e2_ps[k][64 * j:64 * j + 64], c.eW2[:, 2 * k + j, :], e1[:, 2 * k + j],
                                       start=True, stop=True)
                    m.then_inc(s.e2_done, 1)

                def body(i, q):
                    b = q % 2
                    g = i - 4
                    if live(g):
                        eng.wait_ge(s.z2_ok, g + 1)
                        need(eng, s.gateT_ok, g)
                        for t in range(GT):
                            m = eng.transpose(z2T_ps[:, t, :], z2[:, b, t, :], c.ident[:])
                        m.then_inc(s.z2T_done, 1)
                    g = i - 2
                    if live(g):
                        eng.wait_ge(s.z_ok, g + 1)
                        need(eng, s.sim1, g)
                        for t in range(GT):
                            m = eng.transpose(zT_ps[:, t, :], z[:, (q - 2) % U, t, :], c.ident[:])
                        m.then_inc(s.zT_done, 1)
                    g = i - 4
                    if live(g):
                        eng.wait_ge(s.z2T_ok, g + 1)
                        need(eng, s.e2g_ok, 2 * g)
                        for t in range(GT):
                            m = eng.matmul(gl_ps[:, t, :], z2T[:, t * P:t * P + P], c.gate_w[:], start=True, stop=True)
                        m.then_inc(s.gl_done, 1)
                        need(eng, s.x2_ok, g)
                        eng.matmul(h1_ps, c.sW1[:], z2T[:], start=True, stop=True).then_inc(s.h1_done, 1)
                    g = i - 2
                    if live(g):
                        eng.wait_ge(s.zT_ok, g + 1)
                        need(eng, s.e2_ok, 2 * (g - 2))
                        eng.matmul(wT_ps, c.gnn_w[:], zT[:].rearrange("p t f -> p (t f)"), start=True, stop=True).then_inc(s.wT_done, 1)
                    g = i - 4
                    if live(g):
                        need(eng, s.e2_ok, 2 * g)
                        expert1(g, 0)
                        need(eng, s.e2g_ok, 2 * g)
                        expert1(g, 1)
                    g = i - 3
                    if live(g):
                        eng.wait_ge(s.att_ok, g + 1)
                        need(eng, s.z2T_ok, g)
                        for t in range(GT):
                            m = eng.transpose(attT_ps[:, t, :], att[:, t, :], c.ident[:])
                        m.then_inc(s.attT_done, 1)
                    g = i - 2
                    if live(g):
                        eng.wait_ge(s.wT_ok, g + 1)
                        for t in range(GT):
                            for j in range(2):
                                m = eng.matmul(sim_ps[N * j:N * j + N, t, :], wT[:, t * P + N * j:t * P + N * j + N],
                                               zT[:, t, N * j:N * j + N], start=True, stop=True)
                        m.then_inc(s.sim_done, 1)
                    g = i - 4
                    if live(g):
                        eng.wait_ge(s.h1_ok, g + 1)
                        eng.matmul(h2_ps, c.sW2[:], h1[:], start=True, stop=True).then_inc(s.h2_done, 1)
                        if isinstance(i, int):
                            need(eng, s.wT_ok, min(g + 3, G))
                        else:
                            eng.wait_ge(s.wT_ok, g + 3)
                        expert1(g, 2)
                        eng.wait_ge(s.gl_ok, g + 1)
                        expert1(g, 3)
                    g = i - 3
                    if live(g):
                        eng.wait_ge(s.attT_ok, g + 1)
                        need(eng, s.x1_ok, g)
                        for t in range(GT):
                            m = eng.matmul(av_ps[:, t, :], attT[:, t, :], z[:, (q - 3) % U, t, :], start=True, stop=True)
                        m.then_inc(s.av_done, 1)
                    g = i - 4
                    if live(g):
                        eng.wait_ge(s.e1_ok, 4 * g + 2)
                        need(eng, s.e2g_ok, 2 * g)
                        expert2(g, 0)
                        eng.wait_ge(s.gate_ok, g + 1)
                        if isinstance(i, int):
                            need(eng, s.attT_ok, min(g + 2, G))
                        else:
                            eng.wait_ge(s.attT_ok, g + 2)
                        for t in range(GT):
                            m = eng.transpose(gateT_ps[:, t * P:t * P + P], gate[:, t, :], c.ident[:])
                        m.then_inc(s.gateT_done, 1)
                        eng.wait_ge(s.e1_ok, 4 * g + 4)
                        expert2(g, 1)
                        eng.wait_ge(s.gateT_ok, g + 1)
                        for k in range(2):
                            eng.matmul(wide_ps[k], c.tab[0:SE, T_PAIR + P * k:T_PAIR + P * k + P], gateT[0:SE, :],
                                       start=True, stop=True).then_inc(s.wide_done, 1)
                        eng.wait_ge(s.h2_ok, g + 1)
                        eng.wait_ge(s.e2g_ok, 2 * g + 2)
                        for t in range(GT):
                            cols = slice(t * P, t * P + P)
                            eng.matmul(out_ps[:, t, :], h2[:, cols], c.sW3[:], start=True, stop=False)
                            for k in range(2):
                                eng.matmul(out_ps[:, t, :], e2g[:, k, cols], c.eW3[:, k, :], start=False, stop=False)
                            m = eng.matmul(out_ps[:, t, :], gateT[:, cols], c.bias3[:], start=False, stop=True)
                        m.then_inc(s.out_done, 1)
                run(eng, body)


class Memory:
    pass


def build(nc, dram):
    with ExitStack() as ctx:
        c = Memory()

        def sb(name, shape, dt=F32):
            return ctx.enter_context(nc.sbuf_tensor(name, shape, dt))

        def sem(name):
            return ctx.enter_context(nc.semaphore(name))

        c.dram = dram
        c.x = sb("x", [P, T, D])
        c.adj = sb("adj", [P, T, N])
        c.tab = sb("tab", [P, T_ALL])
        c.ident = c.tab[:, T_ID:T_ID + P]
        c.ones = sb("ones", [P, P])
        c.ones16 = sb("ones16", [P, P], BF16)
        c.low16 = sb("low16", [P, P], BF16)
        c.minus_half = sb("minus_half", [P, 2 * GT])
        c.gamma_row = sb("gamma_row", [P, D])
        c.beta_row = sb("beta_row", [P, D])
        c.cols = sb("cols", [P, 14])
        names = ["L0_gnn_gamma", "L0_gnn_beta", "L0_ffn_ln1_w", "L0_ffn_ln2_w", "L1_ffn_sb1", "L1_ffn_sb2"]
        c.gamma, c.beta, c.ln1, c.ln2, c.sb1, c.sb2 = (c.cols[:, n:n + 1] for n in range(6))
        c.eb1, c.eb2 = c.cols[:, 6:10], c.cols[:, 10:12]
        c.w_self = sb("w_self", [D, D])
        c.w_neigh = sb("w_neigh", [D, D])
        c.wqk = sb("wqk", [D, H * HD + KV * HD])
        c.wv = sb("wv", [D, KV * HD])
        c.wo = sb("wo", [D, D])
        c.router = sb("router", [D, NE])
        c.adj_in, c.x_in, c.weights_in, c.ones_ok = sem("adj_in"), sem("x_in"), sem("weights_in"), sem("ones_ok")

        x_rows = dram["x"].rearrange("(t b) n f -> (b n) t f", b=2)
        loads = [(c.tab[:], dram["tab"]), (c.cols[:, 6:10], dram["L1_ffn_eb1T"]), (c.cols[:, 10:12], dram["L1_ffn_eb2T"])]
        loads += [(c.cols[:, n:n + 1], dram[name].rearrange("(p a) -> p a", a=1)) for n, name in enumerate(names)]
        loads += [(c.gamma_row[:], dram["L0_gnn_gamma"].partition_broadcast(P)),
                  (c.beta_row[:], dram["L0_gnn_beta"].partition_broadcast(P)),
                  (c.w_self[:], dram["L0_gnn_W_self"]), (c.w_neigh[:], dram["L0_gnn_W_neigh"]),
                  (c.wqk[:, 0:128], dram["L0_ffn_wqT"]), (c.wqk[:, 128:192], dram["L0_ffn_wkT"]),
                  (c.wv[:], dram["L0_ffn_wvT"]), (c.wo[:], dram["L0_ffn_woT"]), (c.router[:], dram["L0_ffn_router_wT"])]
        c.weights_count = 16 * len(loads)
        c.masked = sb("masked", [P, T, N])
        c.gnn_w = sb("gnn_w", [D, D])
        c.sW1, c.sW2, c.sW3 = (sb(f"sW{n}", [D, D]) for n in (1, 2, 3))
        c.eW1 = sb("eW1", [D, SE, P])
        c.eW2 = sb("eW2", [P, SE, 64])
        c.eW3 = sb("eW3", [P, SE // 2, D])
        c.gate_w = sb("gate_w", [D, SE])
        c.gate_b = sb("gate_b", [P, SE])
        c.bias3 = sb("bias3", [SE + 1, D])
        c.late_loads = [(c.gnn_w[:], dram["L1_gnn_W"]), (c.sW1[:], dram["L1_ffn_sW1"]), (c.sW2[:], dram["L1_ffn_sW2"]),
                        (c.sW3[:], dram["L1_ffn_sW3"]), (c.eW1[:], dram["eW1"]), (c.eW2[:], dram["eW2"]), (c.eW3[:], dram["eW3"]),
                        (c.gate_w[:], dram["L1_ffn_gW"]), (c.gate_b[:], dram["L1_ffn_gb"].partition_broadcast(P)),
                        (c.bias3[0:SE], dram["L1_ffn_eb3"]), (c.bias3[SE:SE + 1], dram["L1_ffn_sb3"].rearrange("(a f) -> a f", a=1))]
        c.late_in = sem("late_in")
        c.late_count = 16 * len(c.late_loads)
        c.stored, c.passed = sem("stored"), sem("passed")

        with nc.Block() as block:
            @block.sync
            def _(sp):
                sp.dma_start(c.adj[:], dram["adj"].rearrange("(t b) n m -> (b n) t m", b=2)).then_inc(c.adj_in, 16)
                for to, of in loads:
                    sp.dma_start(to, of).then_inc(c.weights_in, 16)
                sp.dma_start(c.x[:], x_rows).then_inc(c.x_in, 16)

            @block.gpsimd
            def _(pool):
                pool.memset(c.minus_half[:], -0.5).then_inc(c.ones_ok, 1)

            @block.vector
            def _(dve):
                dve.memset(c.ones16[:], 1.0).then_inc(c.ones_ok, 1)
                dve.memset(c.ones[:], 1.0).then_inc(c.ones_ok, 1)

        graph_conv(nc, c)
        moe_phases(nc, c, sb, sem)
        last_round(nc, c)


def kernel(**inputs):
    import concourse.bacc as _bacc
    from concourse.bass_utils import run_bass_kernel_spmd as _run

    nc = _bacc.Bacc("TRN2", target_bir_lowering=False, num_devices=1)
    w = {k: np.ascontiguousarray(v) for k, v in inputs.items()}
    layout = {k: w[k] for k in ("x", "adj", "nodemask", "L0_gnn_gamma", "L0_gnn_beta", "L0_gnn_W_self", "L0_gnn_W_neigh",
                                "L0_ffn_ln1_w", "L0_ffn_ln2_w", "L1_gnn_W", "L1_ffn_sW1", "L1_ffn_sW2", "L1_ffn_sW3",
                                "L1_ffn_sb1", "L1_ffn_sb2", "L1_ffn_sb3", "L1_ffn_eb3", "L1_ffn_gW", "L1_ffn_gb")}
    for k in ("L0_ffn_wq", "L0_ffn_wk", "L0_ffn_wv", "L0_ffn_wo", "L0_ffn_router_w", "L1_ffn_eb1"):
        layout[k + "T"] = w[k].T
    layout["L1_ffn_eb2T"] = w["L1_ffn_eb2"].reshape(SE // 2, P).T
    layout["w13"] = np.stack([w["L0_ffn_w1"], w["L0_ffn_w3"]], 1).transpose(3, 0, 1, 2)
    layout["w2"] = w["L0_ffn_w2"].transpose(2, 0, 1)
    layout["eW1"] = w["L1_ffn_eW1"].transpose(1, 0, 2)
    layout["eW2"] = w["L1_ffn_eW2"].transpose(1, 0, 2)
    layout["eW3"] = w["L1_ffn_eW3"].reshape(SE // 2, P, D).transpose(1, 0, 2)
    layout["tab"] = tables()
    arrays = {f"in_{k}": np.ascontiguousarray(v) for k, v in layout.items()}
    dram = {}
    for k in layout:
        a = arrays[f"in_{k}"]
        dram[k] = nc.dram_tensor(f"in_{k}", a.shape, mybir.dt.from_np(a.dtype), kind="ExternalInput").ap()
    dram["rows"] = nc.dram_tensor("rows", (NE * REGION, D), F32).ap()
    dram["picked"] = nc.dram_tensor("picked", (SLOTS * P, D), F32).ap()
    dram["out"] = nc.dram_tensor("out_0", (B, N, D), F32, kind="ExternalOutput").ap()
    build(nc, dram)
    r = _run(nc, [arrays], core_ids=[0])
    return r.results[0]["out_0"]
```

```python
from contextlib import ExitStack

import numpy as np

import concourse.bass as bass
from concourse import mybir

F32 = mybir.dt.float32
I32 = mybir.dt.int32
BF16 = mybir.dt.bfloat16
ALU = mybir.AluOpType
ACT = mybir.ActivationFunctionType
AX = mybir.AxisListType.X

P = 128
D = 128
N = 64
B = 128
T = B * N // P
GT = 4
G = T // GT
H, HD = 4, 32
KV = 2
NE, HID = 8, 341
HC = 3
SE = 4
EPS = 1e-5
EPS_RMS = 1e-6
NEG = -1e30
REGION = B * N + P
SLOTS = 2 * B * N // P + NE

T_ID, T_LOW, T_COS, T_SIN, T_CAUSAL, T_REV, T_REGION, T_TILE, T_SLOT, T_PAIR, T_REV4 = (
    0, 128, 256, 288, 320, 384, 392, 400, 464, 464 + SLOTS, 464 + SLOTS + 256)
T_ALL = T_REV4 + SE


def tables():
    t = np.zeros((P, T_ALL), np.float32)
    r = np.arange(P)
    t[:, T_ID:T_ID + P] = np.eye(P)
    t[:, T_LOW:T_LOW + P] = r[:, None] < r[None, :]
    f = np.outer(np.arange(N, dtype=np.float32), 1.0 / 10000.0 ** (np.arange(0, HD, 2, dtype=np.float32) / HD))
    cos, sin = np.cos(f), np.sin(f)
    t[:, T_COS:T_COS + HD] = np.tile(np.concatenate([cos, cos], 1), (2, 1))
    t[:, T_SIN:T_SIN + HD] = np.tile(np.concatenate([-sin, sin], 1), (2, 1))
    n = np.arange(N)
    t[:, T_CAUSAL:T_CAUSAL + N] = np.tile(np.where(n[None, :] <= n[:, None], 0.0, NEG), (2, 1))
    t[:, T_REV:T_REV + NE] = NE - np.arange(NE)
    t[:, T_REGION:T_REGION + NE] = REGION * np.arange(NE)
    t[:, T_TILE:T_TILE + 64] = P * np.arange(64)
    t[:, T_SLOT:T_SLOT + SLOTS] = np.arange(SLOTS)
    for row in range(3 * (SE + 1)):
        e = row % (SE + 1)
        if e < SE:
            t[row, T_PAIR + e // 2 * P + e % 2 * 64:T_PAIR + e // 2 * P + e % 2 * 64 + 64] = 1.0
    t[:, T_REV4:T_REV4 + SE] = SE - np.arange(SE)
    return t


def need(eng, semaphore, count):
    if not isinstance(count, int) or count > 0:
        eng.wait_ge(semaphore, count)


def alone(eng, passed):
    eng.sem_inc(passed, 1)


def live(g, groups=G):
    return not isinstance(g, int) or 0 <= g < groups


def pipeline(eng, body, lag, groups=G, unroll=2, lead=2, prepare=None):
    first = lag + lead + (groups - lag - lead) % unroll
    for i in range(first):
        if prepare and i % unroll == 0:
            prepare(i, unroll)
        body(i, i % unroll)
    with eng.Fori(first, groups - unroll + 1, unroll) as i:
        if prepare:
            prepare(i, unroll)
        for k in range(unroll):
            body(eng.snap(i + k) if k else i, (first + k) % unroll)
    for i in range(groups, groups + lag):
        if prepare and (i - groups) % unroll == 0:
            prepare(i, unroll)
        body(i, i % unroll)


def tile4(g):
    return bass.ds(g * GT, GT)


class Signals:

    def __init__(self, nc, prefix):
        self.nc, self.prefix, self.held = nc, prefix, []

    def new(self, name):
        self.held.append(self.nc.alloc_semaphore(f"{self.prefix}_{name}"))
        return self.held[-1]

    def give_back(self):
        self.nc.clear_and_free_semaphores(self.held)
        self.nc.all_engine_barrier()


def graph_conv(nc, c):
    with ExitStack() as ctx:
        def sb(name, shape, dt=F32):
            return ctx.enter_context(nc.sbuf_tensor("a_" + name, shape, dt))

        def bank(name, shape=(P, GT, D)):
            return ctx.enter_context(nc.psum_tensor("a_" + name, list(shape), F32))

        signals = Signals(nc, "a")
        sem = signals.new

        st = sb("st", [P, 2, GT, 6])
        mv = sb("mv", [P, 2, GT, 2])
        var = sb("var", [P, 2, GT])
        rstd = sb("rstd", [P, 2, GT])
        z = sb("z", [P, 2, GT, D])
        xn = sb("xn", [P, 2, GT, D])
        xnT = sb("xnT", [P, 2, GT, D])
        adj_s = sb("adj_s", [P, 2, GT, P])
        lapT = sb("lapT", [P, 2, GT, P])
        nbT = sb("nbT", [P, 2, GT, P])
        ab = sb("ab", [P, 2, GT, D])
        lg = sb("lg", [P, 2, GT, D])
        deg = sb("deg", [P, 2, T])
        nz = sb("nz", [P, 2, T])
        lnd = sb("lnd", [P, 2, T])
        s0 = sb("s0", [P, 2, T])
        sq = sb("sq", [P, 2, T])
        sc = sb("sc", [P, 2, T])
        zT_ps = bank("zT_ps")
        adjT_ps = bank("adjT_ps")
        nb_ps = bank("nb_ps")
        pre_ps = [bank("pre_ps0"), bank("pre_ps1")]
        deg_ps = bank("deg_ps", (P, 2, T))

        colsum = sem("colsum"); degs = sem("degs"); lns = sem("lns"); scales = sem("scales")
        zeroed = sem("zeroed"); dchain = sem("dchain")
        bn = sem("bn"); stats = sem("stats"); pvar = sem("pvar"); rstd_ok = sem("rstd_ok")
        z_ok = sem("z_ok"); zT_ok = sem("zT_ok"); xnT_ok = sem("xnT_ok"); xg_ok = sem("xg_ok"); xn_ok = sem("xn_ok")
        adj_ok = sem("adj_ok"); adj_half = sem("adj_half"); adjT_ok = sem("adjT_ok"); lapT_ok = sem("lapT_ok")
        nb_ok = sem("nb_ok"); nbT_ok = sem("nbT_ok"); pre_ok = sem("pre_ok")
        ab_ok = sem("ab_ok"); ex_ok = sem("ex_ok"); lg_ok = sem("lg_ok"); sp_ok = sem("sp_ok"); x_ok = sem("x_ok")
        LAG = 3

        with nc.Block() as block:
            @block.vector
            def _(eng):
                eng.wait_ge(c.adj_in, 16)
                eng.tensor_reduce(deg[:, 0, :], c.adj[:], AX, ALU.add).then_inc(dchain, 1)
                eng.wait_ge(colsum, 1)
                for j in range(2):
                    eng.tensor_copy(deg[N * j:N * j + N, 1, :], deg_ps[0:N, j, :]).then_inc(dchain, 1)
                eng.wait_ge(dchain, 3)
                eng.tensor_scalar(nz[:], deg[:], 0.0, None, ALU.not_equal).then_inc(dchain, 1)
                eng.tensor_scalar(sq[:], deg[:], 0.0, None, ALU.is_equal).then_inc(dchain, 1)
                eng.wait_ge(dchain, 5)
                eng.tensor_tensor(deg[:], deg[:], sq[:], ALU.add).then_inc(degs, 1)
                eng.wait_ge(lns, 2)
                eng.tensor_tensor(sq[:], s0[:], s0[:], ALU.mult).then_inc(dchain, 1)
                eng.wait_ge(dchain, 6)
                eng.tensor_tensor(sq[:], sq[:], deg[:], ALU.mult).then_inc(dchain, 1)
                eng.wait_ge(dchain, 7)
                eng.tensor_scalar(sq[:], sq[:], -0.5, 1.5, ALU.mult, ALU.add).then_inc(dchain, 1)
                eng.wait_ge(dchain, 8)
                eng.tensor_tensor(sq[:], sq[:], s0[:], ALU.mult).then_inc(dchain, 1)
                eng.wait_ge(dchain, 9)
                eng.tensor_tensor(sc[:], sq[:], nz[:], ALU.mult).then_inc(dchain, 1)
                eng.wait_ge(dchain, 10)
                eng.tensor_scalar(sc[:, 1, :], sc[:, 1, :], -1.0, None, ALU.mult).then_inc(scales, 1)
                eng.wait_ge(scales, 1)
                eng.wait_ge(c.x_in, 16)

                def body(i, p):
                    g, b = i, p
                    if live(g):
                        for t in range(GT):
                            m = eng.bn_stats(st[:, b, t, :], c.x[:, bass.ds(g * GT + t, 1), :].rearrange("p a f -> p (a f)"))
                        m.then_inc(bn, 1)
                    g, b = i, p
                    if live(g):
                        eng.wait_ge(bn, g + 1)
                        need(eng, rstd_ok, g - 1)
                        need(eng, z_ok, g - 1)
                        alone(eng, c.passed)
                        for t in range(GT):
                            m = eng.bn_aggr(mv[:, b, t, :], st[:, b, t, :])
                        m.then_inc(stats, 1)
                    g, b = i - 2, p
                    if live(g):
                        eng.wait_ge(nb_ok, g + 1)
                        eng.wait_ge(xnT_ok, g + 1)
                        need(eng, pre_ok, g - 1)
                        eng.tensor_tensor(nbT[:, b], nb_ps[:], xnT[:, b], ALU.add).then_inc(nbT_ok, 1)
                    g, b = i - 1, (p + 1) % 2
                    if live(g):
                        eng.wait_ge(adjT_ok, g + 1)
                        need(eng, nb_ok, g - 1)
                        eng.tensor_tensor(lapT[:, b], adjT_ps[:], sc[:, 0, tile4(g)].unsqueeze(2).broadcast_to([P, GT, P]),
                                          ALU.mult).then_inc(lapT_ok, 1)
                    g, b = i, p
                    if live(g):
                        need(eng, adjT_ok, g - 1)
                        eng.wait_ge(zeroed, 1)
                        eng.tensor_tensor(adj_s[N:P, b, :, N:P], c.adj[N:P, tile4(g), :],
                                          sc[N:P, 1, tile4(g)].unsqueeze(2).broadcast_to([N, GT, N]), ALU.mult).then_inc(adj_half, 1)
                    g, b = i - 3, (p + 1) % 2
                    if live(g):
                        eng.wait_ge(lg_ok, g + 1)
                        eng.scalar_tensor_tensor(lg[:, b], pre_ps[b][:], 0.0, lg[:, b], ALU.max, ALU.add).then_inc(sp_ok, 1)
                    g, b = i - 3, (p + 1) % 2
                    if live(g):
                        eng.wait_ge(sp_ok, g + 1)
                        eng.tensor_tensor(c.x[:, tile4(g), :], c.x[:, tile4(g), :], lg[:, b], ALU.add).then_inc(x_ok, 1)
                    g, b = i, p
                    if live(g):
                        eng.wait_ge(rstd_ok, g + 1)
                        need(eng, xg_ok, g - 1)
                        need(eng, zT_ok, g - 1)
                        for t in range(GT):
                            m = eng.tensor_scalar(z[:, b, t, :], c.x[:, bass.ds(g * GT + t, 1), :].rearrange("p a f -> p (a f)"),
                                                  mv[:, b, t, 0:1], rstd[:, b, t:t + 1], ALU.subtract, ALU.mult)
                        m.then_inc(z_ok, 1)
                    if isinstance(i, int) and i == c.first_groups - 1:
                        eng.wait_ge(c.x_rest_in, 16)
                pipeline(eng, body, LAG)

            @block.gpsimd
            def _(eng):
                eng.memset(adj_s[:], 0.0).then_inc(zeroed, 1)
                eng.wait_ge(zeroed, 1)
                eng.wait_ge(scales, 1)
                eng.wait_ge(c.weights_in, c.weights_count)

                def body(i, p):
                    g, b = i, p
                    if live(g):
                        eng.wait_ge(stats, g + 1)
                        alone(eng, c.passed)
                        eng.tensor_scalar(var[:, b], mv[:, b, :, 1], 1.0 + EPS, EPS * EPS, ALU.mult, ALU.add).then_inc(pvar, 1)
                        eng.wait_ge(pvar, g + 1)
                        eng.tensor_tensor(rstd[:, b], var[:, b], c.minus_half[:, 0:GT], ALU.pow).then_inc(rstd_ok, 1)
                    g, b = i - 1, (p + 1) % 2
                    if live(g):
                        eng.wait_ge(z_ok, g + 1)
                        need(eng, nb_ok, g - 1)
                        eng.tensor_tensor(xn[:, b], z[:, b], c.gamma_row[:].unsqueeze(1).broadcast_to([P, GT, D]),
                                          ALU.mult).then_inc(xg_ok, 1)
                    g, b = i, p
                    if live(g):
                        need(eng, adjT_ok, g - 1)
                        eng.tensor_tensor(adj_s[0:N, b, :, 0:N], c.adj[0:N, tile4(g), :],
                                          sc[0:N, 1, tile4(g)].unsqueeze(2).broadcast_to([N, GT, N]), ALU.mult).then_inc(adj_ok, 1)
                    g, b = i - 1, (p + 1) % 2
                    if live(g):
                        eng.wait_ge(xg_ok, g + 1)
                        eng.tensor_tensor(xn[:, b], xn[:, b], c.beta_row[:].unsqueeze(1).broadcast_to([P, GT, D]),
                                          ALU.add).then_inc(xn_ok, 1)
                pipeline(eng, body, LAG)

            @block.scalar
            def _(eng):
                eng.preload_act_table_set("natural_log_exp_and_others")
                eng.wait_ge(degs, 1)
                eng.activation(lnd[:], deg[:], ACT.Ln).then_inc(lns, 1)
                eng.wait_ge(lns, 1)
                eng.activation(s0[:], lnd[:], ACT.Exp, scale=-0.5).then_inc(lns, 1)
                eng.wait_ge(c.weights_in, c.weights_count)

                def body(i, p):
                    g, b = i - 1, (p + 1) % 2
                    if live(g):
                        eng.wait_ge(zT_ok, g + 1)
                        need(eng, pre_ok, g - 1)
                        eng.activation(xnT[:, b], zT_ps[:], ACT.Identity, bias=c.beta[:, 0:1], scale=c.gamma[:, 0:1])\
                           .then_inc(xnT_ok, 1)
                    g, b = i - 2, p
                    if live(g):
                        eng.wait_ge(pre_ok, g + 1)
                        eng.activation(ab[:, b], pre_ps[b][:], ACT.Abs).then_inc(ab_ok, 1)
                        eng.wait_ge(ab_ok, g + 1)
                        eng.activation(ab[:, b], ab[:, b], ACT.Exp, scale=-1.0).then_inc(ex_ok, 1)
                        eng.wait_ge(ex_ok, g + 1)
                        need(eng, x_ok, g - 1)
                        eng.activation(lg[:, b], ab[:, b], ACT.Ln, bias=1.0).then_inc(lg_ok, 1)
                pipeline(eng, body, LAG)

            @block.tensor
            def _(eng):
                eng.wait_ge(c.ones_ok, 5)
                eng.wait_ge(c.adj_in, 16)
                for t in range(T):
                    m = eng.matmul(deg_ps[0:N, :, t], c.adj[:, t, :], c.which[:], start=True, stop=True)
                m.then_inc(colsum, 1)
                eng.wait_ge(c.weights_in, c.weights_count)

                def body(i, p):
                    g, b = i - 2, p
                    if live(g):
                        eng.wait_ge(xn_ok, g + 1)
                        eng.wait_ge(lapT_ok, g + 1)
                        need(eng, nbT_ok, g)
                        for t in range(GT):
                            m = eng.matmul(nb_ps[:, t, :], xn[:, b, t, :], lapT[:, b, t, :], start=True, stop=True)
                        m.then_inc(nb_ok, 1)
                    g, b = i - 1, (p + 1) % 2
                    if live(g):
                        eng.wait_ge(adj_half, g + 1)
                        eng.wait_ge(adj_ok, g + 1)
                        need(eng, lapT_ok, g)
                        for t in range(GT):
                            m = eng.transpose(adjT_ps[:, t, :], adj_s[:, b, t, :], c.ident[:])
                        m.then_inc(adjT_ok, 1)
                        eng.wait_ge(z_ok, g + 1)
                        need(eng, xnT_ok, g)
                        for t in range(GT):
                            m = eng.transpose(zT_ps[:, t, :], z[:, b, t, :], c.ident[:])
                        m.then_inc(zT_ok, 1)
                    g, b = i - 2, p
                    if live(g):
                        eng.wait_ge(nbT_ok, g + 1)
                        need(eng, sp_ok, g - 1)
                        for t in range(GT):
                            eng.matmul(pre_ps[b][:, t, :], xnT[:, b, t, :], c.w_self[:], start=True, stop=False)
                            m = eng.matmul(pre_ps[b][:, t, :], nbT[:, b, t, :], c.w_neigh[:], start=False, stop=True)
                        m.then_inc(pre_ok, 1)
                pipeline(eng, body, LAG)
        signals.give_back()


def plan(c, sb, sem, ps, wide, more, past, part):
    def tmp(name, shape, dt=F32):
        return sb("plan_" + name, shape, dt)

    count = tmp("count", [P, NE]); tiles = tmp("tiles", [P, NE])
    start = tmp("start", [P, NE + 1]); shift = tmp("shift", [P, NE])
    moved = tmp("moved", [P, 2, T])
    which = tmp("which", [P, SLOTS]); begun = tmp("begun", [P, SLOTS]); row = tmp("row", [P, SLOTS])
    pad = tmp("pad", [P, NE]); pad_at = tmp("pad_at", [P, NE], I32)
    zeros = tmp("zeros", [P, D])
    counted, chain, pads_ok = sem("counted"), sem("plan_chain"), sem("pads_ok")
    zero_ok, padded = sem("zero_ok"), sem("padded")

    def count_rows(eng):
        eng.matmul(ps, c.ones16[:], c.cum16[:], start=True, stop=True).then_inc(counted, 1)

    def work_out(eng):
        n = [0]

        def step(instruction):
            n[0] += 1
            instruction.then_inc(chain, 1)
            eng.wait_ge(chain, n[0])

        regions = c.tab[:, T_REGION:T_REGION + NE]
        eng.wait_ge(counted, 1)
        step(eng.tensor_copy(count[:], ps))
        eng.memset(zeros[:], 0.0).then_inc(zero_ok, 1)
        step(eng.tensor_tensor(pad[:], count[:], regions, ALU.add))
        eng.tensor_copy(pad_at[:], pad[:]).then_inc(pads_ok, 1)
        step(eng.tensor_tensor(more, count[:].unsqueeze(2).broadcast_to([P, NE, N]),
                               c.tab[:, T_TILE:T_TILE + N].unsqueeze(1).broadcast_to([P, NE, N]), ALU.is_gt))
        step(eng.tensor_reduce(tiles[:], more, AX, ALU.add))
        step(eng.memset(start[:, 0:1], 0.0))
        for e in range(NE):
            step(eng.tensor_tensor(start[:, e + 1:e + 2], start[:, e:e + 1], tiles[:, e:e + 1], ALU.add))
        step(eng.scalar_tensor_tensor(shift[:], start[:, 0:NE], float(P), regions, ALU.mult, ALU.subtract))
        for k, o in enumerate((c.o1, c.o2)):
            step(eng.tensor_tensor(wide, o[:], shift[:].unsqueeze(1).broadcast_to([P, T, NE]), ALU.mult))
            step(eng.tensor_reduce(moved[:, k], wide, AX, ALU.add))
        step(eng.tensor_tensor(moved[:], moved[:], c.place[:], ALU.add))
        step(eng.tensor_copy(c.back[:], moved[:]))
        slots = c.tab[:, T_SLOT:T_SLOT + SLOTS]
        step(eng.tensor_tensor(past, slots.unsqueeze(2).broadcast_to([P, SLOTS, NE]),
                               start[:, 1:NE + 1].unsqueeze(1).broadcast_to([P, SLOTS, NE]), ALU.is_ge))
        step(eng.tensor_reduce(which[:], past, AX, ALU.add))
        step(eng.tensor_tensor(part, past, tiles[:].unsqueeze(1).broadcast_to([P, SLOTS, NE]), ALU.mult))
        step(eng.tensor_reduce(begun[:], part, AX, ALU.add))
        step(eng.tensor_tensor(row[:], slots, begun[:], ALU.subtract))
        step(eng.tensor_scalar(row[:], row[:], float(P), None, ALU.mult))
        step(eng.scalar_tensor_tensor(row[:], which[:], float(REGION), row[:], ALU.mult, ALU.add))
        step(eng.tensor_scalar(begun[:], slots, start[:, NE:NE + 1], None, ALU.is_lt))
        step(eng.tensor_tensor(row[:], row[:], begun[:], ALU.mult))
        step(eng.tensor_copy(c.source[:], row[:]))
        step(eng.tensor_scalar(which[:], which[:], float(NE - 1), None, ALU.min))
        step(eng.tensor_copy(c.expert[:], which[:]))

    def pad_regions(eng):
        eng.wait_ge(zero_ok, 1)
        eng.wait_ge(pads_ok, 1)
        first = [eng.alloc_register(f"pad{e}") for e in range(NE)]
        eng.load(first, pad_at[0:1, :])
        for e in range(NE):
            row = eng.snap(first[e]).with_bounds(min_val=0, max_val=NE * REGION - P)
            eng.dma_start(c.dram["rows"][bass.ds(row, P), :], zeros[:]).then_inc(padded, 16)
        eng.wait_ge(padded, 16 * NE)

    return count_rows, work_out, pad_regions


def attention(nc, c):
    LAG, U = 5, 4
    TB = 2 * GT
    with ExitStack() as ctx:
        def sb(name, shape, dt=F32):
            return ctx.enter_context(nc.sbuf_tensor("b_" + name, shape, dt))

        signals = Signals(nc, "b")
        sem = signals.new

        st = sb("st", [P, 2, GT, 6])
        mv = sb("mv", [P, 2, GT, 2])
        var = sb("var", [P, 2, 2 * GT])
        rr = sb("rr", [P, 2, 2 * GT])
        minus = sb("minus", [P, 2, GT])
        shift = sb("shift", [P, 2, GT])
        h = sb("h", [P, 2, GT, D])
        f = sb("f", [P, U, GT, D])
        hT = sb("hT", [P, 2, GT, P])
        qk = sb("qk", [P, 2, GT, 2 * H, HD])
        turn = sb("turn", [P, GT * 6, HD])
        half = sb("half", [P, GT * 6, HD])
        qT = sb("qT", [P, 2, GT * P])
        kT = sb("kT", [P, 2, GT * P])
        vx = sb("vx", [P, 2, 2 * GT, KV, 2, HD + 1])
        s_sb = sb("s_sb", [P, 2, GT, H, N])
        mx = sb("mx", [P, GT, H])
        pT = sb("pT", [P, 2, GT, KV, P])
        rcp = sb("rcp", [P, 2, 2 * H])
        y = sb("y", [P, 2, GT, D])
        yT = sb("yT", [P, 2, GT, P])
        junk = sb("junk", [P, GT, D])
        ssq = sb("ssq", [P, 2, GT])
        var3 = sb("var3", [P, 2, GT])
        r3 = sb("r3", [P, 2, GT])
        flat = sb("flat", [P, 2, TB, D])
        fT = sb("fT", [P, 2, GT, P])
        lg = sb("lg", [P, TB, NE])
        m1 = sb("m1", [P, TB]); m2 = sb("m2", [P, TB]); km = sb("km", [P, TB])
        ra = sb("ra", [P, TB, NE]); rb = sb("rb", [P, TB, NE])
        ex = sb("ex", [P, TB, NE + 1])
        rank = sb("rank", [P, TB, NE])
        m16 = sb("m16", [P, TB, NE], BF16)
        zsum = sb("zsum", [P, TB]); wa = sb("wa", [P, TB]); wb = sb("wb", [P, TB])
        slot = sb("slot", [P, 2, 2, TB], I32)
        ps = ctx.enter_context(nc.psum_tensor("b_ps", [P, 8, 512], F32))

        s_ps = ps[:, 0:4, 0:GT * N].rearrange("p h (t n) -> p h t n", n=N)
        v_ps = ps[:, 0, :].rearrange("p (t j e) -> p t j e", t=GT, j=2)
        qT_ps, kT_ps = ps[:, 1, :], ps[:, 2, :]
        fT_ps = ps[:, 3, :].rearrange("p (t f) -> p t f", f=P)
        hT_ps = ps[:, 4, :].rearrange("p (t f) -> p t f", f=P)
        qk_ps = ps[:, 4:6, 0:384].rearrange("p k (a d) -> p k a d", d=HD)
        lg_ps = ps[:, 5, 0:GT * NE].rearrange("p (t e) -> p t e", e=NE)
        rank_ps = ps[:, 5, 384:384 + TB * NE].rearrange("p (t e) -> p t e", e=NE)
        pT_ps = ps[:, 6:8, :].rearrange("p k (t g q) -> p (k t) g q", t=2, g=KV)
        y_ps = ps[:, 6:8, 0:4 * KV * (HD + 1) * 1 * 1].rearrange("p k (a e) -> p k a e", e=HD + 1)
        yT_ps = ps[:, 6, :].rearrange("p (t f) -> p t f", f=P)
        at_ps = ps[:, 7, :].rearrange("p (t f) -> p t f", f=P)

        s = Memory()
        s.rank_got = sem("rank_got")
        s.f_ok, s.shift_ok = sem("f_ok"), sem("shift_ok")
        s.bn, s.stats, s.masked, s.top = sem("bn"), sem("stats"), sem("masked"), sem("top")
        s.centred, s.turned1, s.turned, s.recip = sem("centred"), sem("turned1"), sem("turned"), sem("recip")
        s.y_ok, s.h_ok, s.x1_ok, s.x_ok = sem("y_ok"), sem("h_ok"), sem("x1_ok"), sem("x_ok")
        s.flat_ok, s.lg_ok, s.var_ok, s.rr_ok = sem("flat_ok"), sem("lg_ok"), sem("var_ok"), sem("rr_ok")
        s.var3_ok, s.r3_ok, s.hT_done, s.qk_done = sem("var3_ok"), sem("r3_ok"), sem("hT_done"), sem("qk_done")
        s.v_done, s.qkT_done, s.s_done, s.pT_done = sem("v_done"), sem("qkT_done"), sem("s_done"), sem("pT_done")
        s.y_done, s.yT_done, s.at_done, s.fT_done = sem("y_done"), sem("yT_done"), sem("at_done"), sem("fT_done")
        s.lg_done, s.hT_ok, s.v_ok, s.qkT_ok = sem("lg_done"), sem("hT_ok"), sem("v_ok"), sem("qkT_ok")
        s.e_ok, s.pT_ok, s.yT_ok, s.ssq_ok = sem("e_ok"), sem("pT_ok"), sem("yT_ok"), sem("ssq_ok")
        s.fT_ok, s.rank_in, s.ex_in, s.ex_ok = sem("fT_ok"), sem("rank_in"), sem("ex_in"), sem("ex_ok")
        s.rank_done, s.slot_ok, s.chain, s.filled = sem("rank_done"), sem("slot_ok"), sem("chain"), sem("filled")
        scattered = [sem(f"scattered{k}") for k in range(U)]
        STEPS, FIRST_STEPS = 25, 12

        def as_table(buffer, pattern, a, b):
            return buffer.rearrange(pattern)[:, 0:a * b].rearrange("p (a b) -> p a b", b=b)

        count_rows, work_out, pad_regions = plan(
            c, sb, sem, ps[:, 0, 0:NE], as_table(turn[:], "p a d -> p (a d)", T, NE), as_table(half[:], "p a d -> p (a d)", NE, N),
            as_table(s_sb[:], "p b t h n -> p (b t h n)", SLOTS, NE), as_table(pT[:], "p b t g q -> p (b t g q)", SLOTS, NE))

        with nc.Block() as block:
            @block.sync
            def _(sp):
                for to, of in c.late_loads:
                    sp.dma_start(to, of).then_inc(c.late_in, 16)
                sp.dma_start(c.w13[:], c.dram["w13"]).then_inc(c.experts_in, 16)
                for k in range(HC):
                    n = min(P, HID - k * P)
                    if n < P:
                        sp.wait_ge(c.pad_ok, 1)
                    sp.dma_start(c.w2[0:n, :, k, :], c.dram["w2"][k * P:k * P + n]).then_inc(c.experts_in, 16)
                pad_regions(sp)

            @block.vector
            def _(eng):
                cos = c.tab[:, T_COS:T_COS + HD].unsqueeze(1).unsqueeze(1)
                sin = c.tab[:, T_SIN:T_SIN + HD].unsqueeze(1).unsqueeze(1)
                causal = c.tab[:, T_CAUSAL:T_CAUSAL + N].unsqueeze(1).unsqueeze(1).broadcast_to([P, H, GT, N])
                eng.memset(c.cum[:], 0.0).then_inc(s.filled, 1)
                eng.memset(c.cum16[:], 0.0).then_inc(s.filled, 1)
                eng.tensor_copy(c.low16[:], c.tab[:, T_LOW:T_LOW + P]).then_inc(s.filled, 1)

                def route(g, part, between, par=None):
                    base, count = (g - 1) // 2 * STEPS, [FIRST_STEPS * part]

                    def step(instruction):
                        count[0] += 1
                        instruction.then_inc(s.chain, 1)
                        between(count[0] - FIRST_STEPS * part - 1)
                        eng.wait_ge(s.chain, base + count[0])

                    tiles = bass.ds((g - 1) * GT, TB)
                    o1, o2 = c.o1[:, tiles, :], c.o2[:, tiles, :]
                    rev = c.tab[:, T_REV:T_REV + NE].unsqueeze(1).broadcast_to([P, TB, NE])

                    def wide(a):
                        return a.unsqueeze(2).broadcast_to([P, TB, NE])

                    if part == 0:
                        choose(g, step, o1, o2, rev, wide)
                        assert count[0] == FIRST_STEPS
                    else:
                        place(g, step, o1, o2, tiles, par)
                        assert count[0] == STEPS

                def choose(g, step, o1, o2, rev, wide):
                    step(eng.tensor_reduce(m1[:], lg[:], AX, ALU.max))
                    step(eng.tensor_tensor(ra[:], lg[:], wide(m1[:]), ALU.is_equal))
                    step(eng.tensor_tensor(ra[:], ra[:], rev, ALU.mult))
                    step(eng.tensor_reduce(km[:], ra[:], AX, ALU.max))
                    step(eng.tensor_tensor(o1, ra[:], wide(km[:]), ALU.is_equal))
                    step(eng.scalar_tensor_tensor(rb[:], o1, NEG, lg[:], ALU.mult, ALU.add))
                    step(eng.tensor_reduce(m2[:], rb[:], AX, ALU.max))
                    step(eng.tensor_tensor(rb[:], rb[:], wide(m2[:]), ALU.is_equal))
                    step(eng.tensor_tensor(rb[:], rb[:], rev, ALU.mult))
                    step(eng.tensor_reduce(km[:], rb[:], AX, ALU.max))
                    step(eng.tensor_tensor(o2, rb[:], wide(km[:]), ALU.is_equal))
                    step(eng.tensor_tensor(m16[:], o1, o2, ALU.add))
                    eng.tensor_tensor(ra[:], o1, o2, ALU.add).then_inc(s.rank_in, 2)
                    eng.tensor_tensor(ex[:, :, 0:NE], lg[:], wide(m1[:]), ALU.subtract)
                    eng.tensor_tensor(ex[:, :, NE], m2[:], m1[:], ALU.subtract).then_inc(s.ex_in, 2)

                def place(g, step, o1, o2, tiles, par):
                    eng.wait_ge(s.rank_got, g + 1)
                    eng.wait_ge(s.rank_in, g + 1)
                    step(eng.tensor_reduce(km[:, 0:NE], ra[:].rearrange("p t e -> p e t"), AX, ALU.add))
                    step(eng.tensor_tensor(c.cum[:], c.cum[:], km[:, 0:NE], ALU.add))
                    step(eng.tensor_copy(c.cum16[:], c.cum[:]))
                    step(eng.tensor_tensor(ra[:], rank[:], o1, ALU.mult))
                    step(eng.tensor_reduce(c.place[:, 0, tiles], ra[:], AX, ALU.add))
                    step(eng.tensor_tensor(ra[:], rank[:], o2, ALU.mult))
                    step(eng.tensor_reduce(c.place[:, 1, tiles], ra[:], AX, ALU.add))
                    eng.tensor_copy(slot[:, par], c.place[:, :, tiles]).then_inc(s.slot_ok, 2)
                    eng.wait_ge(s.ex_ok, g + 1)
                    step(eng.tensor_reduce(zsum[:], ex[:, :, 0:NE], AX, ALU.add))
                    step(eng.scalar_tensor_tensor(wa[:], zsum[:], 1e-9, ex[:, :, NE], ALU.mult, ALU.add))
                    step(eng.tensor_scalar(wa[:], wa[:], 1.0, None, ALU.add))
                    step(eng.reciprocal(wb[:], wa[:]))
                    step(eng.tensor_tensor(c.weight[:, 1, tiles], wb[:], ex[:, :, NE], ALU.mult))
                    step(eng.tensor_copy(c.weight[:, 0, tiles], wb[:]))

                def body(i, q):
                    b = q % 2
                    g = i - 5
                    if live(g):
                        eng.wait_ge(s.lg_done, g + 1)
                        eng.tensor_copy(lg[:, (1 - b) * GT:(1 - b) * GT + GT, :], lg_ps).then_inc(s.lg_ok, 1)

                    def x_tile(t):
                        return c.x[:, bass.ds(i * GT + t, 1), :].rearrange("p a f -> p (a f)")

                    def statistics(t):
                        if live(i) and t < GT:
                            m = eng.bn_stats(st[:, b, t, :], x_tile(t))
                            if t == GT - 1:
                                m.then_inc(s.bn, 1)

                    if live(g) and q % 2 == 0:
                        eng.wait_ge(s.lg_ok, g + 1)
                        route(g, 0, statistics)
                    else:
                        for t in range(GT):
                            statistics(t)
                    g = i
                    if live(g):
                        eng.wait_ge(s.bn, g + 1)
                        need(eng, s.rr_ok, g - 1)
                        alone(eng, c.passed)
                        for t in range(GT):
                            m = eng.bn_aggr(mv[:, b, t, :], st[:, b, t, :])
                        m.then_inc(s.stats, 1)
                    g = i - 2
                    if live(g):
                        eng.wait_ge(s.s_done, g + 1)
                        need(eng, s.pT_done, g - 1)
                        eng.tensor_tensor(s_sb[:, b].rearrange("p t h n -> p h t n"), s_ps, causal, ALU.add).then_inc(s.masked, 1)
                    g = i - 2
                    if live(g):
                        eng.wait_ge(s.masked, g + 1)
                        eng.tensor_reduce(mx[:], s_sb[:, b], AX, ALU.max).then_inc(s.top, 1)
                    g = i - 2
                    if live(g):
                        eng.wait_ge(s.top, g + 1)
                        eng.tensor_tensor(s_sb[:, b], s_sb[:, b], mx[:].unsqueeze(3)
                                          .broadcast_to([P, GT, H, N]), ALU.subtract).then_inc(s.centred, 1)
                    g = i - 1
                    if live(g):
                        o = turn[:].rearrange("p (k a) d -> p k a d", k=2)
                        o2 = half[:].rearrange("p (k a) d -> p k a d", k=2)
                        shape = [P, 2, 2 * 6, HD]
                        lo, hi = slice(0, HD // 2), slice(HD // 2, HD)
                        hshape = [P, 2, 2 * 6, HD // 2]
                        eng.wait_ge(s.qk_done, g + 1)
                        need(eng, s.qkT_done, g - 1)
                        need(eng, s.turned, g)
                        eng.tensor_tensor(o, qk_ps, cos.broadcast_to(shape), ALU.mult)
                        eng.tensor_tensor(o2[:, :, :, lo], qk_ps[:, :, :, hi], sin[:, :, :, lo].broadcast_to(hshape), ALU.mult)
                        eng.tensor_tensor(o2[:, :, :, hi], qk_ps[:, :, :, lo], sin[:, :, :, hi].broadcast_to(hshape), ALU.mult)\
                           .then_inc(s.turned1, 1)
                        eng.wait_ge(s.turned1, g + 1)
                        t4, h4 = (a[:].rearrange("p (t a) d -> p t a d", t=GT) for a in (turn, half))
                        eng.tensor_tensor(qk[:, 1 - b, :, 0:H], t4[:, :, 0:H], h4[:, :, 0:H], ALU.add)
                        for k in range(KV):
                            one = slice(H + k, H + k + 1)
                            m = eng.tensor_tensor(qk[:, 1 - b, :, H + 2 * k:H + 2 * k + 2], t4[:, :, one].broadcast_to([P, GT, 2, HD]),
                                                  h4[:, :, one].broadcast_to([P, GT, 2, HD]), ALU.add)
                        m.then_inc(s.turned, 1)
                    g = i - 3
                    if live(g):
                        eng.wait_ge(s.y_done, g + 1)
                        eng.reciprocal(rcp[:], y_ps[:, :, :, HD]).then_inc(s.recip, 1)
                        eng.wait_ge(s.recip, g + 1)
                        need(eng, s.yT_done, g - 1)
                        eng.tensor_tensor(y[:, 1 - b].rearrange("p (k t) (a d) -> p k (t a) d", k=2, d=HD), y_ps[:, :, :, 0:HD],
                                          rcp[:].unsqueeze(3).broadcast_to([P, 2, 2 * H, HD]), ALU.mult).then_inc(s.y_ok, 1)
                    g = i - 5
                    if live(g) and q % 2 == 0:
                        eng.wait_ge(s.rank_done, g + 1)
                        eng.tensor_tensor(rank[:], rank_ps, c.tab[:, T_REGION:T_REGION + NE].unsqueeze(1)
                                          .broadcast_to([P, TB, NE]), ALU.add).then_inc(s.rank_got, 2)
                    if live(i):
                        eng.wait_ge(s.rr_ok, i + 1)
                        need(eng, s.flat_ok, i - 3)
                        need(eng, s.x_ok, i - 3)

                    def normalise(t):
                        if live(i) and t < GT:
                            m = eng.tensor_scalar(f[:, q, t, :], x_tile(t), mv[:, b, t, 0:1], rr[:, b, t:t + 1],
                                                  ALU.subtract, ALU.mult)
                            if t == GT - 1:
                                m.then_inc(s.f_ok, 1)

                    g = i - 5
                    if live(g) and q % 2 == 0:
                        route(g, 1, normalise, (q - 1) % U // 2)
                    else:
                        for t in range(GT):
                            normalise(t)
                    g = i - 3
                    if live(g):
                        fq = f[:, (q + 1) % U]
                        eng.wait_ge(s.at_done, g + 1)
                        eng.wait_ge(s.f_ok, g + 1)
                        eng.tensor_tensor(fq, at_ps, fq, ALU.add).then_inc(s.x1_ok, 1)
                pipeline(eng, body, LAG, unroll=U, lead=U - 1)
                work_out(eng)

            @block.gpsimd
            def _(eng):
                eng.memset(c.w2[64:P, :, HC - 1, :], 0.0).then_inc(c.pad_ok, 1)
                eng.wait_ge(c.pad_ok, 1)
                eng.memset(vx[:], 0.0).then_inc(s.filled, 1)
                eng.wait_ge(s.filled, 4)
                eng.memset(vx[0:N, :, :, :, 0, HD:HD + 1], 1.0).then_inc(s.filled, 1)
                eng.wait_ge(s.filled, 5)
                eng.memset(vx[N:P, :, :, :, 1, HD:HD + 1], 1.0).then_inc(s.filled, 1)
                eng.wait_ge(s.filled, 6)

                def body(i, q):
                    b = q % 2
                    g = i
                    if live(g):
                        eng.wait_ge(s.stats, g + 1)
                        alone(eng, c.passed)
                        eng.tensor_scalar(minus[:, b], mv[:, b, :, 0], -1.0, None, ALU.mult)
                        eng.tensor_scalar(var[:, b, 0:GT], mv[:, b, :, 1], 1.0, EPS, ALU.mult, ALU.add)
                        eng.tensor_scalar(var[:, b, GT:2 * GT], mv[:, b, :, 1], 1.0 + EPS_RMS, EPS_RMS * EPS, ALU.mult, ALU.add)\
                           .then_inc(s.var_ok, 1)
                        eng.wait_ge(s.var_ok, g + 1)
                        need(eng, s.h_ok, g - 1)
                        need(eng, s.f_ok, g - 1)
                        eng.tensor_tensor(rr[:, b], var[:, b], c.minus_half[:], ALU.pow).then_inc(s.rr_ok, 1)
                        eng.wait_ge(s.rr_ok, g + 1)
                        eng.tensor_tensor(shift[:, b], minus[:, b], rr[:, b, GT:2 * GT], ALU.mult).then_inc(s.shift_ok, 1)
                    for g, half in ((i - 6, 0), (i - 7, 1)):
                        last = (q - 6 - half) % U
                        if live(g) and last % 2:
                            par = last // 2
                            eng.wait_ge(s.slot_ok, g + 1)
                            alone(eng, c.passed)
                            for t in range(half * GT, half * GT + GT):
                                for k in range(2):
                                    eng.indirect_dma_start(
                                        c.dram["rows"], bass.IndirectOffsetOnAxis(ap=slot[:, par, k, t:t + 1], axis=0),
                                        flat[:, par, t, :], None).then_inc(scattered[2 * par + half], 16)
                    g = i - 3
                    if live(g):
                        eng.wait_ge(s.ssq_ok, g + 1)
                        alone(eng, c.passed)
                        eng.tensor_scalar(var3[:, 1 - b], ssq[:, 1 - b], 1.0 / D, EPS_RMS, ALU.mult, ALU.add).then_inc(s.var3_ok, 1)
                        eng.wait_ge(s.var3_ok, g + 1)
                        need(eng, s.flat_ok, g - 1)
                        eng.tensor_tensor(r3[:, 1 - b], var3[:, 1 - b], c.minus_half[:, 0:GT], ALU.pow).then_inc(s.r3_ok, 1)
                        fq = f[:, (q + 1) % U]
                        eng.tensor_tensor(c.x[:, tile4(g), :], c.x[:, tile4(g), :], fq, ALU.add).then_inc(s.x_ok, 1)
                pipeline(eng, body, LAG + 2, unroll=U, lead=U - 3)
                for k in range(U):
                    eng.wait_ge(scattered[k], 16 * 2 * GT * G // U)

            @block.scalar
            def _(eng):
                eng.preload_act_table_set("exp_and_others")
                eng.wait_ge(s.filled, 6)

                def body(i, q):
                    b = q % 2
                    g = i - 1
                    if live(g):
                        eng.wait_ge(s.hT_done, g + 1)
                        need(eng, s.v_done, g - 1)
                        eng.activation(hT[:, 1 - b], hT_ps, ACT.Copy, scale=c.ln1).then_inc(s.hT_ok, 1)
                    g = i - 3
                    if live(g):
                        eng.wait_ge(s.pT_done, g + 1)
                        need(eng, s.y_done, g - 1)
                        eng.activation(pT[:, 1 - b], pT_ps, ACT.Copy).then_inc(s.pT_ok, 1)
                    g = i - 2
                    if live(g):
                        eng.wait_ge(s.centred, g + 1)
                        eng.activation(s_sb[:, b], s_sb[:, b], ACT.Exp, scale=float(1.0 / np.sqrt(np.float32(HD)))).then_inc(s.e_ok, 1)
                    g = i - 4
                    if live(g):
                        eng.wait_ge(s.r3_ok, g + 1)
                        need(eng, scattered[q], 32 * (g - q))
                        for t in range(GT):
                            m = eng.activation(flat[:, q // 2, q % 2 * GT + t, :], f[:, q, t, :], ACT.Copy, scale=r3[:, b, t:t + 1])
                        m.then_inc(s.flat_ok, 1)
                    g = i - 1
                    if live(g):
                        eng.wait_ge(s.v_done, g + 1)
                        need(eng, s.y_done, g - 1)
                        for k in range(2):
                            r = slice(N * k, N * k + N)
                            m = eng.activation(vx[r, 1 - b, :, :, k, 0:HD],
                                               v_ps[r].rearrange("p t j (g e) -> p (t j) g e", g=KV), ACT.Copy)
                        m.then_inc(s.v_ok, 1)
                    g = i - 1
                    if live(g):
                        eng.wait_ge(s.qkT_done, g + 1)
                        need(eng, s.s_done, g - 1)
                        eng.activation(qT[:, 1 - b], qT_ps, ACT.Copy)
                        eng.activation(kT[:, 1 - b], kT_ps, ACT.Copy).then_inc(s.qkT_ok, 1)
                    g = i - 3
                    if live(g):
                        eng.wait_ge(s.yT_done, g + 1)
                        need(eng, s.at_done, g - 1)
                        eng.activation(yT[:, 1 - b], yT_ps, ACT.Copy).then_inc(s.yT_ok, 1)
                    g = i - 4
                    if live(g):
                        eng.wait_ge(s.fT_done, g + 1)
                        need(eng, s.lg_done, g - 1)
                        eng.activation(fT[:, b], fT_ps, ACT.Copy, scale=c.ln2).then_inc(s.fT_ok, 1)
                    g = i
                    if live(g):
                        eng.wait_ge(s.shift_ok, g + 1)
                        need(eng, s.hT_done, g - 1)
                        for t in range(GT):
                            m = eng.activation(h[:, b, t, :], c.x[:, bass.ds(g * GT + t, 1), :].rearrange("p a f -> p (a f)"),
                                               ACT.Identity, scale=rr[:, b, GT + t:GT + t + 1], bias=shift[:, b, t:t + 1])
                        m.then_inc(s.h_ok, 1)
                    g = i - 5
                    if live(g) and q % 2 == 0:
                        eng.wait_ge(s.ex_in, g + 1)
                        eng.activation(ex[:], ex[:], ACT.Exp).then_inc(s.ex_ok, 2)
                    g = i - 3
                    if live(g):
                        eng.wait_ge(s.x1_ok, g + 1)
                        need(eng, s.var3_ok, g - 1)
                        need(eng, s.ssq_ok, g)
                        for t in range(GT):
                            m = eng.activation(junk[:, t, :], f[:, (q + 1) % U, t, :], ACT.Square, accum_out=ssq[:, 1 - b, t:t + 1])
                        m.then_inc(s.ssq_ok, 1)
                pipeline(eng, body, LAG, unroll=U, lead=U - 1)

            @block.tensor
            def _(eng):
                eng.wait_ge(s.filled, 6)

                def body(i, q):
                    b = q % 2
                    g = i - 2
                    if live(g):
                        eng.wait_ge(s.qkT_ok, g + 1)
                        eng.wait_ge(s.v_ok, g + 1)
                        need(eng, s.fT_ok, g - 2)
                        for t in range(GT):
                            for j in range(2):
                                cols = slice(t * P + j * N, t * P + j * N + N)
                                for hd in range(H):
                                    r = slice(HD * hd, HD * hd + HD)
                                    m = eng.matmul(s_ps[N * j:N * j + N, hd, t, :], qT[r, b, cols], kT[r, b, cols],
                                                   start=True, stop=True)
                        m.then_inc(s.s_done, 1)
                    g = i - 1
                    if live(g):
                        eng.wait_ge(s.h_ok, g + 1)
                        need(eng, s.turned1, g)
                        for t in range(GT):
                            m = eng.transpose(hT_ps[:, t, :], h[:, 1 - b, t, :], c.ident[:])
                        m.then_inc(s.hT_done, 1)
                    g = i - 3
                    if live(g):
                        eng.wait_ge(s.e_ok, g + 1)
                        need(eng, s.yT_ok, g)
                        need(eng, s.x1_ok, g)
                        for t in range(GT):
                            for k in range(KV):
                                m = eng.transpose(pT_ps[:, t, k, :], s_sb[:, 1 - b, t, 2 * k:2 * k + 2, :].rearrange("p a n -> p (a n)"), c.ident[:])
                        m.then_inc(s.pT_done, 1)
                    g = i - 1
                    if live(g):
                        eng.wait_ge(s.hT_ok, g + 1)
                        need(eng, s.lg_ok, g - 3)
                        for t in range(GT):
                            m = eng.matmul(qk_ps[:, t // 2, t % 2 * 6:t % 2 * 6 + 6, :], hT[:, 1 - b, t, :], c.wqk[:],
                                           start=True, stop=True)
                        m.then_inc(s.qk_done, 1)
                    g = i - 1
                    if live(g):
                        need(eng, s.masked, g)
                        for t in range(GT):
                            for j in range(2):
                                for k in range(2):
                                    m = eng.matmul(v_ps[N * k:N * k + N, t, j, :], hT[:, 1 - b, t, N * j:N * j + N], c.wv[:],
                                                   start=True, stop=True)
                        m.then_inc(s.v_done, 1)
                    g = i - 3
                    if live(g):
                        eng.wait_ge(s.pT_ok, g + 1)
                        for t in range(GT):
                            for j in range(2):
                                for k in range(KV):
                                    o = (t % 2 * KV + k) * 2
                                    m = eng.matmul(y_ps[N * j:N * j + N, t // 2, o:o + 2, :],
                                                   pT[:, 1 - b, t, k, N * j:N * j + N], vx[:, 1 - b, 2 * t + j, k],
                                                   start=True, stop=True)
                        m.then_inc(s.y_done, 1)
                    g = i - 1
                    if live(g):
                        eng.wait_ge(s.turned, g + 1)
                        for t in range(GT):
                            qt = qk[:, 1 - b, t, 0:H, :].rearrange("p a d -> p (a d)")
                            kt = qk[:, 1 - b, t, H:2 * H, :].rearrange("p a d -> p (a d)")
                            eng.transpose(qT_ps[:, t * P:t * P + P], qt, c.ident[:])
                            m = eng.transpose(kT_ps[:, t * P:t * P + P], kt, c.ident[:])
                        m.then_inc(s.qkT_done, 1)
                    g = i - 5
                    if live(g) and q % 2 == 0:
                        eng.wait_ge(s.rank_in, g + 1)
                        need(eng, s.rank_got, g - 1)
                        eng.matmul(rank_ps, c.low16[:], m16[:], start=True, stop=False)
                        for k in range(1, TB):
                            eng.matmul(rank_ps[:, k:TB, :], c.ones16[:], m16[:, 0:TB - k, :], start=False, stop=False)
                        eng.matmul(rank_ps, c.ones16[:], c.cum16[:].unsqueeze(1).broadcast_to([P, TB, NE]),
                                   start=False, stop=True).then_inc(s.rank_done, 2)
                    g = i - 3
                    if live(g):
                        eng.wait_ge(s.y_ok, g + 1)
                        for t in range(GT):
                            m = eng.transpose(yT_ps[:, t, :], y[:, 1 - b, t, :], c.ident[:])
                        m.then_inc(s.yT_done, 1)
                    g = i - 4
                    if live(g):
                        if isinstance(i, int):
                            need(eng, s.masked, min(i - 1, G))
                        eng.wait_ge(s.flat_ok, g + 1)
                        for t in range(GT):
                            m = eng.transpose(fT_ps[:, t, :], flat[:, q // 2, b * GT + t, :], c.ident[:])
                        m.then_inc(s.fT_done, 1)
                    g = i - 3
                    if live(g):
                        eng.wait_ge(s.yT_ok, g + 1)
                        for t in range(GT):
                            m = eng.matmul(at_ps[:, t, :], yT[:, 1 - b, t, :], c.wo[:], start=True, stop=True)
                        m.then_inc(s.at_done, 1)
                    g = i - 4
                    if live(g):
                        eng.wait_ge(s.fT_ok, g + 1)
                        need(eng, s.lg_ok, g)
                        if isinstance(i, int):
                            need(eng, s.turned1, min(i, G))
                        else:
                            eng.wait_ge(s.turned1, i)
                        if q % 2 == 0:
                            need(eng, s.rank_got, g)
                        for t in range(GT):
                            m = eng.matmul(lg_ps[:, t, :], fT[:, b, t, :], c.router[:], start=True, stop=True)
                        m.then_inc(s.lg_done, 1)
                pipeline(eng, body, LAG, unroll=U, lead=U - 1)
                eng.wait_ge(s.slot_ok, G)
                count_rows(eng)
        signals.give_back()


def moe_phases(nc, c, sb, sem):
    c.w13 = sb("w13", [D, NE, 2, HID])
    c.w2 = sb("w2", [P, NE, HC, D])
    c.o1 = sb("o1", [P, T, NE]); c.o2 = sb("o2", [P, T, NE])
    c.place = sb("place", [P, 2, T])
    c.weight = sb("weight", [P, 2, T])
    c.cum = sb("cum", [P, NE]); c.cum16 = sb("cum16", [P, NE], BF16)
    c.back = sb("back", [P, 2, T], I32)
    c.expert = sb("expert", [P, SLOTS], I32)
    c.source = sb("source", [P, SLOTS], I32)
    c.experts_in, c.pad_ok = sem("experts_in"), sem("pad_ok")
    attention(nc, c)
    experts(nc, c)


def experts(nc, c):
    LAG, U = 4, 4
    with ExitStack() as ctx:
        def sb(name, shape, dt=F32):
            return ctx.enter_context(nc.sbuf_tensor("d_" + name, shape, dt))

        rows = sb("rows", [P, U, D])
        rT = sb("rT", [P, 2, P])
        th = sb("th", [P, 2, HID])
        u = sb("u", [P, 2, HID])
        hid = sb("hid", [P, 2, HC * P])
        hT = sb("hT", [P, 2, HC, P])
        y = sb("y", [P, U, D])
        keep = sb("keep", [P, T, N])
        signals = Signals(nc, "d")
        ps = ctx.enter_context(nc.psum_tensor("d_ps", [P, 8, 512], F32))
        a_ps = [ps[:, 0, 0:HID], ps[:, 1, 0:HID]]
        b_ps = [ps[:, 2, 0:HID], ps[:, 3, 0:HID]]
        rT_ps = [ps[:, 4, 0:P], ps[:, 7, 0:P]]
        hT_ps = ps[:, 5, 0:HC * P].rearrange("p (k r) -> p k r", k=HC)
        y_ps = ps[:, 6, 0:D]

        s = Memory()
        s.rT_done, s.rT_ok, s.ab_done, s.th_ok = signals.new("rT_done"), signals.new("rT_ok"), signals.new("ab_done"), signals.new("th_ok")
        s.u_ok, s.hid_ok, s.hT_done, s.hT_ok = signals.new("u_ok"), signals.new("hid_ok"), signals.new("hT_done"), signals.new("hT_ok")
        s.y_done, s.y_ok, s.pad = signals.new("y_done"), signals.new("y_ok"), signals.new("pad")
        s.a_done = signals.new("a_done")
        loaded = [signals.new(f"loaded{k}") for k in range(U)]
        stored = [signals.new(f"stored{k}") for k in range(U)]

        def run(eng, body):
            pipeline(eng, body, LAG, groups=SLOTS, unroll=U, lead=U)

        mask = sb("mask", [P, T, N], I32)
        mask_in = signals.new("mask_in")
        mask_ok = signals.new("mask_ok")

        with nc.Block() as block:
            @block.gpsimd
            def _(eng):
                eng.wait_ge(mask_in, 32)
                eng.tensor_scalar(c.masked[:], mask[:], 0.0, None, ALU.is_equal).then_inc(mask_ok, 1)
                eng.wait_ge(mask_ok, 1)
                eng.tensor_scalar(keep[:], c.masked[:], -1.0, 1.0, ALU.mult, ALU.add).then_inc(mask_ok, 1)
                eng.wait_ge(mask_ok, 2)
                eng.tensor_tensor(c.adj[:], c.adj[:], keep[:], ALU.mult).then_inc(mask_ok, 1)
                eng.tensor_scalar(c.masked[:], c.masked[:], NEG, None, ALU.mult).then_inc(mask_ok, 1)

            @block.sync
            def _(eng):
                for j in range(2):
                    eng.dma_start(mask[N * j:N * j + N], c.dram["nodemask"].rearrange("(t j) n -> j t n", j=2)[j]
                                  .partition_broadcast(N)).then_inc(mask_in, 16)

                def body(i, q):
                    g = i
                    if live(g, SLOTS):
                        row = eng.value_load(c.source[0:1, bass.ds(g, 1)], min_val=0, max_val=NE * REGION - P)
                        need(eng, s.rT_done, g - U + 1)
                        eng.dma_start(rows[:, q, :], c.dram["rows"][bass.ds(row, P), :]).then_inc(loaded[q], 16)
                    g = i - 7
                    if live(g, SLOTS):
                        eng.wait_ge(s.y_ok, g + 1)
                        eng.dma_start(c.dram["picked"][bass.ds(g * P, P), :], y[:, (q + 1) % U, :])\
                           .then_inc(stored[(q + 1) % U], 16)
                pipeline(eng, body, 7, groups=SLOTS, unroll=U, lead=U)
                for k in range(U):
                    eng.wait_ge(stored[k], 16 * SLOTS // U)

            @block.tensor
            def _(eng):
                eng.wait_ge(c.experts_in, 16 * (1 + HC))
                eng.wait_ge(s.pad, 1)
                before = [eng.alloc_register(f"expert_before{k}") for k in range(U)]
                now = [eng.alloc_register(f"expert_now{k}") for k in range(2 * U)]

                def prepare(i, count):
                    for k in range(U):
                        if not isinstance(i, int) or i > 0:
                            eng.reg_mov(before[k], now[U + k])
                    if live(i, SLOTS):
                        eng.load(now, c.expert[0:1, bass.ds(i, 2 * U)])

                def expert_of(k):
                    return eng.snap(now[k] if k >= 0 else before[k + U]).with_bounds(min_val=0, max_val=NE - 1)

                def body(i, turn):
                    q, b = turn % U, turn % 2
                    g = i - 1
                    if live(g, SLOTS):
                        eng.wait_ge(loaded[(q - 1) % U], 4 * (g - (q - 1) % U) + 16)
                        need(eng, s.rT_ok, g - 1)
                        eng.transpose(rT_ps[1 - b], rows[:, (q - 1) % U, :], c.ident[:]).then_inc(s.rT_done, 1)
                    g = i - 2
                    if live(g, SLOTS):
                        e = expert_of(turn - 2)
                        eng.wait_ge(s.rT_ok, g + 1)
                        need(eng, s.hid_ok, g - 1)
                        for k, (out, done) in enumerate(((a_ps[b], s.a_done), (b_ps[b], s.ab_done))):
                            eng.matmul(out, rT[:, b], c.w13[:, bass.ds(e, 1), k, :].rearrange("p a h -> p (a h)"),
                                       start=True, stop=True).then_inc(done, 1)
                    g = i - 3
                    if live(g, SLOTS):
                        eng.wait_ge(s.hid_ok, g + 1)
                        need(eng, s.hT_ok, g)
                        for k in range(HC):
                            m = eng.transpose(hT_ps[:, k, :], hid[:, 1 - b, k * P:k * P + P], c.ident[:])
                        m.then_inc(s.hT_done, 1)
                    g = i - 4
                    if live(g, SLOTS):
                        e = expert_of(turn - 4)
                        eng.wait_ge(s.hT_ok, g + 1)
                        need(eng, s.y_ok, g)
                        for k in range(HC):
                            m = eng.matmul(y_ps, hT[:, b, k, :], c.w2[:, bass.ds(e, 1), k, :].rearrange("p a f -> p (a f)"),
                                           start=(k == 0), stop=(k == HC - 1))
                        m.then_inc(s.y_done, 1)
                pipeline(eng, body, LAG, groups=SLOTS, unroll=2 * U, lead=U, prepare=prepare)

            @block.scalar
            def _(eng):
                def body(i, q):
                    b = q % 2
                    g = i - 1
                    if live(g, SLOTS):
                        eng.wait_ge(s.rT_done, g + 1)
                        need(eng, s.ab_done, g - 1)
                        eng.activation(rT[:, 1 - b], rT_ps[1 - b], ACT.Copy, scale=c.ln2).then_inc(s.rT_ok, 1)
                    g = i - 2
                    if live(g, SLOTS):
                        eng.wait_ge(s.a_done, g + 1)
                        need(eng, s.u_ok, g - 1)
                        eng.activation(th[:, b], a_ps[b], ACT.Tanh, scale=0.5).then_inc(s.th_ok, 1)
                    g = i - 4
                    if live(g, SLOTS):
                        eng.wait_ge(s.y_done, g + 1)
                        need(eng, stored[q], 4 * (g - q))
                        eng.activation(y[:, q, :], y_ps, ACT.Copy).then_inc(s.y_ok, 1)
                run(eng, body)

            @block.vector
            def _(eng):
                eng.memset(hid[:, :, HID:HC * P], 0.0).then_inc(s.pad, 1)

                def body(i, q):
                    b = q % 2
                    g = i - 3
                    if live(g, SLOTS):
                        eng.wait_ge(s.hT_done, g + 1)
                        need(eng, s.y_done, g - 1)
                        eng.tensor_copy(hT[:, 1 - b], hT_ps).then_inc(s.hT_ok, 1)
                    g = i - 2
                    if live(g, SLOTS):
                        eng.wait_ge(s.th_ok, g + 1)
                        eng.scalar_tensor_tensor(u[:, b], th[:, b], 1.0, a_ps[b], ALU.add, ALU.mult).then_inc(s.u_ok, 1)
                        eng.wait_ge(s.u_ok, g + 1)
                        eng.wait_ge(s.ab_done, g + 1)
                        need(eng, s.hT_done, g - 1)
                        eng.scalar_tensor_tensor(hid[:, b, 0:HID], u[:, b], 0.5, b_ps[b], ALU.mult, ALU.mult).then_inc(s.hid_ok, 1)
                run(eng, body)
        signals.give_back()


def last_round(nc, c):
    LAG, U = 5, 4
    with ExitStack() as ctx:
        def sb(name, shape, dt=F32):
            return ctx.enter_context(nc.sbuf_tensor("e_" + name, shape, dt))

        at = sb("at", [P, 2, 2, GT], I32)
        got = sb("got", [P, 2, 2, GT, D])
        st = sb("st", [P, 2, GT, 6]); mv = sb("mv", [P, 2, GT, 2])
        var = sb("var", [P, 2, GT]); rstd = sb("rstd", [P, 2, GT])
        z = sb("z", [P, U, GT, D])
        zT = sb("zT", [P, GT, P]); wT = sb("wT", [P, GT * P])
        sim = sb("sim", [P, GT, N]); top = sb("top", [P, GT]); total = sb("total", [P, GT]); inv = sb("inv", [P, GT])
        att = sb("att", [P, GT, P]); attT = sb("attT", [P, GT, P])
        z2 = sb("z2", [P, 2, GT, D]); z2T = sb("z2T", [P, GT * P])
        h1 = sb("h1", [P, GT * P]); h2 = sb("h2", [P, GT * P])
        e1 = sb("e1", [P, SE, GT * P]); e2 = sb("e2", [P, 2, GT * P]); e2g = sb("e2g", [P, 2, GT * P])
        gl = sb("gl", [P, GT, SE]); ga = sb("ga", [P, GT, SE]); o1 = sb("o1", [P, GT, SE]); o2 = sb("o2", [P, GT, SE])
        gv = sb("gv", [P, GT, SE])
        v1 = sb("v1", [P, GT]); v2 = sb("v2", [P, GT]); km = sb("km", [P, GT]); gd = sb("gd", [P, GT])
        gw1 = sb("gw1", [P, GT]); gw2 = sb("gw2", [P, GT])
        gate = sb("gate", [P, GT, SE + 1]); rest = sb("rest", [P, GT, SE + 1])
        KG = 3 * (SE + 1)
        parts = sb("parts", [P, GT, 3, SE + 1], BF16); gateT = sb("gateT", [KG, GT * P], BF16)
        pair16 = sb("pair16", [KG, 2 * P], BF16); ident16 = sb("ident16", [P, P], BF16)
        bias16 = sb("bias16", [KG, 3, D], BF16); bias_rest = sb("bias_rest", [KG, D])
        ps = ctx.enter_context(nc.psum_tensor("e_ps", [P, 8, 512], F32))

        def tiles(bank):
            return ps[:, bank, :].rearrange("p (t f) -> p t f", f=P)

        z2T_ps, attT_ps, gateT_ps = tiles(0), tiles(0), ps[0:KG, 0, :]
        zT_ps, sim_ps = tiles(1), ps[:, 1, 0:GT * N].rearrange("p (t n) -> p t n", n=N)
        h1_ps, h2_ps, out_ps = ps[:, 2, :], ps[:, 2, :], tiles(2)
        wT_ps, e1c_ps, e2b_ps = ps[:, 3, :], ps[:, 3, :], ps[:, 3, :]
        e1a_ps, e2a_ps = ps[:, 4, :], ps[:, 4, :]
        e1b_ps, wide0_ps = ps[:, 5, :], ps[:, 5, :]
        gl_ps, e1d_ps, wide1_ps = ps[:, 6, 0:GT * SE].rearrange("p (t e) -> p t e", e=SE), ps[:, 6, :], ps[:, 6, :]
        av_ps = tiles(7)
        e1_ps = [e1a_ps, e1b_ps, e1c_ps, e1d_ps]
        e2_ps, wide_ps = [e2a_ps, e2b_ps], [wide0_ps, wide1_ps]

        def sem(name):
            return ctx.enter_context(nc.semaphore("e_" + name))

        s = Memory()
        s.at_ok, s.picked1, s.picked, s.bn = sem("at_ok"), sem("picked1"), sem("picked"), sem("bn")
        s.stats, s.var_ok, s.rstd_ok, s.z_ok = sem("stats"), sem("var_ok"), sem("rstd_ok"), sem("z_ok")
        s.bn2, s.stats2, s.var2_ok, s.rstd2_ok = sem("bn2"), sem("stats2"), sem("var2_ok"), sem("rstd2_ok")
        s.z2_ok, s.zT_done, s.zT_ok, s.wT_done = sem("z2_ok"), sem("zT_done"), sem("zT_ok"), sem("wT_done")
        s.wT_ok, s.sim_done, s.sim1, s.sim2 = sem("wT_ok"), sem("sim_done"), sem("sim1"), sem("sim2")
        s.top_ok, s.sim_ok, s.att_ok, s.total_ok = sem("top_ok"), sem("sim_ok"), sem("att_ok"), sem("total_ok")
        s.inv_ok, s.attT_done, s.attT_ok, s.av_done = sem("inv_ok"), sem("attT_done"), sem("attT_ok"), sem("av_done")
        s.x1_ok, s.z2T_done, s.z2T_ok, s.gl_done = sem("x1_ok"), sem("z2T_done"), sem("z2T_ok"), sem("gl_done")
        s.gl_ok, s.gx_in, s.gx_ok, s.gd_in = sem("gl_ok"), sem("gx_in"), sem("gx_ok"), sem("gd_in")
        s.gd_ok, s.gate_ok, s.gateT_done, s.gateT_ok = sem("gd_ok"), sem("gate_ok"), sem("gateT_done"), sem("gateT_ok")
        s.h1_done, s.h1_ok, s.h2_done, s.h2_ok = sem("h1_done"), sem("h1_ok"), sem("h2_done"), sem("h2_ok")
        s.e1_done, s.e1_ok, s.e2_done, s.e2_ok = sem("e1_done"), sem("e1_ok"), sem("e2_done"), sem("e2_ok")
        s.wide_done, s.e2g_ok, s.out_done, s.x2_ok = sem("wide_done"), sem("e2g_ok"), sem("out_done"), sem("x2_ok")
        s.chain, s.cleared = sem("chain"), sem("cleared")
        got_in = [ctx.enter_context(nc.semaphore(f"e_got{k}")) for k in range(2)]
        STEPS = 22

        def run(eng, body):
            pipeline(eng, body, LAG, unroll=U, lead=U - 1)

        with nc.Block() as block:
            @block.sync
            def _(eng):
                out = c.dram["out"].rearrange("(t b) n f -> (b n) t f", b=2)

                def body(i, q):
                    g = i - 5
                    if live(g):
                        eng.wait_ge(s.x2_ok, g + 1)
                        eng.dma_start(out[:, tile4(g), :], c.x[:, tile4(g), :]).then_inc(c.stored, 16)
                run(eng, body)
                eng.wait_ge(c.stored, 16 * G)

            @block.gpsimd
            def _(eng):
                def rsqrt(g, k, bk, stats, var_ok, used, rstd_ok):
                    eng.wait_ge(stats, g + 1)
                    alone(eng, c.passed)
                    eng.tensor_scalar(var[:, k], mv[:, k, :, 1], 1.0, EPS, ALU.mult, ALU.add).then_inc(var_ok, 1)
                    eng.wait_ge(var_ok, g + 1)
                    need(eng, used, g)
                    eng.tensor_tensor(rstd[:, k], var[:, k], c.minus_half[:, 0:GT], ALU.pow).then_inc(rstd_ok, 1)

                def gather(k, b):
                    for t in range(GT):
                        eng.indirect_dma_start(
                            got[:, b, k, t, :], None, c.dram["picked"],
                            bass.IndirectOffsetOnAxis(ap=at[:, b, k, t:t + 1], axis=0)).then_inc(got_in[b], 16)

                def body(i, q):
                    b = q % 2
                    g = i - 1
                    if live(g):
                        rsqrt(g, 0, 1 - b, s.stats, s.var_ok, s.z_ok, s.rstd_ok)
                    g = i
                    if live(g):
                        eng.wait_ge(s.at_ok, g + 1)
                        need(eng, s.picked, g - 1)
                        alone(eng, c.passed)
                        gather(0, b)
                    g = i - 3
                    if live(g):
                        rsqrt(g, 1, 1 - b, s.stats2, s.var2_ok, s.z2_ok, s.rstd2_ok)
                    g = i
                    if live(g):
                        gather(1, b)
                run(eng, body)

            @block.vector
            def _(eng):
                eng.memset(att[:], 0.0).then_inc(s.cleared, 1)
                eng.memset(gate[:, :, SE:SE + 1], 1.0).then_inc(s.cleared, 1)
                eng.wait_ge(c.late_in, c.late_count)
                eng.tensor_copy(pair16[:], c.tab[0:KG, T_PAIR:T_PAIR + 2 * P]).then_inc(s.cleared, 1)
                eng.tensor_copy(ident16[:], c.ident).then_inc(s.cleared, 1)
                eng.tensor_copy(bias16[:, 0], c.bias3[:]).then_inc(s.cleared, 1)
                eng.wait_ge(s.cleared, 5)
                eng.tensor_tensor(bias_rest[:], c.bias3[:], bias16[:, 0], ALU.subtract).then_inc(s.cleared, 1)
                eng.wait_ge(s.cleared, 6)
                eng.tensor_copy(bias16[:, 1], bias_rest[:]).then_inc(s.cleared, 1)
                eng.wait_ge(s.cleared, 7)
                eng.tensor_tensor(bias16[:, 2], bias_rest[:], bias16[:, 1], ALU.subtract).then_inc(s.cleared, 1)

                def x_of(g, t):
                    return c.x[:, bass.ds(g * GT + t, 1), :].rearrange("p a f -> p (a f)")

                def pick(g, b, k, t):
                    return eng.scalar_tensor_tensor(x_of(g, t), got[:, b, k, t, :], c.weight[:, k, bass.ds(g * GT + t, 1)],
                                                    x_of(g, t), ALU.mult, ALU.add)

                def gates(g, between):
                    base, count = g * STEPS, [0]

                    def step(*instructions):
                        for m in instructions:
                            count[0] += 1
                            m.then_inc(s.chain, 1)
                        between()
                        eng.wait_ge(s.chain, base + count[0])

                    def wide(a):
                        return a[:].unsqueeze(2).broadcast_to([P, GT, SE])

                    rev = c.tab[:, T_REV4:T_REV4 + SE].unsqueeze(1).broadcast_to([P, GT, SE])
                    eng.wait_ge(s.gl_done, g + 1)
                    eng.tensor_tensor(gl[:], gl_ps, c.gate_b[:].unsqueeze(1).broadcast_to([P, GT, SE]), ALU.add).then_inc(s.gl_ok, 1)
                    eng.wait_ge(s.gl_ok, g + 1)
                    step(eng.tensor_reduce(v1[:], gl[:], AX, ALU.max))
                    eng.tensor_tensor(gl[:], gl[:], wide(v1), ALU.subtract).then_inc(s.gx_in, 1)
                    between()
                    eng.wait_ge(s.gx_ok, g + 1)
                    step(eng.tensor_reduce(v2[:], gl[:], AX, ALU.add))
                    step(eng.reciprocal(v1[:], v2[:]))
                    step(eng.tensor_tensor(gv[:], gl[:], wide(v1), ALU.mult))
                    step(eng.tensor_tensor(ga[:], gv[:], wide(v1), ALU.is_equal))
                    step(eng.tensor_tensor(ga[:], ga[:], rev, ALU.mult))
                    step(eng.tensor_reduce(km[:], ga[:], AX, ALU.max))
                    step(eng.tensor_tensor(o1[:], ga[:], wide(km), ALU.is_equal))
                    step(eng.scalar_tensor_tensor(gv[:], o1[:], NEG, gv[:], ALU.mult, ALU.add))
                    step(eng.tensor_reduce(v2[:], gv[:], AX, ALU.max))
                    eng.tensor_tensor(gd[:], v2[:], v1[:], ALU.subtract).then_inc(s.gd_in, 1)
                    step(eng.tensor_tensor(ga[:], gv[:], wide(v2), ALU.is_equal))
                    step(eng.tensor_tensor(ga[:], ga[:], rev, ALU.mult))
                    step(eng.tensor_reduce(km[:], ga[:], AX, ALU.max))
                    step(eng.tensor_tensor(o2[:], ga[:], wide(km), ALU.is_equal))
                    eng.wait_ge(s.gd_ok, g + 1)
                    step(eng.tensor_scalar(gw1[:], gd[:], 1.0, None, ALU.add),
                         eng.tensor_tensor(o2[:], o2[:], wide(gd), ALU.mult))
                    step(eng.reciprocal(gw2[:], gw1[:]),
                         eng.tensor_tensor(o2[:], o2[:], o1[:], ALU.add))
                    step(eng.tensor_tensor(gate[:, :, 0:SE], o2[:], wide(gw2), ALU.mult))
                    need(eng, s.gateT_done, g)
                    step(eng.tensor_copy(parts[:, :, 0], gate[:]))
                    step(eng.tensor_tensor(rest[:], gate[:], parts[:, :, 0], ALU.subtract))
                    step(eng.tensor_copy(parts[:, :, 1], rest[:]))
                    eng.tensor_tensor(parts[:, :, 2], rest[:], parts[:, :, 1], ALU.subtract).then_inc(s.gate_ok, 1)
                    assert count[0] == STEPS

                def moments(g, k, bn, stats, rstd_ok):
                    alone(eng, c.passed)
                    for t in range(GT):
                        m = eng.bn_stats(st[:, k, t, :], x_of(g, t))
                    m.then_inc(bn, 1)
                    eng.wait_ge(bn, g + 1)
                    need(eng, rstd_ok, g)
                    alone(eng, c.passed)
                    for t in range(GT):
                        m = eng.bn_aggr(mv[:, k, t, :], st[:, k, t, :])
                    m.then_inc(stats, 1)

                def body(i, q):
                    b = q % 2
                    g = i - 5
                    if live(g):
                        eng.wait_ge(s.out_done, g + 1)
                        eng.tensor_tensor(c.x[:, tile4(g), :], out_ps, c.x[:, tile4(g), :], ALU.add).then_inc(s.x2_ok, 1)
                    g = i - 1
                    picks = live(g)
                    if picks:
                        eng.wait_ge(got_in[1 - b], 64 * (g - (1 - b)) + 128)

                    turn = [0]

                    def between(g=g, picks=picks):
                        n, t = turn[0] // GT, turn[0] % GT
                        turn[0] += 1
                        if not picks or n > 3:
                            return
                        if n < 2:
                            m, done = pick(g, 1 - b, n, t), (s.picked1, s.picked)[n]
                        elif n == 2:
                            m, done = eng.bn_stats(st[:, 0, t, :], x_of(g, t)), s.bn
                        else:
                            if t == 0:
                                need(eng, s.rstd_ok, g)
                                alone(eng, c.passed)
                            m, done = eng.bn_aggr(mv[:, 0, t, :], st[:, 0, t, :]), s.stats
                        if t == GT - 1:
                            m.then_inc(done, 1)
                            if n < 3:
                                eng.wait_ge(done, g + 1)
                            if n in (1, 2):
                                alone(eng, c.passed)

                    if live(i - 4):
                        gates(i - 4, between)
                    while turn[0] < 4 * GT:
                        between()
                    g = i
                    if live(g):
                        need(eng, got_in[b], 64 * (g - b))
                        eng.tensor_copy(at[:, b], c.back[:, :, tile4(g)]).then_inc(s.at_ok, 1)
                    g = i - 3
                    if live(g):
                        eng.wait_ge(s.att_ok, g + 1)
                        eng.tensor_reduce(total[:], att[:], AX, ALU.add).then_inc(s.total_ok, 1)
                        eng.wait_ge(s.total_ok, g + 1)
                        eng.reciprocal(inv[:], total[:]).then_inc(s.inv_ok, 1)
                    g = i - 1
                    if live(g):
                        eng.wait_ge(s.rstd_ok, g + 1)
                        need(eng, s.av_done, g - 3)
                        for t in range(GT):
                            m = eng.tensor_scalar(z[:, (q - 1) % U, t, :], x_of(g, t), mv[:, 0, t, 0:1], rstd[:, 0, t:t + 1],
                                                  ALU.subtract, ALU.mult)
                        m.then_inc(s.z_ok, 1)
                    g = i - 4
                    if live(g):
                        for k in range(2):
                            eng.wait_ge(s.e2_ok, 2 * g + k + 1)
                            eng.wait_ge(s.wide_done, 2 * g + k + 1)
                            need(eng, s.out_done, g)
                            eng.tensor_tensor(e2g[:, k], e2[:, k], wide_ps[k], ALU.mult).then_inc(s.e2g_ok, 1)
                    g = i - 3
                    if live(g):
                        eng.wait_ge(s.av_done, g + 1)
                        eng.wait_ge(s.inv_ok, g + 1)
                        for t in range(GT):
                            m = eng.scalar_tensor_tensor(x_of(g, t), av_ps[:, t, :], inv[:, t:t + 1], x_of(g, t), ALU.mult, ALU.add)
                        m.then_inc(s.x1_ok, 1)
                        eng.wait_ge(s.x1_ok, g + 1)
                        moments(g, 1, s.bn2, s.stats2, s.rstd2_ok)
                    g = i - 2
                    if live(g):
                        eng.wait_ge(s.sim_done, g + 1)
                        eng.tensor_tensor(sim[:], sim_ps, c.adj[:, tile4(g), :], ALU.mult).then_inc(s.sim1, 1)
                        eng.wait_ge(s.sim1, g + 1)
                        eng.tensor_tensor(sim[:], sim[:], c.masked[:, tile4(g), :], ALU.add).then_inc(s.sim2, 1)
                    g = i - 3
                    if live(g):
                        eng.wait_ge(s.rstd2_ok, g + 1)
                        need(eng, s.z2T_done, g - 1)
                        for t in range(GT):
                            m = eng.tensor_scalar(z2[:, 1 - b, t, :], x_of(g, t), mv[:, 1, t, 0:1], rstd[:, 1, t:t + 1],
                                                  ALU.subtract, ALU.mult)
                        m.then_inc(s.z2_ok, 1)
                    g = i - 2
                    if live(g):
                        eng.wait_ge(s.sim2, g + 1)
                        eng.tensor_reduce(top[:], sim[:], AX, ALU.max).then_inc(s.top_ok, 1)
                        eng.wait_ge(s.top_ok, g + 1)
                        eng.tensor_tensor(sim[:], sim[:], top[:].unsqueeze(2).broadcast_to([P, GT, N]), ALU.subtract)\
                           .then_inc(s.sim_ok, 1)
                run(eng, body)

            @block.scalar
            def _(eng):
                eng.preload_act_table_set("exp_and_others")
                eng.wait_ge(s.cleared, 8)

                def relu(out, in_, bias):
                    return eng.activation(out, in_, ACT.Relu, bias=bias)

                def body(i, q):
                    g = i - 2
                    if live(g):
                        eng.wait_ge(s.zT_done, g + 1)
                        need(eng, s.sim_done, g)
                        eng.activation(zT[:], zT_ps, ACT.Copy).then_inc(s.zT_ok, 1)
                    g = i - 4
                    if live(g):
                        eng.wait_ge(s.z2T_done, g + 1)
                        need(eng, s.e1_done, 4 * g)
                        eng.activation(z2T[:], z2T_ps.rearrange("p t f -> p (t f)"), ACT.Copy).then_inc(s.z2T_ok, 1)
                    g = i - 3
                    if live(g):
                        eng.wait_ge(s.sim_ok, g + 1)
                        need(eng, s.attT_done, g)
                        need(eng, s.total_ok, g)
                        for j in range(2):
                            r = slice(N * j, N * j + N)
                            m = eng.activation(att[r, :, r], sim[r], ACT.Exp)
                        m.then_inc(s.att_ok, 1)
                    g = i - 4
                    if live(g):
                        eng.wait_ge(s.gx_in, g + 1)
                        eng.activation(gl[:], gl[:], ACT.Exp).then_inc(s.gx_ok, 1)
                    g = i - 2
                    if live(g):
                        eng.wait_ge(s.wT_done, g + 1)
                        eng.activation(wT[:], wT_ps, ACT.Copy).then_inc(s.wT_ok, 1)
                    g = i - 4
                    if live(g):
                        eng.wait_ge(s.h1_done, g + 1)
                        need(eng, s.h2_done, g)
                        relu(h1[:], h1_ps, c.sb1).then_inc(s.h1_ok, 1)
                    g = i - 4
                    if live(g):
                        for e in range(2):
                            eng.wait_ge(s.e1_done, 4 * g + e + 1)
                            relu(e1[:, e], e1_ps[e], c.eb1[:, e:e + 1]).then_inc(s.e1_ok, 1)
                    g = i - 3
                    if live(g):
                        eng.wait_ge(s.attT_done, g + 1)
                        need(eng, s.av_done, g)
                        eng.activation(attT[:], attT_ps, ACT.Copy).then_inc(s.attT_ok, 1)
                    g = i - 4
                    if live(g):
                        eng.wait_ge(s.gd_in, g + 1)
                        eng.activation(gd[:], gd[:], ACT.Exp).then_inc(s.gd_ok, 1)
                        eng.wait_ge(s.h2_done, g + 1)
                        need(eng, s.out_done, g)
                        relu(h2[:], h2_ps, c.sb2).then_inc(s.h2_ok, 1)
                        for e in range(2, 4):
                            eng.wait_ge(s.e1_done, 4 * g + e + 1)
                            relu(e1[:, e], e1_ps[e], c.eb1[:, e:e + 1]).then_inc(s.e1_ok, 1)
                        eng.wait_ge(s.e2_done, 2 * g + 1)
                        relu(e2[:, 0], e2_ps[0], c.eb2[:, 0:1]).then_inc(s.e2_ok, 1)
                        eng.wait_ge(s.gateT_done, g + 1)
                        eng.activation(gateT[:], gateT_ps, ACT.Copy).then_inc(s.gateT_ok, 1)
                        eng.wait_ge(s.e2_done, 2 * g + 2)
                        relu(e2[:, 1], e2_ps[1], c.eb2[:, 1:2]).then_inc(s.e2_ok, 1)
                run(eng, body)

            @block.tensor
            def _(eng):
                eng.wait_ge(s.cleared, 8)
                eng.wait_ge(c.late_in, c.late_count)

                def expert1(g, e):
                    eng.matmul(e1_ps[e], c.eW1[:, e, :], z2T[:], start=True, stop=True).then_inc(s.e1_done, 1)

                def expert2(g, k):
                    for j in range(2):
                        m = eng.matmul(e2_ps[k][64 * j:64 * j + 64], c.eW2[:, 2 * k + j, :], e1[:, 2 * k + j],
                                       start=True, stop=True)
                    m.then_inc(s.e2_done, 1)

                def body(i, q):
                    b = q % 2
                    g = i - 2
                    if live(g):
                        eng.wait_ge(s.z_ok, g + 1)
                        need(eng, s.sim1, g)
                        for t in range(GT):
                            m = eng.transpose(zT_ps[:, t, :], z[:, (q - 2) % U, t, :], c.ident[:])
                        m.then_inc(s.zT_done, 1)
                    g = i - 4
                    if live(g):
                        eng.wait_ge(s.z2_ok, g + 1)
                        need(eng, s.gateT_ok, g)
                        for t in range(GT):
                            m = eng.transpose(z2T_ps[:, t, :], z2[:, b, t, :], c.ident[:])
                        m.then_inc(s.z2T_done, 1)
                    g = i - 2
                    if live(g):
                        eng.wait_ge(s.zT_ok, g + 1)
                        need(eng, s.e2_ok, 2 * (g - 2))
                        eng.matmul(wT_ps, c.gnn_w[:], zT[:].rearrange("p t f -> p (t f)"), start=True, stop=True).then_inc(s.wT_done, 1)
                    g = i - 4
                    if live(g):
                        eng.wait_ge(s.z2T_ok, g + 1)
                        need(eng, s.e2g_ok, 2 * g)
                        for t in range(GT):
                            m = eng.matmul(gl_ps[:, t, :], z2T[:, t * P:t * P + P], c.gate_w[:], start=True, stop=True)
                        m.then_inc(s.gl_done, 1)
                        need(eng, s.x2_ok, g)
                        eng.matmul(h1_ps, c.sW1[:], z2T[:], start=True, stop=True).then_inc(s.h1_done, 1)
                    g = i - 4
                    if live(g):
                        need(eng, s.e2_ok, 2 * g)
                        expert1(g, 0)
                        need(eng, s.e2g_ok, 2 * g)
                        expert1(g, 1)
                    g = i - 3
                    if live(g):
                        eng.wait_ge(s.att_ok, g + 1)
                        need(eng, s.z2T_ok, g)
                        for t in range(GT):
                            m = eng.transpose(attT_ps[:, t, :], att[:, t, :], c.ident[:])
                        m.then_inc(s.attT_done, 1)
                    g = i - 2
                    if live(g):
                        eng.wait_ge(s.wT_ok, g + 1)
                        for t in range(GT):
                            for j in range(2):
                                m = eng.matmul(sim_ps[N * j:N * j + N, t, :], wT[:, t * P + N * j:t * P + N * j + N],
                                               zT[:, t, N * j:N * j + N], start=True, stop=True)
                        m.then_inc(s.sim_done, 1)
                    g = i - 4
                    if live(g):
                        eng.wait_ge(s.h1_ok, g + 1)
                        eng.matmul(h2_ps, c.sW2[:], h1[:], start=True, stop=True).then_inc(s.h2_done, 1)
                        if isinstance(i, int):
                            need(eng, s.wT_ok, min(g + 3, G))
                        else:
                            eng.wait_ge(s.wT_ok, g + 3)
                        expert1(g, 2)
                        eng.wait_ge(s.gl_ok, g + 1)
                        expert1(g, 3)
                    g = i - 3
                    if live(g):
                        eng.wait_ge(s.attT_ok, g + 1)
                        need(eng, s.x1_ok, g)
                        for t in range(GT):
                            m = eng.matmul(av_ps[:, t, :], attT[:, t, :], z[:, (q - 3) % U, t, :], start=True, stop=True)
                        m.then_inc(s.av_done, 1)
                    g = i - 4
                    if live(g):
                        eng.wait_ge(s.e1_ok, 4 * g + 2)
                        need(eng, s.e2g_ok, 2 * g)
                        expert2(g, 0)
                        eng.wait_ge(s.gate_ok, g + 1)
                        if isinstance(i, int):
                            need(eng, s.attT_ok, min(g + 2, G))
                        else:
                            eng.wait_ge(s.attT_ok, g + 2)
                        for t in range(GT):
                            m = eng.matmul(gateT_ps[:, t * P:t * P + P], parts[:, t].rearrange("p k e -> p (k e)"), ident16[:],
                                           start=True, stop=True)
                        m.then_inc(s.gateT_done, 1)
                        eng.wait_ge(s.e1_ok, 4 * g + 4)
                        expert2(g, 1)
                        eng.wait_ge(s.gateT_ok, g + 1)
                        for k in range(2):
                            eng.matmul(wide_ps[k], pair16[:, P * k:P * k + P], gateT[:], start=True, stop=True).then_inc(s.wide_done, 1)
                        eng.wait_ge(s.h2_ok, g + 1)
                        eng.wait_ge(s.e2g_ok, 2 * g + 2)
                        for t in range(GT):
                            cols = slice(t * P, t * P + P)
                            eng.matmul(out_ps[:, t, :], h2[:, cols], c.sW3[:], start=True, stop=False)
                            for k in range(2):
                                eng.matmul(out_ps[:, t, :], e2g[:, k, cols], c.eW3[:, k, :], start=False, stop=False)
                            for k in range(3):
                                m = eng.matmul(out_ps[:, t, :], gateT[:, cols], bias16[:, k], start=False, stop=(k == 2))
                        m.then_inc(s.out_done, 1)
                run(eng, body)


class Memory:
    pass


def build(nc, dram):
    with ExitStack() as ctx:
        c = Memory()

        def sb(name, shape, dt=F32):
            return ctx.enter_context(nc.sbuf_tensor(name, shape, dt))

        def sem(name):
            return ctx.enter_context(nc.semaphore(name))

        c.dram = dram
        c.x = sb("x", [P, T, D])
        c.adj = sb("adj", [P, T, N])
        c.tab = sb("tab", [P, T_ALL])
        c.ident = c.tab[:, T_ID:T_ID + P]
        c.which = sb("which", [P, 2])
        c.ones16 = sb("ones16", [P, P], BF16)
        c.low16 = sb("low16", [P, P], BF16)
        c.minus_half = sb("minus_half", [P, 2 * GT])
        c.gamma_row = sb("gamma_row", [P, D])
        c.beta_row = sb("beta_row", [P, D])
        c.cols = sb("cols", [P, 14])
        names = ["L0_gnn_gamma", "L0_gnn_beta", "L0_ffn_ln1_w", "L0_ffn_ln2_w", "L1_ffn_sb1", "L1_ffn_sb2"]
        c.gamma, c.beta, c.ln1, c.ln2, c.sb1, c.sb2 = (c.cols[:, n:n + 1] for n in range(6))
        c.eb1, c.eb2 = c.cols[:, 6:10], c.cols[:, 10:12]
        c.w_self = sb("w_self", [D, D])
        c.w_neigh = sb("w_neigh", [D, D])
        c.wqk = sb("wqk", [D, H * HD + KV * HD])
        c.wv = sb("wv", [D, KV * HD])
        c.wo = sb("wo", [D, D])
        c.router = sb("router", [D, NE])
        c.adj_in, c.x_in, c.weights_in, c.ones_ok = sem("adj_in"), sem("x_in"), sem("weights_in"), sem("ones_ok")

        x_rows = dram["x"].rearrange("(t b) n f -> (b n) t f", b=2)
        loads = [(c.tab[:], dram["tab"]), (c.cols[:, 6:10], dram["L1_ffn_eb1T"]), (c.cols[:, 10:12], dram["L1_ffn_eb2T"])]
        loads += [(c.cols[:, n:n + 1], dram[name].rearrange("(p a) -> p a", a=1)) for n, name in enumerate(names)]
        loads += [(c.gamma_row[:], dram["L0_gnn_gamma"].partition_broadcast(P)),
                  (c.beta_row[:], dram["L0_gnn_beta"].partition_broadcast(P)),
                  (c.w_self[:], dram["L0_gnn_W_self"]), (c.w_neigh[:], dram["L0_gnn_W_neigh"]),
                  (c.wqk[:, 0:128], dram["L0_ffn_wqT"]), (c.wqk[:, 128:192], dram["L0_ffn_wkT"]),
                  (c.wv[:], dram["L0_ffn_wvT"]), (c.wo[:], dram["L0_ffn_woT"]), (c.router[:], dram["L0_ffn_router_wT"])]
        c.weights_count = 16 * len(loads)
        c.masked = sb("masked", [P, T, N])
        c.gnn_w = sb("gnn_w", [D, D])
        c.sW1, c.sW2, c.sW3 = (sb(f"sW{n}", [D, D]) for n in (1, 2, 3))
        c.eW1 = sb("eW1", [D, SE, P])
        c.eW2 = sb("eW2", [P, SE, 64])
        c.eW3 = sb("eW3", [P, SE // 2, D])
        c.gate_w = sb("gate_w", [D, SE])
        c.gate_b = sb("gate_b", [P, SE])
        c.bias3 = sb("bias3", [3 * (SE + 1), D])
        c.late_loads = [(c.gnn_w[:], dram["L1_gnn_W"]), (c.sW1[:], dram["L1_ffn_sW1"]), (c.sW2[:], dram["L1_ffn_sW2"]),
                        (c.sW3[:], dram["L1_ffn_sW3"]), (c.eW1[:], dram["eW1"]), (c.eW2[:], dram["eW2"]), (c.eW3[:], dram["eW3"]),
                        (c.gate_w[:], dram["L1_ffn_gW"]), (c.gate_b[:], dram["L1_ffn_gb"].partition_broadcast(P)),
                        *((c.bias3[k:k + SE], dram["L1_ffn_eb3"]) for k in (0, SE + 1, 2 * (SE + 1))),
                        *((c.bias3[k + SE:k + SE + 1], dram["L1_ffn_sb3"].rearrange("(a f) -> a f", a=1))
                          for k in (0, SE + 1, 2 * (SE + 1)))]
        c.late_in, c.x_rest_in = sem("late_in"), sem("x_rest_in")
        c.first_groups = 6
        c.late_count = 16 * len(c.late_loads)
        c.stored, c.passed = sem("stored"), sem("passed")

        with nc.Block() as block:
            @block.sync
            def _(sp):
                sp.dma_start(c.adj[:], dram["adj"].rearrange("(t b) n m -> (b n) t m", b=2)).then_inc(c.adj_in, 16)
                for to, of in loads:
                    sp.dma_start(to, of).then_inc(c.weights_in, 16)
                first = c.first_groups * GT
                sp.dma_start(c.x[:, 0:first, :], x_rows[:, 0:first, :]).then_inc(c.x_in, 16)
                sp.dma_start(c.x[:, first:T, :], x_rows[:, first:T, :]).then_inc(c.x_rest_in, 16)

            @block.gpsimd
            def _(pool):
                pool.memset(c.minus_half[:], -0.5).then_inc(c.ones_ok, 1)
                pool.memset(c.which[:], 0.0).then_inc(c.ones_ok, 1)
                pool.wait_ge(c.ones_ok, 3)
                pool.memset(c.which[0:N, 0:1], 1.0).then_inc(c.ones_ok, 1)
                pool.wait_ge(c.ones_ok, 4)
                pool.memset(c.which[N:P, 1:2], 1.0).then_inc(c.ones_ok, 1)

            @block.vector
            def _(dve):
                dve.memset(c.ones16[:], 1.0).then_inc(c.ones_ok, 1)

        graph_conv(nc, c)
        moe_phases(nc, c, sb, sem)
        last_round(nc, c)


def kernel(**inputs):
    import concourse.bacc as _bacc
    from concourse.bass_utils import run_bass_kernel_spmd as _run

    nc = _bacc.Bacc("TRN2", target_bir_lowering=False, num_devices=1)
    w = {k: np.ascontiguousarray(v) for k, v in inputs.items()}
    layout = {k: w[k] for k in ("x", "adj", "nodemask", "L0_gnn_gamma", "L0_gnn_beta", "L0_gnn_W_self", "L0_gnn_W_neigh",
                                "L0_ffn_ln1_w", "L0_ffn_ln2_w", "L1_gnn_W", "L1_ffn_sW1", "L1_ffn_sW2", "L1_ffn_sW3",
                                "L1_ffn_sb1", "L1_ffn_sb2", "L1_ffn_sb3", "L1_ffn_eb3", "L1_ffn_gW", "L1_ffn_gb")}
    for k in ("L0_ffn_wq", "L0_ffn_wk", "L0_ffn_wv", "L0_ffn_wo", "L0_ffn_router_w", "L1_ffn_eb1"):
        layout[k + "T"] = w[k].T
    layout["L1_ffn_eb2T"] = w["L1_ffn_eb2"].reshape(SE // 2, P).T
    layout["w13"] = np.stack([w["L0_ffn_w1"], w["L0_ffn_w3"]], 1).transpose(3, 0, 1, 2)
    layout["w2"] = w["L0_ffn_w2"].transpose(2, 0, 1)
    layout["eW1"] = w["L1_ffn_eW1"].transpose(1, 0, 2)
    layout["eW2"] = w["L1_ffn_eW2"].transpose(1, 0, 2)
    layout["eW3"] = w["L1_ffn_eW3"].reshape(SE // 2, P, D).transpose(1, 0, 2)
    layout["tab"] = tables()
    arrays = {f"in_{k}": np.ascontiguousarray(v) for k, v in layout.items()}
    dram = {}
    for k in layout:
        a = arrays[f"in_{k}"]
        dram[k] = nc.dram_tensor(f"in_{k}", a.shape, mybir.dt.from_np(a.dtype), kind="ExternalInput").ap()
    dram["rows"] = nc.dram_tensor("rows", (NE * REGION, D), F32).ap()
    dram["picked"] = nc.dram_tensor("picked", (SLOTS * P, D), F32).ap()
    dram["out"] = nc.dram_tensor("out_0", (B, N, D), F32, kind="ExternalOutput").ap()
    build(nc, dram)
    r = _run(nc, [arrays], core_ids=[0])
    return r.results[0]["out_0"]
```
